# Optimizing a Trainium2 kernel written in Bass

```python
import numpy as np
import jax
import jax.numpy as jnp

def _softmax(x, axis=-1):
    return jax.nn.softmax(x, axis=axis)

def _gelu(x):
    return jax.nn.gelu(x, approximate=True)

def _silu(x):
    return jax.nn.silu(x)

def _sigmoid(x):
    return jax.nn.sigmoid(x)

def _layernorm(x, axis=-1, eps=1e-05):
    m = jnp.mean(x, axis=axis, keepdims=True)
    v = jnp.var(x, axis=axis, keepdims=True)
    return (x - m) / jnp.sqrt(v + eps)

def _scatter_add(tgt, idx, src, axis=0):
    return tgt.at[idx].add(src)

def _segment_sum(src, seg, n):
    return jax.ops.segment_sum(src, seg, n)
kernel_name = 'mk_seq_preln_d2_jaxref_r8_714adf'

def setup_inputs(seed: int=0):
    np.random.seed(seed)
    _w = jnp.asarray

    def _L0_attn_setup():
        import jax, jax.numpy as jnp
        import numpy as np
        D_MODEL = 128
        D_STATE = 128
        MLP_RATIO = 2
        LN_EPS = 1e-05

        def _layernorm(x, g, b):
            mu = jnp.mean(x, axis=-1, keepdims=True)
            var = jnp.var(x, axis=-1, keepdims=True)
            return (x - mu) * jax.lax.rsqrt(var + LN_EPS) * g + b

        def _lru(u, w_in, log_lambda, w_out, D_skip):
            lam = jax.nn.sigmoid(log_lambda)
            u_proj = jnp.einsum('btd,sd->bts', u, w_in)
            B, T, S = u_proj.shape

            def step(x, u_t):
                x = lam * x + (1.0 - lam) * u_t
                return (x, x)
            x0 = jnp.zeros((B, S), dtype=u_proj.dtype)
            _, ys = jax.lax.scan(step, x0, jnp.swapaxes(u_proj, 0, 1))
            y_states = jnp.swapaxes(ys, 0, 1)
            return jnp.einsum('bts,ds->btd', y_states, w_out) + u * D_skip
        key = jax.random.key(seed)
        ks = jax.random.split(key, 8)
        B, T = (4, 512)
        d, s, f = (D_MODEL, D_STATE, D_MODEL * MLP_RATIO)
        inp = {'x': jax.random.normal(ks[0], (B, T, d), dtype=jnp.float32), 'w_in': jax.random.normal(ks[1], (s, d), dtype=jnp.float32) / np.sqrt(d), 'log_lambda': jnp.full((s,), 2.0, dtype=jnp.float32), 'w_out': jax.random.normal(ks[2], (d, s), dtype=jnp.float32) / np.sqrt(s), 'D_skip': jnp.full((d,), 0.1, dtype=jnp.float32), 'ln1_g': jnp.ones((d,), dtype=jnp.float32), 'ln1_b': jnp.zeros((d,), dtype=jnp.float32), 'ln2_g': jnp.ones((d,), dtype=jnp.float32), 'ln2_b': jnp.zeros((d,), dtype=jnp.float32), 'w1': jax.random.normal(ks[3], (f, d), dtype=jnp.float32) / np.sqrt(d), 'b1': jnp.zeros((f,), dtype=jnp.float32), 'w2': jax.random.normal(ks[4], (d, f), dtype=jnp.float32) / np.sqrt(f), 'b2': jnp.zeros((d,), dtype=jnp.float32)}
        return inp
    _L0_attn_in = _L0_attn_setup()

    def _L0_ffn_setup():
        import jax, jax.numpy as jnp
        import numpy as np
        B, S, H, E, K = (4, 256, 128, 8, 2)
        key = jax.random.key(seed)
        k0, k1, k2, k3 = jax.random.split(key, 4)
        x = jax.random.normal(k0, (B, S, H), dtype=jnp.float32)
        router_w = jax.random.normal(k1, (E, H), dtype=jnp.float32) * np.float32(1.0 / np.sqrt(H))
        xav1 = np.float32(np.sqrt(2.0 / (2 * H + H)))
        w1 = jax.random.normal(k2, (E, 2 * H, H), dtype=jnp.float32) * xav1
        w2 = jax.random.normal(k3, (E, H, 2 * H), dtype=jnp.float32) * xav1
        return {'x': x, 'router_w': router_w, 'w1': w1, 'w2': w2}
    _L0_ffn_in = _L0_ffn_setup()

    def _L1_attn_setup():
        import jax, jax.numpy as jnp
        import numpy as np
        DIM = 128
        NUM_HEADS = 16
        DIM_HEAD = DIM // NUM_HEADS

        def _softmax(logits, axis=-1):
            logits = logits - jnp.max(logits, axis=axis, keepdims=True)
            e = jnp.exp(logits)
            return e / jnp.sum(e, axis=axis, keepdims=True)
        key = jax.random.key(seed)
        kx, kq, kk, kv, ko = jax.random.split(key, 5)
        s = 1.0 / np.sqrt(DIM)
        return {'x': jax.random.normal(kx, (4, 256, DIM), dtype=jnp.float32), 'Wq': jax.random.uniform(kq, (DIM, DIM), jnp.float32, -s, s), 'Wk': jax.random.uniform(kk, (DIM, DIM), jnp.float32, -s, s), 'Wv': jax.random.uniform(kv, (DIM, DIM), jnp.float32, -s, s), 'Wo': jax.random.uniform(ko, (DIM, DIM), jnp.float32, -s, s)}
    _L1_attn_in = _L1_attn_setup()

    def _L1_ffn_setup():
        import jax, jax.numpy as jnp
        import numpy as np
        H = 128
        I = 4 * H
        E = 8
        K = 2
        B, S = (2, 128)
        STD = 0.02 / np.sqrt(H)
        key = jax.random.key(seed)
        ks = jax.random.split(key, 8)
        x = jax.random.normal(ks[0], (B, S, H), dtype=jnp.float32)
        gate_w = jax.random.normal(ks[1], (H, E), dtype=jnp.float32) * STD
        bias = jnp.zeros((E,), dtype=jnp.float32)
        up_w = jax.random.normal(ks[2], (E, H, I), dtype=jnp.float32) * STD
        up_b = jnp.zeros((E, I), dtype=jnp.float32)
        down_w = jax.random.normal(ks[3], (E, I, H), dtype=jnp.float32) * STD
        down_b = jnp.zeros((E, H), dtype=jnp.float32)
        sw_up = jax.random.normal(ks[4], (H, I), dtype=jnp.float32) * STD
        sb_up = jnp.zeros((I,), dtype=jnp.float32)
        sw_down = jax.random.normal(ks[5], (I, H), dtype=jnp.float32) * STD
        sb_down = jnp.zeros((H,), dtype=jnp.float32)
        return {'x': x, 'gate_w': gate_w, 'bias': bias, 'up_w': up_w, 'up_b': up_b, 'down_w': down_w, 'down_b': down_b, 'sw_up': sw_up, 'sb_up': sb_up, 'sw_down': sw_down, 'sb_down': sb_down}
    _L1_ffn_in = _L1_ffn_setup()
    _d = {'L0_attn_x': _L0_attn_in['x'], 'L0_attn_w_in': _L0_attn_in['w_in'], 'L0_attn_log_lambda': _L0_attn_in['log_lambda'], 'L0_attn_w_out': _L0_attn_in['w_out'], 'L0_attn_D_skip': _L0_attn_in['D_skip'], 'L0_attn_ln1_g': _L0_attn_in['ln1_g'], 'L0_attn_ln1_b': _L0_attn_in['ln1_b'], 'L0_attn_ln2_g': _L0_attn_in['ln2_g'], 'L0_attn_ln2_b': _L0_attn_in['ln2_b'], 'L0_attn_w1': _L0_attn_in['w1'], 'L0_attn_b1': _L0_attn_in['b1'], 'L0_attn_w2': _L0_attn_in['w2'], 'L0_attn_b2': _L0_attn_in['b2'], 'L0_ffn_router_w': _L0_ffn_in['router_w'], 'L0_ffn_w1': _L0_ffn_in['w1'], 'L0_ffn_w2': _L0_ffn_in['w2'], 'L1_attn_Wq': _L1_attn_in['Wq'], 'L1_attn_Wk': _L1_attn_in['Wk'], 'L1_attn_Wv': _L1_attn_in['Wv'], 'L1_attn_Wo': _L1_attn_in['Wo'], 'L1_ffn_gate_w': _L1_ffn_in['gate_w'], 'L1_ffn_bias': _L1_ffn_in['bias'], 'L1_ffn_up_w': _L1_ffn_in['up_w'], 'L1_ffn_up_b': _L1_ffn_in['up_b'], 'L1_ffn_down_w': _L1_ffn_in['down_w'], 'L1_ffn_down_b': _L1_ffn_in['down_b'], 'L1_ffn_sw_up': _L1_ffn_in['sw_up'], 'L1_ffn_sb_up': _L1_ffn_in['sb_up'], 'L1_ffn_sw_down': _L1_ffn_in['sw_down'], 'L1_ffn_sb_down': _L1_ffn_in['sb_down']}
    _x0 = _d['L0_attn_x']
    _d['L0_attn_x'] = jax.random.normal(jax.random.fold_in(jax.random.key(seed), 1), (8, 512, 128), dtype=_x0.dtype)
    del _x0
    return _d

def reference(L0_attn_x, L0_attn_w_in, L0_attn_log_lambda, L0_attn_w_out, L0_attn_D_skip, L0_attn_ln1_g, L0_attn_ln1_b, L0_attn_ln2_g, L0_attn_ln2_b, L0_attn_w1, L0_attn_b1, L0_attn_w2, L0_attn_b2, L0_ffn_router_w, L0_ffn_w1, L0_ffn_w2, L1_attn_Wq, L1_attn_Wk, L1_attn_Wv, L1_attn_Wo, L1_ffn_gate_w, L1_ffn_bias, L1_ffn_up_w, L1_ffn_up_b, L1_ffn_down_w, L1_ffn_down_b, L1_ffn_sw_up, L1_ffn_sb_up, L1_ffn_sw_down, L1_ffn_sb_down):

    def _L0_attn_ref(x, w_in, log_lambda, w_out, D_skip, ln1_g, ln1_b, ln2_g, ln2_b, w1, b1, w2, b2):
        import jax, jax.numpy as jnp
        import numpy as np
        D_MODEL = 128
        D_STATE = 128
        MLP_RATIO = 2
        LN_EPS = 1e-05

        def _layernorm(x, g, b):
            mu = jnp.mean(x, axis=-1, keepdims=True)
            var = jnp.var(x, axis=-1, keepdims=True)
            return (x - mu) * jax.lax.rsqrt(var + LN_EPS) * g + b

        def _lru(u, w_in, log_lambda, w_out, D_skip):
            lam = jax.nn.sigmoid(log_lambda)
            u_proj = jnp.einsum('btd,sd->bts', u, w_in)
            B, T, S = u_proj.shape

            def step(x, u_t):
                x = lam * x + (1.0 - lam) * u_t
                return (x, x)
            x0 = jnp.zeros((B, S), dtype=u_proj.dtype)
            _, ys = jax.lax.scan(step, x0, jnp.swapaxes(u_proj, 0, 1))
            y_states = jnp.swapaxes(ys, 0, 1)
            return jnp.einsum('bts,ds->btd', y_states, w_out) + u * D_skip
        x = x + _lru(_layernorm(x, ln1_g, ln1_b), w_in, log_lambda, w_out, D_skip)
        h = _layernorm(x, ln2_g, ln2_b)
        h = jax.nn.relu(jnp.einsum('btd,fd->btf', h, w1) + b1)
        x = x + jnp.einsum('btf,df->btd', h, w2) + b2
        return x

    def _L0_ffn_ref(x, router_w, w1, w2):
        import jax, jax.numpy as jnp
        import numpy as np
        B, S, H, E, K = (4, 256, 128, 8, 2)
        bsz, seq, hidden = x.shape
        n_experts = w1.shape[0]
        tokens = x.reshape(-1, hidden)
        T = tokens.shape[0]
        logits = tokens @ router_w.T
        topv, topi = jax.lax.top_k(logits, K)
        w = jax.nn.softmax(topv, axis=-1).astype(tokens.dtype)
        gate = jnp.zeros((T, n_experts), tokens.dtype).at[jnp.arange(T)[:, None], topi].add(w)
        out = jnp.zeros_like(tokens)
        for e in range(n_experts):
            h = jax.nn.gelu(tokens @ w1[e].T, approximate=False)
            y = h @ w2[e].T
            out = out + gate[:, e:e + 1] * y
        return out.reshape(bsz, seq, hidden)

    def _L1_attn_ref(x, Wq, Wk, Wv, Wo):
        import jax, jax.numpy as jnp
        import numpy as np
        DIM = 128
        NUM_HEADS = 16
        DIM_HEAD = DIM // NUM_HEADS

        def _softmax(logits, axis=-1):
            logits = logits - jnp.max(logits, axis=axis, keepdims=True)
            e = jnp.exp(logits)
            return e / jnp.sum(e, axis=axis, keepdims=True)
        B, T, D = x.shape
        H, Dh = (NUM_HEADS, DIM_HEAD)
        q = (x @ Wq.T).reshape(B, T, H, Dh).transpose(0, 2, 1, 3)
        k = (x @ Wk.T).reshape(B, T, H, Dh).transpose(0, 2, 1, 3)
        v = (x @ Wv.T).reshape(B, T, H, Dh).transpose(0, 2, 1, 3)
        scale = Dh ** (-0.5)
        logits = jnp.einsum('bhqd,bhkd->bhqk', q, k) * scale
        causal_mask = jnp.triu(jnp.ones((T, T), dtype=bool), k=1)
        neg = -jnp.finfo(logits.dtype).max
        logits = jnp.where(causal_mask, neg, logits)
        attn = _softmax(logits, axis=-1)
        out = jnp.einsum('bhqk,bhkd->bhqd', attn, v)
        out = out.transpose(0, 2, 1, 3).reshape(B, T, D)
        return out @ Wo.T

    def _L1_ffn_ref(x, gate_w, bias, up_w, up_b, down_w, down_b, sw_up, sb_up, sw_down, sb_down):
        import jax, jax.numpy as jnp
        import numpy as np
        H = 128
        I = 4 * H
        E = 8
        K = 2
        B, S = (2, 128)
        STD = 0.02 / np.sqrt(H)
        b, s, h = x.shape
        xf = x.reshape(-1, h)
        T = xf.shape[0]
        scores = jax.nn.sigmoid(xf @ gate_w + bias)
        top_scores, top_idx = jax.lax.top_k(scores, K)
        top_scores = top_scores / (jnp.sum(top_scores, axis=-1, keepdims=True) + 1e-06)
        w = jnp.zeros((T, E), dtype=xf.dtype).at[jnp.arange(T)[:, None], top_idx].add(top_scores)
        up = jnp.einsum('th,ehi->tei', xf, up_w) + up_b
        hact = jax.nn.gelu(up, approximate=False)
        eo = jnp.einsum('tei,eih->teh', hact, down_w) + down_b
        combined = jnp.einsum('teh,te->th', eo * 0.1, w)
        shared = (jax.nn.gelu(xf @ sw_up + sb_up, approximate=False) @ sw_down + sb_down) * 0.1
        out = (shared + combined).reshape(b, s, h)
        out = out / (jnp.max(jnp.abs(out), axis=-1, keepdims=True) + 1e-06)
        return out
    x = L0_attn_x
    x = x + _L0_attn_ref(_layernorm(x, axis=-1), L0_attn_w_in, L0_attn_log_lambda, L0_attn_w_out, L0_attn_D_skip, L0_attn_ln1_g, L0_attn_ln1_b, L0_attn_ln2_g, L0_attn_ln2_b, L0_attn_w1, L0_attn_b1, L0_attn_w2, L0_attn_b2)
    x = x + _L0_ffn_ref(_layernorm(x, axis=-1), L0_ffn_router_w, L0_ffn_w1, L0_ffn_w2)
    x = x + _L1_attn_ref(_layernorm(x, axis=-1), L1_attn_Wq, L1_attn_Wk, L1_attn_Wv, L1_attn_Wo)
    x = x + _L1_ffn_ref(_layernorm(x, axis=-1), L1_ffn_gate_w, L1_ffn_bias, L1_ffn_up_w, L1_ffn_up_b, L1_ffn_down_w, L1_ffn_down_b, L1_ffn_sw_up, L1_ffn_sb_up, L1_ffn_sw_down, L1_ffn_sb_down)
    return x

_drawn_inputs = setup_inputs


def setup_inputs(seed=0):
    import zlib

    import numpy as np

    out = dict(_drawn_inputs(seed))
    spreads = {'L0_attn_log_lambda': (2.0, 0.2),
     'L0_attn_D_skip': (0.10000000149011612, 0.6),
     'L0_attn_ln1_g': (1.0, 0.2),
     'L0_attn_ln1_b': (0.0, 0.1),
     'L0_attn_ln2_g': (1.0, 0.2),
     'L0_attn_ln2_b': (0.0, 0.1),
     'L0_attn_b1': (0.0, 0.1),
     'L0_attn_b2': (0.0, 0.1),
     'L1_ffn_bias': (0.0, 0.1),
     'L1_ffn_up_b': (0.0, 0.8),
     'L1_ffn_down_b': (0.0, 0.1),
     'L1_ffn_sb_up': (0.0, 0.8),
     'L1_ffn_sb_down': (0.0, 0.1)}
    factors = {'L1_attn_Wq': 8.0,
     'L1_attn_Wk': 8.0,
     'L1_ffn_up_w': 27.42,
     'L1_ffn_down_w': 8.0,
     'L1_ffn_sw_up': 8.0,
     'L1_ffn_sw_down': 8.0}
    for name, (base, spread) in spreads.items():
        noise = np.random.default_rng([zlib.crc32(name.encode()), seed]).standard_normal(out[name].shape)
        drawn = base * np.exp(spread * noise) if base else spread * noise
        out[name] = jnp.asarray(drawn.astype(out[name].dtype))
    for name, factor in factors.items():
        out[name] = (out[name] * factor).astype(out[name].dtype)
    return out
```

```python
import concourse.bass as bass
from concourse import mybir
from contextlib import ExitStack

F32 = mybir.dt.float32
F32R = mybir.dt.float32r
BF16 = mybir.dt.bfloat16
ALU = mybir.AluOpType
ACT = mybir.ActivationFunctionType
AX = mybir.AxisListType

P = 128
B, T = 8, 512
TB = T // P
NT = B * TB
E = 8
F0 = 2
F1 = 4
H, DH = 16, 8
HG = 4
G = H // HG
SLAB = P // HG
EPS = 1e-5
NEG = -1e30
BIG = 3e38
VEC = ['L0_attn_log_lambda', 'L0_attn_D_skip', 'L0_attn_ln1_g', 'L0_attn_ln1_b', 'L0_attn_ln2_g',
       'L0_attn_ln2_b', 'L0_attn_b1', 'L1_ffn_sb_up']
LAM, DSK, G1, B1V, G2, B2V, HB, SBU = 0, 1, 2, 3, 4, 5, 6, 8
NVEC = 12


class Shared:
    pass


def hold(eng, sem, count):
    eng.wait_ge(sem, count)
    if not isinstance(count, int):
        eng.sem_inc(hold.pace[eng.engine])


def setup(nc, s, A, sem, sb):
    stage = sb("stage", [P, 2 * E * F0, P])
    nat = sb("nat", [P, 10, P])
    vrow = sb("vrow", [NVEC, P])
    uprow = sb("uprow", [E * F1, P])
    rtrow = sb("rtrow", [E, P])
    brow = sb("brow", [1, 2 * P + E])
    sel = sb("sel", [1, 3, P])
    one = sb("one", [1, P])
    lamc = sb("lamc", [P, 2])
    win = sb("win", [P, P])
    wq_t = sb("wq_t", [P, 2, P])
    x_in = s.x_in
    w_in = sem("w_in")
    cst, cst2, chain, lam_in, lam_r, win_r = (sem(n) for n in ("cst", "cst2", "chain_setup", "lam_in", "lam_r", "win_r"))
    turned, evac_a, evac_v = sem("turned"), sem("evac_a"), sem("evac_v")

    jobs = []
    for e in range(0, E, 2):
        jobs.append([(stage[:, 2 * e + k, :], P) for k in range(4)] + [s.w1T[:, e:e + 2, :].rearrange("p e f -> p (e f)")])
    for e in range(0, E, 2):
        jobs.append([(stage[:, 2 * E + 2 * e + k, :], P) for k in range(4)] + [s.w2T[:, 2 * e:2 * e + 4, :].rearrange("p c d -> p (c d)")])
    jobs.append([(nat[:, k, :], P) for k in (1, 2, 3)] + [s.m1T[:, :]])
    jobs.append([(nat[:, k, :], P) for k in (4, 5, 8, 9)] + [s.m2T[:, :]])
    jobs.append([(nat[:, k, :], P) for k in (6, 7)] + [wq_t[:, :, :].rearrange("p k d -> p (k d)")])
    jobs.append([(win[:, :], P)] + [s.winT[:, :]])

    with nc.Block() as block:
        @block.sync
        def _(sp):
            n = 0
            for k, name in enumerate(VEC):
                r = [0, 1, 2, 3, 4, 5, 6, 8][k]
                a = A[name].rearrange("(c p) -> c p", p=P)
                sp.dma_start(vrow[r:r + a.shape[0], :], a).then_inc(w_in, 16)
                n += 1
            sp.dma_start(x_in[0], A['L0_attn_x'].rearrange("b (j p) d -> p (b j) d", p=P)).then_inc(x_in[1], 16)
            sp.dma_start(uprow[:, :], A['L1_ffn_up_b'].rearrange("e (c p) -> (e c) p", p=P)).then_inc(w_in, 16)
            sp.dma_start(nat[:, 0, :], A['L0_attn_w_in']).then_inc(w_in, 16)
            sp.dma_start(nat[:, 1, :], A['L0_attn_w_out']).then_inc(w_in, 16)
            sp.dma_start(nat[:, 2:4, :], A['L0_attn_w1'].rearrange("(c p) d -> p c d", p=P)).then_inc(w_in, 16)
            sp.dma_start(nat[:, 4:6, :], A['L0_attn_w2'].rearrange("p (c d) -> p c d", c=2)).then_inc(w_in, 16)
            for k, name in enumerate(['L1_attn_Wq', 'L1_attn_Wk', 'L1_attn_Wv', 'L1_attn_Wo']):
                sp.dma_start(nat[:, 6 + k, :], A[name]).then_inc(w_in, 16)
            sp.dma_start(rtrow[:, :], A['L0_ffn_router_w']).then_inc(w_in, 16)
            sp.dma_start(brow[:, 0:P], A['L0_attn_b2'].rearrange("(a n) -> a n", a=1)).then_inc(w_in, 16)
            sp.dma_start(brow[:, 2 * P:2 * P + E], A['L1_ffn_bias'].rearrange("(a n) -> a n", a=1)).then_inc(w_in, 16)
            sp.dma_start(s.down9[0:E, :], A['L1_ffn_down_b']).then_inc(w_in, 16)
            sp.dma_start(s.down9[E:E + 1, :], A['L1_ffn_sb_down'].rearrange("(a n) -> a n", a=1)).then_inc(w_in, 16)
            sp.dma_start(s.gateW[:, :], A['L1_ffn_gate_w']).then_inc(w_in, 16)
            n += 14
            sp.dma_start(s.swup[:, :], A['L1_ffn_sw_up']).then_inc(w_in, 16)
            sp.dma_start(s.swdn[:, :, :], A['L1_ffn_sw_down'].rearrange("(c p) d -> p c d", p=P)).then_inc(w_in, 16)
            sp.dma_start(stage[:, 0:2 * E, :], A['L0_ffn_w1'].rearrange("e (c p) d -> p (e c) d", p=P)).then_inc(w_in, 16)
            sp.dma_start(stage[:, 2 * E:4 * E, :].rearrange("p (e c) f -> p e (c f)", e=E),
                         A['L0_ffn_w2'].rearrange("e p f -> p e f")).then_inc(w_in, 16)
            sp.dma_start(s.up[:, :, :], A['L1_ffn_up_w'].rearrange("e p f -> p e f")).then_inc(w_in, 16)
            sp.dma_start(s.down[:, :, :], A['L1_ffn_down_w'].rearrange("e (c p) d -> p (e c) d", p=P)).then_inc(w_in, 16)

        loads = len(VEC) + 14 + 1 + 6

        @block.gpsimd
        def _(pool):
            pool.memset(s.ident[:, :], 0.0).then_inc(cst, 1)
            pool.memset(s.identb[:, :], 0.0).then_inc(cst, 1)
            pool.memset(s.later[:, :], 0.0).then_inc(cst, 1)
            pool.memset(s.laterT[:, :], 0.0).then_inc(cst, 1)
            pool.wait_ge(cst, 4)
            for m in (s.ident, s.identb):
                pool.affine_select(out=m[:, :], in_=m[:, :], compare_op=ALU.not_equal, fill=1.0, base=0,
                                   pattern=[[-1, P]], channel_multiplier=1).then_inc(cst, 1)
            pool.affine_select(out=s.later[:, :], in_=s.later[:, :], compare_op=ALU.is_ge, fill=NEG, base=0,
                               pattern=[[-1, P]], channel_multiplier=1).then_inc(cst, 1)
            pool.affine_select(out=s.laterT[:, :], in_=s.laterT[:, :], compare_op=ALU.is_ge, fill=NEG, base=0,
                               pattern=[[1, P]], channel_multiplier=-1).then_inc(cst, 1)
            for e in range(E):
                pool.memset(s.rev[:, e:e + 1], float(E - e)).then_inc(cst, 1)
            pool.memset(s.eps1[:, :], EPS).then_inc(cst, 1)
            pool.memset(s.eps2[:, :], EPS * EPS).then_inc(cst, 1)
            pool.memset(one[:, :], 1.0).then_inc(cst, 1)
            pool.memset(sel[:, :, :], 0.0).then_inc(cst, 1)
            pool.memset(s.qkT[:, :, :, :], 0.0).then_inc(cst, 1)
            pool.wait_ge(cst, 8 + E + 5)
            selv = sel[:, :, :].rearrange("p r (g c) -> p r g c", g=HG)
            pool.memset(selv[:, 0, :, DH:2 * DH], -1.0).then_inc(cst2, 1)
            pool.memset(selv[:, 1, :, 2 * DH:3 * DH], -1.0).then_inc(cst2, 1)
            pool.memset(selv[:, 1, :, 3 * DH:3 * DH + 2], 1.0).then_inc(cst2, 1)
            pool.memset(selv[:, 2, :, 3 * DH:3 * DH + 2], 1.0).then_inc(cst2, 1)

        NC1 = 8 + E + 5

        @block.scalar
        def _(act):
            act.wait_ge(evac_v, 2)
            act.activation(lamc[:, 0:1], s.vec[:, LAM:LAM + 1], ACT.Sigmoid).then_inc(lam_in, 1)
            for g in range(0, len(jobs), 2):
                act.wait_ge(turned, 5 + g + 1)
                w = P * (len(jobs[g]) - 1)
                act.copy(jobs[g][-1], s.ps[:, (g % 4) * 512:(g % 4) * 512 + w]).then_inc(evac_a, 1)

        @block.vector
        def _(dve):
            n = [0]

            def chained(ins):
                n[0] += 1
                ins.then_inc(chain, 1)
                dve.wait_ge(chain, n[0])

            bank = lambda k, w: s.ps[:, k * 512:k * 512 + w]
            dve.wait_ge(turned, 5)
            dve.tensor_copy(s.vec[:, :], bank(4, NVEC)).then_inc(evac_v, 1)
            dve.tensor_copy(s.upb[:, :], bank(5, E * F1)).then_inc(evac_v, 1)
            dve.tensor_copy(s.rT[:, :], bank(6, E)).then_inc(evac_v, 1)
            dve.tensor_copy(s.bcast[:, :], bank(7, 2 * P + E)).then_inc(evac_v, 1)
            dve.tensor_copy(s.sgn[:, :], s.ps[:, 4 * 512 + 64:4 * 512 + 67]).then_inc(evac_v, 1)
            dve.wait_ge(evac_v, 5)
            dve.wait_ge(lam_in, 1)
            chained(dve.memset(s.lam[:, :], 1.0))
            chained(dve.tensor_scalar(s.lam[:, :], s.lam[:, :], lamc[:, 0:1], None, ALU.mult))
            chained(dve.tensor_scalar(lamc[:, 1:2], lamc[:, 0:1], -1.0, 1.0, ALU.mult, ALU.add))
            dve.tensor_scalar(win[:, :], nat[:, 0, :], lamc[:, 1:2], None, ALU.mult).then_inc(win_r, 1)
            dve.tensor_scalar(s.dskip[:, :], s.ident[:, :], s.vec[:, DSK:DSK + 1], None, ALU.mult).then_inc(chain, 1)
            for g in range(1, len(jobs), 2):
                dve.wait_ge(turned, 5 + g + 1)
                w = P * (len(jobs[g]) - 1)
                dve.tensor_copy(jobs[g][-1], s.ps[:, (g % 4) * 512:(g % 4) * 512 + w]).then_inc(evac_v, 1)
            dve.wait_ge(evac_a, 6)
            for k in range(2):
                for t in range(3):
                    dve.tensor_copy(s.qkT[:, k, :, :].rearrange("p G (g c) -> p (G g) c", g=HG)[:, :, DH * t:DH * t + DH],
                                    wq_t[:, k, :].rearrange("p (h d) -> p h d", d=DH)).then_inc(chain, 1)

        @block.tensor
        def _(pe):
            pe.wait_ge(w_in, 16 * loads)
            pe.wait_ge(cst, NC1)
            pe.wait_ge(cst2, 4)
            at = lambda k, a, b: s.ps[:, k * 512 + a:k * 512 + b]
            pe.transpose(at(4, 0, NVEC), vrow[:, :], s.ident[0:NVEC, 0:NVEC]).then_inc(turned, 1)
            pe.transpose(at(5, 0, E * F1), uprow[:, :], s.ident[0:E * F1, 0:E * F1]).then_inc(turned, 1)
            pe.transpose(at(6, 0, E), rtrow[:, :], s.ident[0:E, 0:E]).then_inc(turned, 1)
            for a, b in ((0, P), (2 * P, 2 * P + E)):
                pe.matmul(at(7, a, b), one[:, :], brow[:, a:b], start=True, stop=True)
            pe.matmul(at(7, P, 2 * P), one[:, :], one[:, :], start=True, stop=True).then_inc(turned, 1)
            for r in range(3):
                m = pe.matmul(at(4, 64 + r, 65 + r), sel[:, r, :], one[:, 0:1], start=True, stop=True)
            m.then_inc(turned, 1)
            for g, job in enumerate(jobs):
                if g >= 4:
                    pe.wait_ge(*((evac_a, (g - 4) // 2 + 1) if g % 2 == 0 else (evac_v, 5 + (g - 4) // 2 + 1)))
                if g == len(jobs) - 1:
                    pe.wait_ge(win_r, 1)
                for k, (src, rows) in enumerate(job[:-1]):
                    m = pe.transpose(at(g % 4, k * P, k * P + P), src, s.ident[:, :])
                m.then_inc(turned, 1)


def token_stats(nc, s, sem, tag):
    st_ready, mv_ready, std_ready, done = (sem(n + tag) for n in ("st", "mv", "std", "rs"))
    with nc.Block() as block:
        @block.vector
        def _(dve):
            if tag == "a":
                dve.wait_ge(s.x_in[1], 16)
            with dve.Fori(0, B) as i:
                for j in range(TB):
                    m = dve.bn_stats(s.st[:, j, :], s.X[:, bass.ds(TB * i + j, 1), :])
                m.then_inc(st_ready, 1)
                hold(dve, st_ready, i + 1)
                for j in range(TB):
                    m = dve.bn_aggr(s.mvt[:, j, :], s.st[:, j, :])
                m.then_inc(mv_ready, 1)
                hold(dve, mv_ready, 2 * i + 1)
                dve.tensor_copy(s.mv[:, bass.ds(TB * i, TB), :], s.mvt[:, :, :]).then_inc(mv_ready, 1)
            dve.wait_ge(std_ready, 1)
            dve.reciprocal(s.rstd[:, :], s.std[:, :]).then_inc(done, 1)
            if tag == "a":
                dve.wait_ge(std_ready, 2)
                dve.reciprocal(s.rr[:, :], s.std2[:, :]).then_inc(done, 1)
            dve.wait_ge(done, 1 + (tag == "a"))

        @block.scalar
        def _(act):
            act.wait_ge(mv_ready, 2 * B)
            act.activation(s.std[:, :], s.mv[:, :, 1], ACT.Sqrt, bias=s.eps1[:, :]).then_inc(std_ready, 1)
            if tag == "a":
                act.activation(s.std2[:, :], s.mv[:, :, 1], ACT.Sqrt, bias=s.eps2[:, :], scale=1.0 + EPS)\
                   .then_inc(std_ready, 1)


def lru_block(nc, s, sem, sb):
    two = range(2)
    u0 = [sb(f"u0{k}", [P, TB, P]) for k in two]
    n1 = [sb(f"n1{k}", [P, TB, P]) for k in two]
    u1 = [sb(f"u1{k}", [P, T]) for k in two]
    y = [sb(f"y{k}", [P, T]) for k in two]
    x1 = [sb(f"x1{k}", [P, TB, P]) for k in two]
    hm = [sb(f"hm{k}", [P, F0, T]) for k in two]
    st2 = [sb(f"st2{k}", [P, TB, 6]) for k in two]
    mv2 = [sb(f"mv2{k}", [P, TB, 2]) for k in two]
    mu = [sb(f"mu{k}", [P, TB]) for k in two]
    r0 = [sb(f"r0{k}", [P, TB]) for k in two]
    sd2 = [sb(f"sd2{k}", [P, TB]) for k in two]
    names = ("n1_ready", "u_turned", "u1_ready", "up_ready", "y_ready", "x1_ready", "mv2_ready", "sd2_ready", "n2_ready",
             "h_turned", "h_ready", "hid_ready", "hm_ready", "mlp_ready", "x_done", "x1b_ready")
    (n1_ready, u_turned, u1_ready, up_ready, y_ready, x1_ready, mv2_ready, sd2_ready, n2_ready,
     h_turned, h_ready, hid_ready, hm_ready, mlp_ready, x_done, x1b_ready) = (sem(n) for n in names)
    chain = sem("chain_lru")
    psT = [s.ps[:, 512 * k:512 * k + 512] for k in (0, 1)]
    psU = [s.ps[:, 512 * k:512 * k + 512] for k in (2, 3)]
    psX = [s.ps[:, 512 * k:512 * k + 512] for k in (4, 5)]
    flat = lambda t: t[:, :, :].rearrange("p j d -> p (j d)")
    KCH = 12

    with nc.Block() as block:
        @block.vector
        def _(dve):
            with dve.Fori(0, B // 2) as i:
                n = [0]

                def link(ins):
                    n[0] += 1
                    ins.then_inc(chain, 1)

                def settle():
                    hold(dve, chain, KCH * i + n[0])

                for k in two:
                    tiles = bass.ds(2 * TB * i + TB * k, TB)
                    dve.tensor_copy(mu[k][:, :], s.mv[:, tiles, 0])
                    dve.tensor_copy(r0[k][:, :], s.rstd[:, tiles])
                    dve.tensor_copy(sd2[k][:, :], s.rr[:, tiles])
                    link(dve.tensor_copy(x1[k][:, :, :], s.X[:, tiles, :]))
                    settle()
                    for j in range(TB):
                        dve.tensor_scalar(u0[k][:, j, :], x1[k][:, j, :], mu[k][:, j:j + 1], r0[k][:, j:j + 1],
                                          ALU.subtract, ALU.mult)
                    for j in range(TB):
                        m = dve.tensor_scalar(n1[k][:, j, :], x1[k][:, j, :], mu[k][:, j:j + 1], sd2[k][:, j:j + 1],
                                              ALU.subtract, ALU.mult)
                    m.then_inc(n1_ready, 1)
                for k in two:
                    hold(dve, up_ready, 2 * i + (k + 1))
                    dve.tensor_tensor_scan(y[k][:, :], s.lam[:, :], psU[k], 0.0, ALU.mult, ALU.add).then_inc(y_ready, 1)
                for k in two:
                    hold(dve, x1_ready, 2 * i + (k + 1))
                    link(dve.tensor_tensor(flat(x1[k]), psX[k], flat(u0[k]), ALU.add))
                    settle()
                    for j in range(TB):
                        m = dve.bn_stats(st2[k][:, j, :], x1[k][:, j, :])
                    link(m)
                    settle()
                    for j in range(TB):
                        m = dve.bn_aggr(mv2[k][:, j, :], st2[k][:, j, :])
                    m.then_inc(mv2_ready, 1)
                    hold(dve, sd2_ready, 2 * i + (k + 1))
                    link(dve.reciprocal(sd2[k][:, :], sd2[k][:, :]))
                    settle()
                    for j in range(TB):
                        m = dve.tensor_scalar(n1[k][:, j, :], x1[k][:, j, :], mv2[k][:, j, 0:1], sd2[k][:, j:j + 1],
                                              ALU.subtract, ALU.mult)
                    m.then_inc(n2_ready, 1)
                for k in two:
                    hold(dve, mlp_ready, 2 * i + (k + 1))
                    hold(dve, x1b_ready, 2 * i + (k + 1))
                    link(dve.tensor_tensor(flat(u0[k]), psT[k], flat(x1[k]), ALU.add))
                    settle()
                    xs = s.X[:, bass.ds(2 * TB * i + TB * k, TB), :]
                    link(dve.tensor_tensor(xs, xs, u0[k][:, :, :], ALU.add))
                    settle()
                assert n[0] == KCH, (n, KCH)

        @block.gpsimd
        def _(pool):
            with pool.Fori(0, B // 2) as i:
                for k in two:
                    hold(pool, n2_ready, 2 * i + (k + 1))
                    pool.tensor_tensor(x1[k][:, :, :], x1[k][:, :, :], s.b2row[:, :, :], ALU.add).then_inc(x1b_ready, 1)

        @block.scalar
        def _(act):
            with act.Fori(0, B // 2) as i:
                for k in two:
                    hold(act, u_turned, 2 * i + (k + 1))
                    act.activation(u1[k][:, :], psT[k], ACT.Identity, bias=s.vec[:, B1V:B1V + 1],
                                   scale=s.vec[:, G1:G1 + 1]).then_inc(u1_ready, 1)
                for k in two:
                    hold(act, mv2_ready, 2 * i + (k + 1))
                    act.activation(sd2[k][:, :], mv2[k][:, :, 1], ACT.Sqrt, bias=s.eps1[:, :]).then_inc(sd2_ready, 1)
                for k in two:
                    hold(act, h_turned, 2 * i + (k + 1))
                    act.activation(y[k][:, :], psT[k], ACT.Identity, bias=s.vec[:, B2V:B2V + 1],
                                   scale=s.vec[:, G2:G2 + 1]).then_inc(h_ready, 1)
                for k in two:
                    hold(act, hid_ready, 2 * i + (k + 1))
                    for c, ps in enumerate((psU[k], psX[k])):
                        m = act.activation(hm[k][:, c, :], ps, ACT.Relu, bias=s.vec[:, HB + c:HB + c + 1])
                    m.then_inc(hm_ready, 1)

        @block.tensor
        def _(pe):
            with pe.Fori(0, B // 2) as i:
                for k in two:
                    pe.wait_ge(n1_ready, 2 * i + (k + 1))
                    for j in range(TB):
                        m = pe.transpose(psT[k][:, j * P:j * P + P], n1[k][:, j, :], s.ident[:, :])
                    m.then_inc(u_turned, 1)
                for k in two:
                    pe.wait_ge(u1_ready, 2 * i + (k + 1))
                    pe.matmul(psU[k], s.winT[:, :], u1[k][:, :], start=True, stop=True).then_inc(up_ready, 1)
                for k in two:
                    pe.wait_ge(y_ready, 2 * i + (k + 1))
                    for j in range(TB):
                        o = psX[k][:, j * P:j * P + P]
                        pe.matmul(o, y[k][:, j * P:j * P + P], s.m1T[:, 0:P], start=True, stop=False)
                        m = pe.matmul(o, u1[k][:, j * P:j * P + P], s.dskip[:, :], start=False, stop=True)
                    m.then_inc(x1_ready, 1)
                for k in two:
                    pe.wait_ge(n2_ready, 2 * i + (k + 1))
                    for j in range(TB):
                        m = pe.transpose(psT[k][:, j * P:j * P + P], n1[k][:, j, :], s.ident[:, :])
                    m.then_inc(h_turned, 1)
                for k in two:
                    pe.wait_ge(h_ready, 2 * i + (k + 1))
                    for c, ps in enumerate((psU[k], psX[k])):
                        m = pe.matmul(ps, s.m1T[:, P + c * P:2 * P + c * P], y[k][:, :], start=True, stop=True)
                    m.then_inc(hid_ready, 1)
                for k in two:
                    pe.wait_ge(hm_ready, 2 * i + (k + 1))
                    for j in range(TB):
                        for c in range(F0):
                            m = pe.matmul(psT[k][:, j * P:j * P + P], hm[k][:, c, j * P:j * P + P],
                                          s.m2T[:, c * P:c * P + P], start=(c == 0), stop=(c == F0 - 1))
                    m.then_inc(mlp_ready, 1)


def normalise(dve, s, nb, mu, r, i, chain, count):
    tiles = bass.ds(TB * i, TB)
    dve.tensor_copy(mu[:, :], s.mv[:, tiles, 0])
    dve.tensor_copy(r[:, :], s.rstd[:, tiles])
    dve.tensor_copy(nb[:, :, :], s.X[:, tiles, :]).then_inc(chain, 1)
    hold(dve, chain, count)
    for j in range(TB):
        m = dve.tensor_scalar(nb[:, j, :], nb[:, j, :], mu[:, j:j + 1], r[:, j:j + 1], ALU.subtract, ALU.mult)
    return m


def route(nc, s, sem, layer):
    tag = '_' + str(layer)
    (nb_ready, turned, xs_ready, logit_ready, logit_read, xf_done, chain, exp_in, exp_ready, gates) = (
        sem(n + tag) for n in ("nb_ready", "turned", "xs_ready", "logit_ready", "logit_read", "xf_done", "chain",
                               "exp_in", "exp_ready", "gates"))
    nb, xs = s.nb, s.xs
    W = s.rT if layer == 0 else s.gateW
    two = range(2)
    psT = [s.ps[:, 512 * k:512 * k + 512] for k in two]
    psL = [s.ps[:, 512 * (2 + k):512 * (2 + k) + TB * E].rearrange("p (j e) -> p j e", e=E) for k in two]
    with nc.Block() as block:
        @block.vector
        def _(dve):
            with dve.Fori(0, B // 2) as i:
                for k in two:
                    b = 2 * i + k
                    normalise(dve, s, nb[k], s.mu[k], s.r[k], b, chain, b + 1).then_inc(nb_ready, 1)
                for k in two:
                    b = 2 * i + k
                    hold(dve, logit_ready, b + 1)
                    dve.tensor_copy(s.L[:, bass.ds(TB * b, TB), :], psL[k]).then_inc(logit_read, 1)
            dve.wait_ge(logit_read, B)
            n = [B]

            def link(ins):
                n[0] += 1
                ins.then_inc(chain, 1)
                dve.wait_ge(chain, n[0])

            wide = [P, NT, E]
            rev = s.rev[:, :].unsqueeze(1).broadcast_to(wide)
            bc = lambda t: t.unsqueeze(2).broadcast_to(wide)
            if layer == 1:
                link(dve.tensor_tensor(s.L[:, :, :], s.L[:, :, :],
                                       s.bcast[:, 2 * P:2 * P + E].unsqueeze(1).broadcast_to(wide), ALU.add))
            for top, hot in ((s.top[:, 0, :], s.hot[:, 0, :, :]), (s.top[:, 1, :], s.hot[:, 1, :, :])):
                link(dve.tensor_reduce(top, s.L[:, :, :], AX.X, ALU.max))
                link(dve.tensor_tensor(hot, s.L[:, :, :], bc(top), ALU.is_equal))
                link(dve.tensor_tensor(hot, hot, rev, ALU.mult))
                link(dve.tensor_reduce(s.gt[:, :], hot, AX.X, ALU.max))
                link(dve.tensor_tensor(hot, hot, bc(s.gt[:, :]), ALU.is_equal))
                link(dve.scalar_tensor_tensor(s.L[:, :, :], hot, -BIG, s.L[:, :, :], ALU.mult, ALU.add))
            if layer == 0:
                dve.tensor_tensor(s.top[:, 1, :], s.top[:, 1, :], s.top[:, 0, :], ALU.subtract).then_inc(exp_in, 1)
                dve.wait_ge(exp_ready, 1)
                link(dve.tensor_scalar(s.gt[:, :], s.top[:, 1, :], 1.0, None, ALU.add))
                link(dve.reciprocal(s.top[:, 0, :], s.gt[:, :]))
                link(dve.tensor_tensor(s.top[:, 1, :], s.top[:, 1, :], s.top[:, 0, :], ALU.mult))
            else:
                dve.nop().then_inc(exp_in, 1)
                dve.wait_ge(exp_ready, 1)
                link(dve.tensor_tensor(s.gt[:, :], s.top[:, 0, :], s.top[:, 1, :], ALU.add))
                link(dve.tensor_scalar(s.gt[:, :], s.gt[:, :], 1e-6, None, ALU.add))
                link(dve.reciprocal(s.gt[:, :], s.gt[:, :]))
                link(dve.tensor_tensor(s.top[:, :, :], s.top[:, :, :], s.gt[:, :].unsqueeze(1).broadcast_to([P, 2, NT]), ALU.mult))
            for k in two:
                link(dve.tensor_tensor(s.hot[:, k, :, :], s.hot[:, k, :, :], bc(s.top[:, k, :]), ALU.mult))
            dve.wait_ge(xf_done, B + 2)
            link(dve.tensor_tensor(s.gate9[:, :, 0:E], s.hot[:, 0, :, :], s.hot[:, 1, :, :], ALU.add))

        @block.scalar
        def _(act):
            with act.Fori(0, B // 2) as i:
                for k in two:
                    hold(act, turned, 2 * i + (k + 1))
                    act.activation(xs[k][:, :], psT[k], ACT.Identity).then_inc(xs_ready, 1)
            act.wait_ge(exp_in, 1)
            act.activation(s.top[:, 0:2, :] if layer else s.top[:, 1, :], s.top[:, 0:2, :] if layer else s.top[:, 1, :],
                           ACT.Sigmoid if layer else ACT.Exp).then_inc(exp_ready, 1)

        @block.gpsimd
        def _(pool):
            pool.sem_inc(xf_done, 2)
            pool.memset(s.gate9[:, :, :], 1.0)
            with pool.Fori(0, B // 2) as i:
                for k in two:
                    hold(pool, xs_ready, 2 * i + (k + 1))
                    pool.tensor_copy(s.xf[:, bass.ds(T * (2 * i + k), T)], xs[k][:, :]).then_inc(xf_done, 1)
            pool.wait_ge(xf_done, B + 2)

        @block.tensor
        def _(pe):
            with pe.Fori(0, B // 2) as i:
                for k in two:
                    pe.wait_ge(nb_ready, 2 * i + (k + 1))
                    if k == 0:
                        pe.wait_ge(xf_done, 2 * i + 2)
                    for j in range(TB):
                        m = pe.transpose(psT[k][:, j * P:j * P + P], nb[k][:, j, :], s.ident[:, :])
                    m.then_inc(turned, 1)
                for k in two:
                    pe.wait_ge(xs_ready, 2 * i + (k + 1))
                    for j in range(TB):
                        m = pe.matmul(psL[k][:, j, :], xs[k][:, j * P:j * P + P], W[:, :], start=True, stop=True)
                    m.then_inc(logit_ready, 1)


def experts(nc, s, sem, layer):
    tag = "x" + str(layer)
    (hid_ready, gelu_done, y_ready, y_read, chain, gt_in, gt_ready, gT_ready) = (
        sem(n + tag) for n in ("hid_ready", "gelu_done", "y_ready", "y_read", "chain", "gt_in", "gt_ready", "gT_ready"))
    two = range(2)
    NC = F0 if layer == 0 else F1
    NE = E + layer
    hb = s.hb
    bank = lambda k: s.ps[:, 512 * k:512 * k + 512]
    psY = [bank(4), bank(5)]
    psG, psB = s.ps[0:E + 1, 512 * 6:512 * 7], bank(7)

    def up(e, c):
        if layer == 0:
            return s.w1T[:, e, c * P:c * P + P]
        return s.up[:, e, c * P:c * P + P] if e < E else s.swup[:, c * P:c * P + P]

    def down(e, c):
        if layer == 0:
            return s.w2T[:, e * F0 + c, :]
        return s.down[:, e * F1 + c, :] if e < E else s.swdn[:, c, :]

    NP = NC // 2
    with nc.Block() as block:
        @block.tensor
        def _(pe):
            pe.sem_inc(y_ready, 1)
            with pe.Fori(0, B) as b:
                x = s.xf[:, bass.ds(T * b, T)]
                if layer == 1:
                    pe.wait_ge(gt_in, b + 1)
                    for j in range(TB):
                        m = pe.transpose(psG[:, j * P:j * P + P], s.gb[:, j, :], s.ident[:, :])
                    m.then_inc(gt_ready, 1)

                def second(e):
                    pe.wait_ge(gelu_done, NE * NP * b + (NP * (e + 1) + 2))
                    pe.wait_ge(y_read, NE * b + max(e + 1, 2))
                    for j in range(TB):
                        for c in range(NC):
                            m = pe.matmul(psY[e % 2][:, j * P:j * P + P], hb[e % 2][:, c, j * P:j * P + P], down(e, c),
                                          start=(c == 0), stop=(c == NC - 1))
                    m.then_inc(y_ready, 1)

                for e in range(NE):
                    for q in range(NP):
                        n = NP * e + q
                        pe.wait_ge(gelu_done, NE * NP * b + (n + 1))
                        for c in two:
                            m = pe.matmul(bank(2 * (n % 2) + c), up(e, 2 * q + c), x, start=True, stop=True)
                        m.then_inc(hid_ready, 1)
                    if e >= 1:
                        second(e - 1)
                second(NE - 1)
                if layer == 1:
                    pe.wait_ge(gT_ready, b + 1)
                    for j in range(TB):
                        m = pe.matmul(psB[:, j * P:j * P + P], s.gT[:, j * P:j * P + P], s.down9[:, :], start=True, stop=True)
                    m.then_inc(y_ready, 1)

        @block.scalar
        def _(act):
            act.sem_inc(gelu_done, 2)
            with act.Fori(0, B) as b:
                for e in range(NE):
                    for q in range(NP):
                        n = NP * e + q
                        hold(act, hid_ready, NE * NP * b + (n + 1))
                        if q == 0:
                            hold(act, y_ready, (NE + layer) * b + max(e, 1))
                        if layer == 0:
                            m = act.activation(hb[e % 2][:, 2 * q:2 * q + 2, :], s.ps[:, 1024 * (n % 2):1024 * (n % 2) + 1024],
                                               ACT.Gelu)
                        else:
                            for c in two:
                                col = e * F1 + 2 * q + c
                                bias = s.upb[:, col:col + 1] if e < E else s.vec[:, SBU + 2 * q + c:SBU + 2 * q + c + 1]
                                m = act.activation(hb[e % 2][:, 2 * q + c, :], bank(2 * (n % 2) + c), ACT.Gelu, bias=bias)
                        m.then_inc(gelu_done, 1)

        @block.vector
        def _(dve):
            dve.sem_inc(y_read, 2)
            NL = 7 if layer else 2
            with dve.Fori(0, B) as b:
                tiles = bass.ds(TB * b, TB)
                n = [0]

                def link(ins):
                    n[0] += 1
                    ins.then_inc(chain, 1)

                def settle():
                    hold(dve, chain, NL * b + n[0])

                m = dve.tensor_copy(s.gb[:, :, :], s.gate9[:, tiles, :])
                if layer == 1:
                    m.then_inc(gt_in, 1)
                    hold(dve, gt_ready, b + 1)
                    dve.tensor_copy(s.gT[:, :], psG).then_inc(gT_ready, 1)
                    hold(dve, gT_ready, b + 1)
                else:
                    link(m)
                    settle()
                for e in range(NE):
                    hold(dve, y_ready, (NE + layer) * b + (e + 2))
                    if e >= 1:
                        hold(dve, y_read, 2 + NE * b + e)
                    for j in range(TB):
                        if e == 0:
                            m = dve.tensor_scalar(s.acc[:, j, :], psY[0][:, j * P:j * P + P], s.gb[:, j, e:e + 1], None, ALU.mult)
                        else:
                            m = dve.scalar_tensor_tensor(s.acc[:, j, :], psY[e % 2][:, j * P:j * P + P], s.gb[:, j, e:e + 1],
                                                         s.acc[:, j, :], ALU.mult, ALU.add)
                    m.then_inc(y_read, 1)
                hold(dve, y_read, 2 + NE * b + NE)
                acc = s.acc[:, :, :]
                if layer == 1:
                    hold(dve, y_ready, (NE + 1) * b + (NE + 2))
                    link(dve.tensor_tensor(s.acc[:, :, :].rearrange("p j d -> p (j d)"), psB,
                                           s.acc[:, :, :].rearrange("p j d -> p (j d)"), ALU.add))
                    settle()
                    link(dve.tensor_scalar(acc, acc, 0.1, None, ALU.mult))
                    settle()
                    link(dve.tensor_reduce(s.mu[0][:, :], acc, AX.X, ALU.max, apply_absolute_value=True))
                    settle()
                    link(dve.tensor_scalar(s.mu[0][:, :], s.mu[0][:, :], 1e-6, None, ALU.add))
                    settle()
                    link(dve.reciprocal(s.mu[0][:, :], s.mu[0][:, :]))
                    settle()
                    link(dve.tensor_tensor(acc, acc, s.mu[0][:, :].unsqueeze(2).broadcast_to([P, TB, P]), ALU.mult))
                    settle()
                xs = s.X[:, tiles, :]
                link(dve.tensor_tensor(xs, xs, acc, ALU.add))
                settle()
                assert n[0] == NL, (n, NL)


def attention(nc, s, sem, sb):
    NCH = 5 * HG // 2
    names = ("nb_ready", "turned", "xs_ready", "q_ps", "qh_ready", "q_ready", "v_ps", "v_ready", "kz_in", "s_ready", "s_read",
             "mc_ready", "mt_ps", "q2_ready", "st_ready", "p_ready", "pv_ready", "o_ready", "ot_ps", "a_ready",
             "at_ps", "af_ready", "wo_ps", "x_done", "misc_free")
    q = {n: sem(n + "t") for n in names}
    chain = sem("chain_t")
    zeroed = sem("zeroed")
    Q, Kd = sb("Q", [P, G, T], F32R), sb("Kd", [P, G, T], F32R)
    KZ = sb("KZ", [P, H, T], F32R)
    Hs = [sb(f"Hs{k}", [P, T], F32R) for k in range(2)]
    Vz = sb("Vz", [P, TB, H, SLAB])
    Q2 = [sb(f"Q2{k}", [P, T], F32R) for k in range(2)]
    Mc = sb("Mc", [P, TB, P])
    Pb = sb("Pb", [P, 2 * NCH, T])
    m = sb("m", [P, H, TB])
    OT, AF, AT = sb("OT", [P, T]), sb("AF", [P, T]), sb("AT", [P, TB, P])
    bank = lambda k: s.ps[:, 512 * k:512 * k + 512]
    MISC, PV = bank(7), bank(6)
    rbank = lambda k: s.ps[:, 512 * k:512 * k + 512]
    NPJ = 2 * G
    units = [((0, 1), (3,)), ((2, 3), (3,)), ((0, 1), (2, 0)), ((2, 3), (2, 0)), ((0, 1, 2, 3), (1,))]
    NU = len(units)

    def place(u):
        heads, tiles = units[u]
        if len(heads) == 4:
            return [(g, 1, 256 * g) for g in heads]
        out = []
        for k, g in enumerate(heads):
            out += [(g, tiles[0], 512 * k)] + ([(g, 0, 512 * k + 384)] if len(tiles) > 1 else [])
        return out

    chunks = []
    for p in range(2):
        for g in (2 * p, 2 * p + 1):
            chunks += [[(g, 0, 0)], [(g, 1, 0), (g, 3, 384)]]
        chunks.append([(2 * p, 2, 0), (2 * p + 1, 2, 256)])
    where = {(g, kt): (c, col) for c, ch in enumerate(chunks) for g, kt, col in ch}

    with nc.Block() as block:
        @block.sync
        def _(sp):
            sp.wait_ge(zeroed, 4)
            with sp.Fori(0, B) as b:
                hold(sp, q["q_ready"], NPJ * b + NPJ)
                for g in range(HG):
                    sp.dma_start(KZ[SLAB * g:SLAB * g + SLAB, g:H:HG, :].bitcast(F32),
                                 Kd[SLAB * g:SLAB * g + SLAB, :, :].bitcast(F32))\
                      .then_inc(q["kz_in"], 16)
                hold(sp, q["kz_in"], 16 * HG * b + 16 * HG)

        @block.vector
        def _(dve):
            dve.sem_inc(q["s_read"], 2)
            dve.wait_ge(zeroed, 4)
            NL = 2 + 2 * G
            with dve.Fori(0, B) as b:
                n = [0]

                def link(ins):
                    n[0] += 1
                    ins.then_inc(chain, 1)
                    hold(dve, chain, NL * b + n[0])

                tiles = bass.ds(TB * b, TB)
                dve.tensor_copy(s.mu[0][:, :], s.mv[:, tiles, 0])
                dve.tensor_copy(s.r[0][:, :], s.rstd[:, tiles])
                link(dve.tensor_copy(s.nb[0][:, :, :], s.X[:, tiles, :]))
                for j in range(TB):
                    w = dve.tensor_scalar(s.nb[0][:, j, :], s.nb[0][:, j, :], s.mu[0][:, j:j + 1], s.r[0][:, j:j + 1],
                                          ALU.subtract, ALU.mult)
                w.then_inc(q["nb_ready"], 1)
                hold(dve, q["v_ps"], b + 1)
                dve.tensor_copy(Vz[:, :, :, 0:DH], PV.rearrange("p (j h d) -> p j h d", j=TB, d=DH)).then_inc(q["v_ready"], 1)
                for k in range(NPJ):
                    hold(dve, q["qh_ready"], NPJ * b + (k + 1))
                    dst = Q[:, k, :] if k < G else Kd[:, k - G, :]
                    dve.scalar_tensor_tensor(dst, Hs[k % 2][:, :].bitcast(F32), s.sgn[:, k // G:k // G + 1], bank(k % 4),
                                             ALU.mult, ALU.add).then_inc(q["q_ready"], 1)

                def maxima(gg):
                    for u in range(NU):
                        o = NU * gg + u
                        hold(dve, q["s_ready"], NU * G * b + (o + 1))
                        ps = s.ps[:, 1024 * (o % 2):1024 * (o % 2) + 1024]
                        heads, qt = units[u]
                        h0 = HG * gg + heads[0]
                        if len(heads) == 4:
                            w = dve.tensor_reduce(m[:, h0:h0 + 4, 1], ps.rearrange("p (h k) -> p h k", h=4), AX.X, ALU.max)
                        else:
                            v = ps.rearrange("p (h k) -> p h k", h=2)
                            if len(qt) == 1:
                                w = dve.tensor_reduce(m[:, h0:h0 + 2, 3], v, AX.X, ALU.max)
                            else:
                                dve.tensor_reduce(m[:, h0:h0 + 2, 2], v[:, :, 0:384], AX.X, ALU.max)
                                w = dve.tensor_reduce(m[:, h0:h0 + 2, 0], v[:, :, 384:512], AX.X, ALU.max)
                        w.then_inc(q["s_read"], 1)

                def shift(gg):
                    hold(dve, q["s_read"], NU * G * b + (NU * gg + NU + 2))
                    mg = m[:, HG * gg:HG * gg + HG, :].rearrange("p h t -> p t h")
                    slab = Mc[:, :, :].rearrange("p t (g c) -> p t g c", g=HG)
                    hi, lo = slab[:, :, :, 3 * DH], slab[:, :, :, 3 * DH + 1]
                    link(dve.tensor_scalar(hi.bitcast(F32R), mg, -1.0, None, ALU.mult))
                    dve.scalar_tensor_tensor(lo.bitcast(F32R), mg, -1.0, hi, ALU.mult, ALU.subtract).then_inc(q["mc_ready"], 1)
                    hold(dve, q["mt_ps"], G * b + (gg + 1))
                    dve.tensor_tensor(Q2[gg % 2][:, :], MISC, Q[:, gg, :].bitcast(F32), ALU.add).then_inc(q["q2_ready"], 1)

                def outputs(gg):
                    hold(dve, q["pv_ready"], G * b + (gg + 1))
                    dve.tensor_copy(OT[:, :], PV).then_inc(q["o_ready"], 1)
                    hold(dve, q["ot_ps"], G * b + (gg + 1))
                    v = MISC.rearrange("p (t g c) -> p t g c", t=TB, g=HG)
                    link(dve.reciprocal(s.rd[:, :, :], v[:, :, :, DH]))
                    dst = AT[:, :, HG * DH * gg:HG * DH * gg + HG * DH].rearrange("p t (g d) -> p t g d", d=DH)
                    dve.tensor_tensor(dst, v[:, :, :, 0:DH], s.rd[:, :, :].unsqueeze(3).broadcast_to([P, TB, HG, DH]), ALU.mult)\
                       .then_inc(q["a_ready"], 1)

                maxima(0)
                shift(0)
                for gg in range(G):
                    if gg + 1 < G:
                        maxima(gg + 1)
                    if gg >= 1:
                        outputs(gg - 1)
                    if gg + 1 < G:
                        shift(gg + 1)
                outputs(G - 1)
                hold(dve, q["wo_ps"], b + 1)
                xs = s.X[:, tiles, :]
                link(dve.tensor_tensor(xs, xs, MISC.rearrange("p (j d) -> p j d", j=TB), ALU.add))
                assert n[0] == NL, (n, NL)

        @block.scalar
        def _(act):
            act.sem_inc(q["p_ready"], 2)
            with act.Fori(0, B) as b:
                hold(act, q["turned"], b + 1)
                act.activation(s.xs[0][:, :], MISC, ACT.Identity).then_inc(q["xs_ready"], 1)
                for k in range(NPJ):
                    hold(act, q["q_ps"], NPJ * b + (k + 1))
                    if k >= 2:
                        hold(act, q["q_ready"], NPJ * b + (k - 1))
                    act.activation(Hs[k % 2][:, :], bank(k % 4), ACT.Identity, bias=s.sgn[:, 2:3] if k >= G else 0.0)\
                       .then_inc(q["qh_ready"], 1)
                for gg in range(G):
                    for c, ch in enumerate(chunks):
                        o = NCH * gg + c
                        hold(act, q["st_ready"], NCH * G * b + (o + 1))
                        if c == 0:
                            if gg >= 2:
                                hold(act, q["pv_ready"], G * b + (gg - 1))
                        act.activation(Pb[:, NCH * (gg % 2) + c, :], bank(4 + o % 2), ACT.Exp, scale=DH ** -0.5)\
                           .then_inc(q["p_ready"], 1)
                hold(act, q["at_ps"], b + 1)
                act.activation(AF[:, :], MISC, ACT.Identity).then_inc(q["af_ready"], 1)

        @block.gpsimd
        def _(pool):
            pool.memset(KZ[:, :, :].bitcast(F32), 0.0).then_inc(zeroed, 1)
            pool.memset(Vz[:, :, :, :], 0.0).then_inc(zeroed, 1)
            pool.memset(Mc[:, :, :], 0.0).then_inc(zeroed, 1)
            pool.wait_ge(zeroed, 3)
            pool.memset(Vz[:, :, :, DH:DH + 1], 1.0).then_inc(zeroed, 1)

        @block.tensor
        def _(pe):
            with pe.Fori(0, B) as b:
                pe.wait_ge(q["nb_ready"], b + 1)
                for j in range(TB):
                    w = pe.transpose(MISC[:, j * P:j * P + P], s.nb[0][:, j, :], s.ident[:, :])
                w.then_inc(q["turned"], 1)
                pe.wait_ge(q["xs_ready"], b + 1)
                for j in range(TB):
                    w = pe.matmul(PV[:, j * P:j * P + P], s.xs[0][:, j * P:j * P + P], s.m2T[:, 2 * P:3 * P], start=True, stop=True)
                w.then_inc(q["v_ps"], 1)
                for k in range(NPJ):
                    if k >= 4:
                        pe.wait_ge(q["q_ready"], NPJ * b + (k - 3))
                    pe.matmul(bank(k % 4), s.qkT[:, k // G, k % G, :], s.xs[0][:, :], start=True, stop=True).then_inc(q["q_ps"], 1)
                pe.wait_ge(q["q_ready"], NPJ * b + NPJ)
                pe.wait_ge(q["kz_in"], 16 * HG * b + 16 * HG)
                pe.wait_ge(q["v_ready"], b + 1)

                def row_scores(gg, first, end):
                    for u in range(first, end):
                        o = NU * gg + u
                        pe.wait_ge(q["s_read"], NU * G * b + (o + 1))
                        for g, qt, col in place(u):
                            c = 1024 * (o % 2) + col
                            w = (qt + 1) * P
                            pe.matmul(s.ps[:, c:c + w], Q[:, gg, qt * P:qt * P + P], KZ[:, HG * gg + g, 0:w], start=True, stop=False)
                            last = pe.matmul(s.ps[:, c + w - P:c + w], s.identb[:, :], s.later[:, :], start=False, stop=True)
                        last.then_inc(q["s_ready"], 1)

                def shift(gg):
                    pe.wait_ge(q["mc_ready"], G * b + (gg + 1))
                    if gg >= 2:
                        pe.wait_ge(q["a_ready"], G * b + (gg - 1))
                    for t in range(TB):
                        w = pe.transpose(MISC[:, t * P:t * P + P], Mc[:, t, :], s.ident[:, :])
                    w.then_inc(q["mt_ps"], 1)

                def weights(gg, first, end):
                    pe.wait_ge(q["q2_ready"], G * b + (gg + 1))
                    for c, ch in list(enumerate(chunks))[first:end]:
                        o = NCH * gg + c
                        pe.wait_ge(q["p_ready"], NCH * G * b + (o + 1))
                        for g, kt, col in ch:
                            ps = bank(4 + o % 2)
                            pe.matmul(ps[:, col:col + T - kt * P], KZ[:, HG * gg + g, kt * P:kt * P + P],
                                      Q2[gg % 2][:, kt * P:T], start=True, stop=False)
                            w = pe.matmul(ps[:, col:col + P], s.identb[:, :], s.laterT[:, :], start=False, stop=True)
                        w.then_inc(q["st_ready"], 1)

                def values(gg):
                    pe.wait_ge(q["p_ready"], NCH * G * b + (NCH * (gg + 1) + 2))
                    if gg >= 1:
                        pe.wait_ge(q["o_ready"], G * b + gg)
                    for kt in range(TB):
                        for g in range(HG):
                            c, col = where[g, kt]
                            w = pe.matmul(PV[SLAB * g:SLAB * g + SLAB, kt * P:T], Vz[:, kt, HG * gg + g, :],
                                          Pb[:, NCH * (gg % 2) + c, col:col + T - kt * P], start=(kt == 0), stop=(kt == TB - 1))
                    w.then_inc(q["pv_ready"], 1)

                def turn(gg):
                    pe.wait_ge(q["o_ready"], G * b + (gg + 1))
                    if gg + 1 < G:
                        pe.wait_ge(q["q2_ready"], G * b + (gg + 2))
                    for t in range(TB):
                        w = pe.transpose(MISC[:, t * P:t * P + P], OT[:, t * P:t * P + P], s.ident[:, :])
                    w.then_inc(q["ot_ps"], 1)

                row_scores(0, 0, NU)
                for gg in range(G):
                    ahead = gg + 1 < G
                    if ahead:
                        row_scores(gg + 1, 0, 2)
                    shift(gg)
                    weights(gg, 0, 4)
                    if ahead:
                        row_scores(gg + 1, 2, 3)
                    if gg >= 1:
                        values(gg - 1)
                    weights(gg, 4, 6)
                    if ahead:
                        row_scores(gg + 1, 3, 4)
                    weights(gg, 6, 8)
                    if ahead:
                        row_scores(gg + 1, 4, 5)
                    weights(gg, 8, NCH)
                    if gg >= 1:
                        turn(gg - 1)
                values(G - 1)
                turn(G - 1)
                pe.wait_ge(q["a_ready"], G * b + G)
                for t in range(TB):
                    w = pe.transpose(MISC[:, t * P:t * P + P], AT[:, t, :], s.ident[:, :])
                w.then_inc(q["at_ps"], 1)
                pe.wait_ge(q["af_ready"], b + 1)
                for j in range(TB):
                    w = pe.matmul(MISC[:, j * P:j * P + P], AF[:, j * P:j * P + P], s.m2T[:, 3 * P:4 * P], start=True, stop=True)
                w.then_inc(q["wo_ps"], 1)


def build(nc, A, out):
    with ExitStack() as ctx:
        def allocator(stack):
            return lambda name, shape, dt=F32: stack.enter_context(nc.sbuf_tensor(name, shape, dt))

        def sem(name):
            return ctx.enter_context(nc.semaphore(name))

        sb = allocator(ctx)
        hold.pace = {e.engine: sem(f"pace_{n}") for n, e in
                     (("dve", nc.vector), ("act", nc.scalar), ("pool", nc.gpsimd), ("sp", nc.sync))}

        def phase(fn, *args, buffers=True):
            with ExitStack() as own:
                fn(nc, s, *args, sem, *([allocator(own)] if buffers else []))

        s = Shared()
        s.ps = ctx.enter_context(nc.psum_tensor("ps", [P, 8 * 512], F32))
        s.X = sb("X", [P, NT, P])
        s.x_in = (s.X[:, :, :], ctx.enter_context(nc.semaphore("x_in")))
        s.ident, s.identb = sb("ident", [P, P]), sb("identb", [P, P], BF16)
        s.later, s.laterT = sb("later", [P, P], BF16), sb("laterT", [P, P], BF16)
        s.rev, s.eps1, s.eps2 = sb("rev", [P, E]), sb("eps1", [P, 1]), sb("eps2", [P, 1])
        s.junk = sb("junk", [P, 1])
        s.vec, s.upb, s.rT, s.gateW = sb("vec", [P, NVEC]), sb("upb", [P, E * F1]), sb("rT", [P, E]), sb("gateW", [P, E])
        s.bcast, s.sgn, s.lam = sb("bcast", [P, 2 * P + E]), sb("sgn", [P, 3]), sb("lam", [P, T])
        s.dskip, s.winT, s.m1T, s.m2T = sb("dskip", [P, P]), sb("winT", [P, P]), sb("m1T", [P, 3 * P]), sb("m2T", [P, 4 * P])
        s.qkT = sb("qkT", [P, 2, G, P])
        s.down9 = sb("down9", [E + 1, P])
        s.up, s.down = sb("up", [P, E, F1 * P]), sb("down", [P, E * F1, P])
        s.swup, s.swdn = sb("swup", [P, F1 * P]), sb("swdn", [P, F1, P])
        s.st, s.mvt, s.mv = sb("st", [P, TB, 6]), sb("mvt", [P, TB, 2]), sb("mv", [P, NT, 2])
        s.std, s.std2, s.rstd, s.rr = (sb(n, [P, NT]) for n in ("std", "std2", "rstd", "rr"))
        s.mu, s.r = [sb(f"muc{k}", [P, TB]) for k in range(2)], [sb(f"rc{k}", [P, TB]) for k in range(2)]
        s.rd = sb("rd", [P, TB, HG])
        s.nb, s.xs = [sb(f"nb{k}", [P, TB, P]) for k in range(2)], [sb(f"xs{k}", [P, T]) for k in range(2)]
        s.b2row = s.bcast[:, 0:P].unsqueeze(1).broadcast_to([P, TB, P])

        def ffn(layer):
            with ExitStack() as own:
                fs = allocator(own)
                s.xf = fs(f"xf{layer}", [P, B * T])
                s.L, s.hot = fs(f"L{layer}", [P, NT, E]), fs(f"hot{layer}", [P, 2, NT, E])
                s.top, s.gt = fs(f"top{layer}", [P, 2, NT]), fs(f"gt{layer}", [P, NT])
                s.gate9, s.gb = fs(f"gate9{layer}", [P, NT, E + 1]), fs(f"gb{layer}", [P, TB, E + 1])
                s.gT, s.acc = fs(f"gT{layer}", [E + 1, T]), fs(f"acc{layer}", [P, TB, P])
                s.hb = [fs(f"hb{layer}{k}", [P, F1, T]) for k in range(2)]
                phase(route_layer[layer], buffers=False)
                phase(experts_layer[layer], buffers=False)

        with ExitStack() as early:
            es = allocator(early)
            s.w1T, s.w2T = es("w1T", [P, E, F0 * P]), es("w2T", [P, E * F0, P])
            with ExitStack() as own:
                setup(nc, s, A, sem, allocator(own))
            phase(stats_a, buffers=False)
            phase(lru_block)
            phase(stats_b, buffers=False)
            ffn(0)
        phase(stats_c, buffers=False)
        phase(attention)
        phase(stats_d, buffers=False)
        ffn(1)

        stored = sem("stored")
        with nc.Block() as block:
            @block.sync
            def _(sp):
                sp.dma_start(out.rearrange("b (j p) d -> p (b j) d", p=P), s.X[:, :, :]).then_inc(stored, 16)
                sp.wait_ge(stored, 16)


def stats_a(nc, s, sem):
    token_stats(nc, s, sem, "a")


def stats_b(nc, s, sem):
    token_stats(nc, s, sem, "b")


def stats_c(nc, s, sem):
    token_stats(nc, s, sem, "c")


def stats_d(nc, s, sem):
    token_stats(nc, s, sem, "d")


def route0(nc, s, sem):
    route(nc, s, sem, 0)


def route1(nc, s, sem):
    route(nc, s, sem, 1)


def experts0(nc, s, sem):
    experts(nc, s, sem, 0)


def experts1(nc, s, sem):
    experts(nc, s, sem, 1)


route_layer, experts_layer = (route0, route1), (experts0, experts1)

_INS = ['L0_attn_x', 'L0_attn_w_in', 'L0_attn_log_lambda', 'L0_attn_w_out', 'L0_attn_D_skip', 'L0_attn_ln1_g', 'L0_attn_ln1_b', 'L0_attn_ln2_g', 'L0_attn_ln2_b', 'L0_attn_w1', 'L0_attn_b1', 'L0_attn_w2', 'L0_attn_b2', 'L0_ffn_router_w', 'L0_ffn_w1', 'L0_ffn_w2', 'L1_attn_Wq', 'L1_attn_Wk', 'L1_attn_Wv', 'L1_attn_Wo', 'L1_ffn_gate_w', 'L1_ffn_bias', 'L1_ffn_up_w', 'L1_ffn_up_b', 'L1_ffn_down_w', 'L1_ffn_down_b', 'L1_ffn_sw_up', 'L1_ffn_sb_up', 'L1_ffn_sw_down', 'L1_ffn_sb_down']


def kernel(**inputs):
    import numpy as _np
    import concourse.bacc as _bacc
    from concourse import mybir as _mybir
    from concourse.bass_utils import run_bass_kernel_spmd as _run

    nc = _bacc.Bacc("TRN2", target_bir_lowering=False, num_devices=1)
    arrays, args = {}, {}
    for name in _INS:
        a = _np.ascontiguousarray(inputs[name])
        arrays[f"in_{name}_dram"] = a
        args[name] = nc.dram_tensor(f"in_{name}_dram", a.shape, _mybir.dt.from_np(a.dtype), kind="ExternalInput").ap()
    out = nc.dram_tensor("out_0_dram", (8, 512, 128), _mybir.dt.float32, kind="ExternalOutput").ap()
    build(nc, args, out)
    r = _run(nc, [arrays], core_ids=[0])
    return r.results[0]["out_0_dram"]
```

```python
import concourse.bass as bass
from concourse import mybir
from contextlib import ExitStack

F32 = mybir.dt.float32
F32R = mybir.dt.float32r
BF16 = mybir.dt.bfloat16
I32 = mybir.dt.int32
ALU = mybir.AluOpType
ACT = mybir.ActivationFunctionType
AX = mybir.AxisListType

P = 128
B, T = 8, 512
TB = T // P
NT = B * TB
E = 8
F0 = 2
F1 = 4
H, DH = 16, 8
HG = 4
NG = 2
GT = NT // NG
GS = -(-(2 * GT + E - 1) // 8) * 8
G = H // HG
SLAB = P // HG
EPS = 1e-5
NEG = -1e30
BIG = 3e38
VEC = ['L0_attn_log_lambda', 'L0_attn_D_skip', 'L0_attn_ln1_g', 'L0_attn_ln1_b', 'L0_attn_ln2_g',
       'L0_attn_ln2_b', 'L0_attn_b1', 'L1_ffn_sb_up']
LAM, DSK, G1, B1V, G2, B2V, HB, SBU = 0, 1, 2, 3, 4, 5, 6, 8
NVEC = 12


class Shared:
    pass


def wait_apart(eng, sem, count):
    eng.wait_ge(sem, count)
    if not isinstance(count, int):
        eng.sem_inc(wait_apart.pace[eng.engine])


def setup(nc, s, A, sem, sb):
    stage = sb("stage", [P, 2 * E * F0, P])
    nat = sb("nat", [P, 10, P])
    vrow = sb("vrow", [NVEC, P])
    uprow = sb("uprow", [E * F1, P])
    rtrow = sb("rtrow", [E, P])
    brow = sb("brow", [1, 2 * P + E])
    sel = sb("sel", [1, 3, P])
    one = sb("one", [1, P])
    lamc = sb("lamc", [P, 2])
    win = sb("win", [P, P])
    wq_t = sb("wq_t", [P, 2, P])
    x_in = s.x_in
    w_in = sem("w_in")
    cst, cst2, chain, lam_in, lam_r, win_r = (sem(n) for n in ("cst", "cst2", "chain_setup", "lam_in", "lam_r", "win_r"))
    turned, evac_a, evac_v = sem("turned"), sem("evac_a"), sem("evac_v")

    jobs = []
    for e in range(0, E, 2):
        jobs.append([(stage[:, 2 * e + k, :], P) for k in range(4)] + [s.w1T[:, e:e + 2, :].rearrange("p e f -> p (e f)")])
    for e in range(0, E, 2):
        jobs.append([(stage[:, 2 * E + 2 * e + k, :], P) for k in range(4)] + [s.w2T[:, 2 * e:2 * e + 4, :].rearrange("p c d -> p (c d)")])
    jobs.append([(nat[:, k, :], P) for k in (1, 2, 3)] + [s.m1T[:, :]])
    jobs.append([(nat[:, k, :], P) for k in (4, 5, 8, 9)] + [s.m2T[:, :]])
    jobs.append([(nat[:, k, :], P) for k in (6, 7)] + [wq_t[:, :, :].rearrange("p k d -> p (k d)")])
    jobs.append([(win[:, :], P)] + [s.winT[:, :]])

    with nc.Block() as block:
        @block.sync
        def _(sp):
            for k, name in enumerate(VEC):
                r = [0, 1, 2, 3, 4, 5, 6, 8][k]
                a = A[name].rearrange("(c p) -> c p", p=P)
                sp.dma_start(vrow[r:r + a.shape[0], :], a).then_inc(w_in, 16)
            sp.dma_start(x_in[0], A['L0_attn_x'].rearrange("b (j p) d -> p (b j) d", p=P)).then_inc(x_in[1], 16)
            sp.dma_start(uprow[:, :], A['L1_ffn_up_b'].rearrange("e (c p) -> (e c) p", p=P)).then_inc(w_in, 16)
            sp.dma_start(nat[:, 0, :], A['L0_attn_w_in']).then_inc(w_in, 16)
            sp.dma_start(nat[:, 1, :], A['L0_attn_w_out']).then_inc(w_in, 16)
            sp.dma_start(nat[:, 2:4, :], A['L0_attn_w1'].rearrange("(c p) d -> p c d", p=P)).then_inc(w_in, 16)
            sp.dma_start(nat[:, 4:6, :], A['L0_attn_w2'].rearrange("p (c d) -> p c d", c=2)).then_inc(w_in, 16)
            for k, name in enumerate(['L1_attn_Wq', 'L1_attn_Wk', 'L1_attn_Wv', 'L1_attn_Wo']):
                sp.dma_start(nat[:, 6 + k, :], A[name]).then_inc(w_in, 16)
            sp.dma_start(rtrow[:, :], A['L0_ffn_router_w']).then_inc(w_in, 16)
            sp.dma_start(brow[:, 0:P], A['L0_attn_b2'].rearrange("(a n) -> a n", a=1)).then_inc(w_in, 16)
            sp.dma_start(brow[:, 2 * P:2 * P + E], A['L1_ffn_bias'].rearrange("(a n) -> a n", a=1)).then_inc(w_in, 16)
            sp.dma_start(s.down9[0:E, :], A['L1_ffn_down_b']).then_inc(w_in, 16)
            sp.dma_start(s.down9[E:E + 1, :], A['L1_ffn_sb_down'].rearrange("(a n) -> a n", a=1)).then_inc(w_in, 16)
            sp.dma_start(s.gateW[:, :], A['L1_ffn_gate_w']).then_inc(w_in, 16)
            sp.dma_start(s.swup[:, :], A['L1_ffn_sw_up']).then_inc(w_in, 16)
            sp.dma_start(s.swdn[:, :, :], A['L1_ffn_sw_down'].rearrange("(c p) d -> p c d", p=P)).then_inc(w_in, 16)
            sp.dma_start(stage[:, 0:2 * E, :], A['L0_ffn_w1'].rearrange("e (c p) d -> p (e c) d", p=P)).then_inc(w_in, 16)
            sp.dma_start(stage[:, 2 * E:4 * E, :].rearrange("p (e c) f -> p e (c f)", e=E),
                         A['L0_ffn_w2'].rearrange("e p f -> p e f")).then_inc(w_in, 16)
            sp.dma_start(s.up[:, :, :], A['L1_ffn_up_w'].rearrange("e p f -> p e f")).then_inc(w_in, 16)
            sp.dma_start(s.down[:, :, :], A['L1_ffn_down_w'].rearrange("e (c p) d -> p (e c) d", p=P)).then_inc(w_in, 16)

            sp.wait_ge(cst, 7)
            for x in s.xslots:
                sp.dma_start(x.rearrange("(n p) d -> p n d", p=P), s.zero[:, :].unsqueeze(1).broadcast_to([P, GS, P]))\
                  .then_inc(s.zeroed, 16)

        loads = len(VEC) + 14 + 1 + 6

        @block.gpsimd
        def _(pool):
            pool.memset(s.ident[:, :], 0.0).then_inc(cst, 1)
            pool.memset(s.identb[:, :], 0.0).then_inc(cst, 1)
            pool.memset(s.later[:, :], 0.0).then_inc(cst, 1)
            pool.memset(s.laterT[:, :], 0.0).then_inc(cst, 1)
            pool.memset(s.before[:, :], 1.0).then_inc(cst, 1)
            pool.memset(s.zero[:, :], 0.0).then_inc(cst, 1)
            pool.memset(s.keep[:, :], 1.0).then_inc(cst, 1)
            pool.wait_ge(cst, 7)
            pool.affine_select(out=s.before[:, :], in_=s.before[:, :], compare_op=ALU.is_gt, fill=0.0, base=0,
                               pattern=[[1, P]], channel_multiplier=-1).then_inc(cst, 1)
            pool.memset(s.keep[:, 0:NG * E * GT:GT], 0.0).then_inc(cst, 1)
            pool.memset(s.keep[:, NG * E * GT:NG * E * GT + NG * E:E], 0.0).then_inc(cst, 1)
            pool.memset(s.onesb[:, :], 1.0).then_inc(cst, 1)
            pool.iota(s.tileno[:, :], pattern=[[1, GS]], base=0, channel_multiplier=0, allow_small_or_imprecise_dtypes=True).then_inc(cst, 1)
            for m in (s.ident, s.identb):
                pool.affine_select(out=m[:, :], in_=m[:, :], compare_op=ALU.not_equal, fill=1.0, base=0,
                                   pattern=[[-1, P]], channel_multiplier=1).then_inc(cst, 1)
            pool.affine_select(out=s.later[:, :], in_=s.later[:, :], compare_op=ALU.is_ge, fill=NEG, base=0,
                               pattern=[[-1, P]], channel_multiplier=1).then_inc(cst, 1)
            pool.affine_select(out=s.laterT[:, :], in_=s.laterT[:, :], compare_op=ALU.is_ge, fill=NEG, base=0,
                               pattern=[[1, P]], channel_multiplier=-1).then_inc(cst, 1)
            for e in range(E):
                pool.memset(s.rev[:, e:e + 1], float(E - e)).then_inc(cst, 1)
            pool.memset(s.eps1[:, :], EPS).then_inc(cst, 1)
            pool.memset(s.eps2[:, :], EPS * EPS).then_inc(cst, 1)
            pool.memset(one[:, :], 1.0).then_inc(cst, 1)
            pool.memset(sel[:, :, :], 0.0).then_inc(cst, 1)
            pool.memset(s.qkT[:, :, :, :], 0.0).then_inc(cst, 1)
            pool.wait_ge(cst, 16 + E + 5)
            selv = sel[:, :, :].rearrange("p r (g c) -> p r g c", g=HG)
            pool.memset(selv[:, 0, :, DH:2 * DH], -1.0).then_inc(cst2, 1)
            pool.memset(selv[:, 1, :, 2 * DH:3 * DH], -1.0).then_inc(cst2, 1)
            pool.memset(selv[:, 1, :, 3 * DH:3 * DH + 2], 1.0).then_inc(cst2, 1)
            pool.memset(selv[:, 2, :, 3 * DH:3 * DH + 2], 1.0).then_inc(cst2, 1)

        NC1 = 16 + E + 5

        @block.scalar
        def _(act):
            act.wait_ge(evac_v, 2)
            act.activation(lamc[:, 0:1], s.vec[:, LAM:LAM + 1], ACT.Sigmoid).then_inc(lam_in, 1)
            for g in range(0, len(jobs), 2):
                act.wait_ge(turned, 5 + g + 1)
                w = P * (len(jobs[g]) - 1)
                act.copy(jobs[g][-1], s.ps[:, (g % 4) * 512:(g % 4) * 512 + w]).then_inc(evac_a, 1)

        @block.vector
        def _(dve):
            n = [0]

            def chained(ins):
                n[0] += 1
                ins.then_inc(chain, 1)
                dve.wait_ge(chain, n[0])

            bank = lambda k, w: s.ps[:, k * 512:k * 512 + w]
            dve.wait_ge(turned, 5)
            dve.tensor_copy(s.vec[:, :], bank(4, NVEC)).then_inc(evac_v, 1)
            dve.tensor_copy(s.upb[:, :], bank(5, E * F1)).then_inc(evac_v, 1)
            dve.tensor_copy(s.rT[:, :], bank(6, E)).then_inc(evac_v, 1)
            dve.tensor_copy(s.bcast[:, :], bank(7, 2 * P + E)).then_inc(evac_v, 1)
            dve.tensor_copy(s.sgn[:, :], s.ps[:, 4 * 512 + 64:4 * 512 + 67]).then_inc(evac_v, 1)
            dve.wait_ge(evac_v, 5)
            dve.wait_ge(lam_in, 1)
            chained(dve.memset(s.lam[:, :], 1.0))
            chained(dve.tensor_scalar(s.lam[:, :], s.lam[:, :], lamc[:, 0:1], None, ALU.mult))
            chained(dve.tensor_scalar(lamc[:, 1:2], lamc[:, 0:1], -1.0, 1.0, ALU.mult, ALU.add))
            dve.tensor_scalar(win[:, :], nat[:, 0, :], lamc[:, 1:2], None, ALU.mult).then_inc(win_r, 1)
            dve.tensor_scalar(s.dskip[:, :], s.ident[:, :], s.vec[:, DSK:DSK + 1], None, ALU.mult).then_inc(chain, 1)
            for g in range(1, len(jobs), 2):
                dve.wait_ge(turned, 5 + g + 1)
                w = P * (len(jobs[g]) - 1)
                dve.tensor_copy(jobs[g][-1], s.ps[:, (g % 4) * 512:(g % 4) * 512 + w]).then_inc(evac_v, 1)
            dve.wait_ge(evac_a, 6)
            for k in range(2):
                for t in range(3):
                    dve.tensor_copy(s.qkT[:, k, :, :].rearrange("p G (g c) -> p (G g) c", g=HG)[:, :, DH * t:DH * t + DH],
                                    wq_t[:, k, :].rearrange("p (h d) -> p h d", d=DH)).then_inc(chain, 1)

        @block.tensor
        def _(pe):
            pe.wait_ge(w_in, 16 * loads)
            pe.wait_ge(cst, NC1)
            pe.wait_ge(cst2, 4)
            at = lambda k, a, b: s.ps[:, k * 512 + a:k * 512 + b]
            pe.transpose(at(4, 0, NVEC), vrow[:, :], s.ident[0:NVEC, 0:NVEC]).then_inc(turned, 1)
            pe.transpose(at(5, 0, E * F1), uprow[:, :], s.ident[0:E * F1, 0:E * F1]).then_inc(turned, 1)
            pe.transpose(at(6, 0, E), rtrow[:, :], s.ident[0:E, 0:E]).then_inc(turned, 1)
            for a, b in ((0, P), (2 * P, 2 * P + E)):
                pe.matmul(at(7, a, b), one[:, :], brow[:, a:b], start=True, stop=True)
            pe.matmul(at(7, P, 2 * P), one[:, :], one[:, :], start=True, stop=True).then_inc(turned, 1)
            for r in range(3):
                m = pe.matmul(at(4, 64 + r, 65 + r), sel[:, r, :], one[:, 0:1], start=True, stop=True)
            m.then_inc(turned, 1)
            for g, job in enumerate(jobs):
                if g >= 4:
                    pe.wait_ge(*((evac_a, (g - 4) // 2 + 1) if g % 2 == 0 else (evac_v, 5 + (g - 4) // 2 + 1)))
                if g == len(jobs) - 1:
                    pe.wait_ge(win_r, 1)
                for k, (src, rows) in enumerate(job[:-1]):
                    m = pe.transpose(at(g % 4, k * P, k * P + P), src, s.ident[:, :])
                m.then_inc(turned, 1)


def token_stats(nc, s, k):
    st_ready, mv_ready, std_ready, done = s.stats_sems
    stds = k + (k > 0)
    with nc.Block() as block:
        @block.vector
        def _(dve):
            if k == 0:
                dve.wait_ge(s.x_in[1], 16)
            with dve.Fori(0, B) as i:
                for j in range(TB):
                    m = dve.bn_stats(s.st[:, j, :], s.X[:, bass.ds(TB * i + j, 1), :])
                m.then_inc(st_ready, 1)
                wait_apart(dve, st_ready, i + (B * k + 1))
                for j in range(TB):
                    m = dve.bn_aggr(s.mvt[:, j, :], s.st[:, j, :])
                m.then_inc(mv_ready, 1)
                dve.wait_ge(mv_ready, 2 * i + (2 * B * k + 1))
                dve.tensor_copy(s.mv[:, bass.ds(TB * i, TB), :], s.mvt[:, :, :]).then_inc(mv_ready, 1)
            dve.wait_ge(std_ready, stds + 1)
            dve.reciprocal(s.rstd[:, :], s.std[:, :]).then_inc(done, 1)
            if k == 0:
                dve.wait_ge(std_ready, 2)
                dve.reciprocal(s.rr[:, :], s.std2[:, :]).then_inc(done, 1)
            dve.wait_ge(done, stds + 1 + (k == 0))

        @block.scalar
        def _(act):
            act.wait_ge(mv_ready, 2 * B * (k + 1))
            act.activation(s.std[:, :], s.mv[:, :, 1], ACT.Sqrt, bias=s.eps1[:, :]).then_inc(std_ready, 1)
            if k == 0:
                act.activation(s.std2[:, :], s.mv[:, :, 1], ACT.Sqrt, bias=s.eps2[:, :], scale=1.0 + EPS)\
                   .then_inc(std_ready, 1)


def lru_block(nc, s, sem, sb):
    two = range(2)
    u0 = [sb(f"u0{k}", [P, TB, P]) for k in two]
    n1 = [sb(f"n1{k}", [P, TB, P]) for k in two]
    u1 = [sb(f"u1{k}", [P, T]) for k in two]
    y = [sb(f"y{k}", [P, T]) for k in two]
    x1 = [sb(f"x1{k}", [P, TB, P]) for k in two]
    hm = [sb(f"hm{k}", [P, F0, T]) for k in two]
    st2 = [sb(f"st2{k}", [P, TB, 6]) for k in two]
    mv2 = [sb(f"mv2{k}", [P, TB, 2]) for k in two]
    mu = [sb(f"mu{k}", [P, TB]) for k in two]
    r0 = [sb(f"r0{k}", [P, TB]) for k in two]
    sd2 = [sb(f"sd2{k}", [P, TB]) for k in two]
    names = ("n1_ready", "u_turned", "u1_ready", "up_ready", "y_ready", "x1_ready", "mv2_ready", "sd2_ready", "n2_ready",
             "h_turned", "h_ready", "hid_ready", "hm_ready", "mlp_ready", "x_done", "x1b_ready")
    (n1_ready, u_turned, u1_ready, up_ready, y_ready, x1_ready, mv2_ready, sd2_ready, n2_ready,
     h_turned, h_ready, hid_ready, hm_ready, mlp_ready, x_done, x1b_ready) = (sem(n) for n in names)
    chain = sem("chain_lru")
    psT = [s.ps[:, 512 * k:512 * k + 512] for k in (0, 1)]
    psU = [s.ps[:, 512 * k:512 * k + 512] for k in (2, 3)]
    psX = [s.ps[:, 512 * k:512 * k + 512] for k in (4, 5)]
    flat = lambda t: t[:, :, :].rearrange("p j d -> p (j d)")
    KCH = 12

    with nc.Block() as block:
        @block.vector
        def _(dve):
            with dve.Fori(0, B // 2) as i:
                n = [0]

                def link(ins):
                    n[0] += 1
                    ins.then_inc(chain, 1)

                def settle():
                    dve.wait_ge(chain, KCH * i + n[0])

                for k in two:
                    tiles = bass.ds(2 * TB * i + TB * k, TB)
                    dve.tensor_copy(mu[k][:, :], s.mv[:, tiles, 0])
                    dve.tensor_copy(r0[k][:, :], s.rstd[:, tiles])
                    dve.tensor_copy(sd2[k][:, :], s.rr[:, tiles])
                    link(dve.tensor_copy(x1[k][:, :, :], s.X[:, tiles, :]))
                    settle()
                    for j in range(TB):
                        dve.tensor_scalar(u0[k][:, j, :], x1[k][:, j, :], mu[k][:, j:j + 1], r0[k][:, j:j + 1],
                                          ALU.subtract, ALU.mult)
                    for j in range(TB):
                        m = dve.tensor_scalar(n1[k][:, j, :], x1[k][:, j, :], mu[k][:, j:j + 1], sd2[k][:, j:j + 1],
                                              ALU.subtract, ALU.mult)
                    m.then_inc(n1_ready, 1)
                for k in two:
                    dve.wait_ge(up_ready, 2 * i + (k + 1))
                    dve.tensor_tensor_scan(y[k][:, :], s.lam[:, :], psU[k], 0.0, ALU.mult, ALU.add).then_inc(y_ready, 1)
                for k in two:
                    dve.wait_ge(x1_ready, 2 * i + (k + 1))
                    link(dve.tensor_tensor(flat(x1[k]), psX[k], flat(u0[k]), ALU.add))
                    settle()
                    for j in range(TB):
                        m = dve.bn_stats(st2[k][:, j, :], x1[k][:, j, :])
                    link(m)
                    wait_apart(dve, chain, KCH * i + n[0])
                    for j in range(TB):
                        m = dve.bn_aggr(mv2[k][:, j, :], st2[k][:, j, :])
                    m.then_inc(mv2_ready, 1)
                    dve.wait_ge(sd2_ready, 2 * i + (k + 1))
                    link(dve.reciprocal(sd2[k][:, :], sd2[k][:, :]))
                    settle()
                    for j in range(TB):
                        m = dve.tensor_scalar(n1[k][:, j, :], x1[k][:, j, :], mv2[k][:, j, 0:1], sd2[k][:, j:j + 1],
                                              ALU.subtract, ALU.mult)
                    m.then_inc(n2_ready, 1)
                for k in two:
                    dve.wait_ge(mlp_ready, 2 * i + (k + 1))
                    dve.wait_ge(x1b_ready, 2 * i + (k + 1))
                    link(dve.tensor_tensor(flat(u0[k]), psT[k], flat(x1[k]), ALU.add))
                    settle()
                    xs = s.X[:, bass.ds(2 * TB * i + TB * k, TB), :]
                    link(dve.tensor_tensor(xs, xs, u0[k][:, :, :], ALU.add))
                    settle()
                assert n[0] == KCH, (n, KCH)

        @block.gpsimd
        def _(pool):
            with pool.Fori(0, B // 2) as i:
                for k in two:
                    pool.wait_ge(n2_ready, 2 * i + (k + 1))
                    pool.tensor_tensor(x1[k][:, :, :], x1[k][:, :, :], s.b2row[:, :, :], ALU.add).then_inc(x1b_ready, 1)

        @block.scalar
        def _(act):
            with act.Fori(0, B // 2) as i:
                for k in two:
                    act.wait_ge(u_turned, 2 * i + (k + 1))
                    act.activation(u1[k][:, :], psT[k], ACT.Identity, bias=s.vec[:, B1V:B1V + 1],
                                   scale=s.vec[:, G1:G1 + 1]).then_inc(u1_ready, 1)
                for k in two:
                    act.wait_ge(mv2_ready, 2 * i + (k + 1))
                    act.activation(sd2[k][:, :], mv2[k][:, :, 1], ACT.Sqrt, bias=s.eps1[:, :]).then_inc(sd2_ready, 1)
                for k in two:
                    act.wait_ge(h_turned, 2 * i + (k + 1))
                    act.activation(y[k][:, :], psT[k], ACT.Identity, bias=s.vec[:, B2V:B2V + 1],
                                   scale=s.vec[:, G2:G2 + 1]).then_inc(h_ready, 1)
                for k in two:
                    act.wait_ge(hid_ready, 2 * i + (k + 1))
                    for c, ps in enumerate((psU[k], psX[k])):
                        m = act.activation(hm[k][:, c, :], ps, ACT.Relu, bias=s.vec[:, HB + c:HB + c + 1])
                    m.then_inc(hm_ready, 1)

        @block.tensor
        def _(pe):
            with pe.Fori(0, B // 2) as i:
                for k in two:
                    pe.wait_ge(n1_ready, 2 * i + (k + 1))
                    for j in range(TB):
                        m = pe.transpose(psT[k][:, j * P:j * P + P], n1[k][:, j, :], s.ident[:, :])
                    m.then_inc(u_turned, 1)
                for k in two:
                    pe.wait_ge(u1_ready, 2 * i + (k + 1))
                    pe.matmul(psU[k], s.winT[:, :], u1[k][:, :], start=True, stop=True).then_inc(up_ready, 1)
                for k in two:
                    pe.wait_ge(y_ready, 2 * i + (k + 1))
                    for j in range(TB):
                        o = psX[k][:, j * P:j * P + P]
                        pe.matmul(o, y[k][:, j * P:j * P + P], s.m1T[:, 0:P], start=True, stop=False)
                        m = pe.matmul(o, u1[k][:, j * P:j * P + P], s.dskip[:, :], start=False, stop=True)
                    m.then_inc(x1_ready, 1)
                for k in two:
                    pe.wait_ge(n2_ready, 2 * i + (k + 1))
                    for j in range(TB):
                        m = pe.transpose(psT[k][:, j * P:j * P + P], n1[k][:, j, :], s.ident[:, :])
                    m.then_inc(h_turned, 1)
                for k in two:
                    pe.wait_ge(h_ready, 2 * i + (k + 1))
                    for c, ps in enumerate((psU[k], psX[k])):
                        m = pe.matmul(ps, s.m1T[:, P + c * P:2 * P + c * P], y[k][:, :], start=True, stop=True)
                    m.then_inc(hid_ready, 1)
                for k in two:
                    pe.wait_ge(hm_ready, 2 * i + (k + 1))
                    for j in range(TB):
                        for c in range(F0):
                            m = pe.matmul(psT[k][:, j * P:j * P + P], hm[k][:, c, j * P:j * P + P],
                                          s.m2T[:, c * P:c * P + P], start=(c == 0), stop=(c == F0 - 1))
                    m.then_inc(mlp_ready, 1)


def normalise(dve, s, nb, mu, r, i, chain, count):
    tiles = bass.ds(TB * i, TB)
    dve.tensor_copy(mu[:, :], s.mv[:, tiles, 0])
    dve.tensor_copy(r[:, :], s.rstd[:, tiles])
    dve.tensor_copy(nb[:, :, :], s.X[:, tiles, :]).then_inc(chain, 1)
    dve.wait_ge(chain, count)
    for j in range(TB):
        m = dve.tensor_scalar(nb[:, j, :], nb[:, j, :], mu[:, j:j + 1], r[:, j:j + 1], ALU.subtract, ALU.mult)
    return m


def route(nc, s, sem, layer):
    tag = "_" + str(layer)
    (nb_ready, turned, xs_ready, xn_ready, logit_ready, logit_read, xf_done, chain, exp_in, exp_ready, mb_ready,
     rank_ps) = (
        sem(n + tag) for n in ("nb_ready", "turned", "xs_ready", "xn_ready", "logit_ready", "logit_read", "xf_done",
                               "chain", "exp_in", "exp_ready", "mb_ready", "rank_ps"))
    nb, xs = s.nb, s.xs
    W = s.rT if layer == 0 else s.gateW
    two = range(2)
    psT = [s.ps[:, 512 * k:512 * k + 512] for k in two]
    psL = [s.ps[:, 512 * (2 + k):512 * (2 + k) + TB * E].rearrange("p (j e) -> p j e", e=E) for k in two]
    psR, psC = s.ps[:, 4 * 512:4 * 512 + NT * E], s.ps[:, 5 * 512:5 * 512 + NT * E]
    with nc.Block() as block:
        @block.vector
        def _(dve):
            with dve.Fori(0, B // 2) as i:
                for k in two:
                    b = 2 * i + k
                    dve.wait_ge(xn_ready, b + 1)
                    normalise(dve, s, nb[k], s.mu[k], s.r[k], b, chain, b + 1).then_inc(nb_ready, 1)
                for k in two:
                    b = 2 * i + k
                    dve.wait_ge(logit_ready, b + 1)
                    dve.tensor_copy(s.L[:, bass.ds(TB * b, TB), :], psL[k]).then_inc(logit_read, 1)
            dve.wait_ge(logit_read, B)
            n = [B]

            def link(ins):
                n[0] += 1
                ins.then_inc(chain, 1)
                dve.wait_ge(chain, n[0])

            wide = [P, NT, E]
            rev = s.rev[:, :].unsqueeze(1).broadcast_to(wide)
            bc = lambda t: t.unsqueeze(2).broadcast_to(wide)
            if layer == 1:
                link(dve.tensor_tensor(s.L[:, :, :], s.L[:, :, :],
                                       s.bcast[:, 2 * P:2 * P + E].unsqueeze(1).broadcast_to(wide), ALU.add))
            for top, hot in ((s.top[:, 0, :], s.hot[:, 0, :, :]), (s.top[:, 1, :], s.hot[:, 1, :, :])):
                link(dve.tensor_reduce(top, s.L[:, :, :], AX.X, ALU.max))
                link(dve.tensor_tensor(hot, s.L[:, :, :], bc(top), ALU.is_equal))
                link(dve.tensor_tensor(hot, hot, rev, ALU.mult))
                link(dve.tensor_reduce(s.gt[:, :], hot, AX.X, ALU.max))
                link(dve.tensor_tensor(hot, hot, bc(s.gt[:, :]), ALU.is_equal))
                link(dve.scalar_tensor_tensor(s.L[:, :, :], hot, -BIG, s.L[:, :, :], ALU.mult, ALU.add))
            by_group = lambda t: t.rearrange("p (g j) e -> p g j e", g=NG)
            Mb = s.Mb[:, :, :, :].rearrange("p g e j -> p g j e")
            dve.tensor_tensor(Mb, by_group(s.hot[:, 0, :, :]), by_group(s.hot[:, 1, :, :]), ALU.add).then_inc(mb_ready, 1)
            if layer == 0:
                dve.tensor_tensor(s.top[:, 1, :], s.top[:, 1, :], s.top[:, 0, :], ALU.subtract).then_inc(exp_in, 1)
                dve.wait_ge(exp_ready, 1)
                link(dve.tensor_scalar(s.gt[:, :], s.top[:, 1, :], 1.0, None, ALU.add))
                link(dve.reciprocal(s.top[:, 0, :], s.gt[:, :]))
                link(dve.tensor_tensor(s.top[:, 1, :], s.top[:, 1, :], s.top[:, 0, :], ALU.mult))
            else:
                dve.nop().then_inc(exp_in, 1)
                dve.wait_ge(exp_ready, 1)
                link(dve.tensor_tensor(s.gt[:, :], s.top[:, 0, :], s.top[:, 1, :], ALU.add))
                link(dve.tensor_scalar(s.gt[:, :], s.gt[:, :], 1e-6, None, ALU.add))
                link(dve.reciprocal(s.gt[:, :], s.gt[:, :]))
                link(dve.tensor_tensor(s.top[:, :, :], s.top[:, :, :], s.gt[:, :].unsqueeze(1).broadcast_to([P, 2, NT]), ALU.mult))
                for k in two:
                    link(dve.tensor_tensor(s.wg[:, k, :, :], s.hot[:, k, :, :], bc(s.top[:, k, :]), ALU.mult))
                dve.wait_ge(xf_done, B + 2)
                link(dve.tensor_tensor(s.gate9[:, :, 0:E], s.wg[:, 0, :, :], s.wg[:, 1, :, :], ALU.add))
            dve.wait_ge(rank_ps, 1)
            GE = NG * E
            C = s.C[:, :, :]
            flatC = C.rearrange("p a j -> p (a j)")
            link(dve.tensor_tensor_scan(flatC, s.keep[:, 0:GE * GT], psC, 0.0, ALU.mult, ALU.add))
            link(dve.tensor_copy(s.tot[:, :], C[:, :, GT - 1]))
            link(dve.tensor_tensor(flatC, flatC, psC, ALU.subtract))
            link(dve.tensor_tensor(flatC, flatC, psR, ALU.add))
            link(dve.tensor_scalar(s.toti[:, :], s.tot[:, :], float(P - 1), None, ALU.add))
            link(dve.tensor_scalar(s.toti[:, :], s.toti[:, :], 7, None, ALU.arith_shift_right))
            link(dve.tensor_copy(s.tot[:, :], s.toti[:, :]))
            link(dve.tensor_tensor_scan(s.ends[:, :], s.keep[:, GE * GT:GE * GT + GE], s.tot[:, :], 0.0, ALU.mult, ALU.add))
            link(dve.tensor_tensor(s.tot[:, :], s.ends[:, :], s.tot[:, :], ALU.subtract))
            link(dve.tensor_scalar(s.tot[:, :], s.tot[:, :], float(P), None, ALU.mult))
            link(dve.tensor_tensor(C, C, s.tot[:, :].unsqueeze(2).broadcast_to([P, GE, GT]), ALU.add))
            pos = C.rearrange("p (g e) j -> p g j e", g=NG)
            for k in two:
                hot = by_group(s.hot[:, k, :, :])
                link(dve.tensor_tensor(hot, hot, pos, ALU.mult))
                link(dve.tensor_reduce(s.gt[:, :], s.hot[:, k, :, :], AX.X, ALU.add))
                link(dve.tensor_copy(s.slot[:, k, :], s.gt[:, :]))
            for g in range(NG):
                cmp = s.cmp[0:1, :, :]
                link(dve.tensor_tensor(cmp, s.tileno[0:1, :].unsqueeze(2).broadcast_to([1, GS, E]),
                                       s.ends[0:1, E * g:E * g + E].unsqueeze(1).broadcast_to([1, GS, E]), ALU.is_ge))
                link(dve.tensor_reduce(s.tef[0:1, GS * g:GS * g + GS], cmp, AX.X, ALU.add))
            link(dve.tensor_scalar(s.te[0:1, :], s.tef[0:1, :], float(E - 1), None, ALU.min))

        @block.scalar
        def _(act):
            act.sem_inc(xn_ready, 2)
            with act.Fori(0, B // 2) as i:
                for k in two:
                    b = 2 * i + k
                    act.wait_ge(nb_ready, b + 1)
                    act.activation(s.XN[:, bass.ds(TB * b, TB), :], nb[k][:, :, :], ACT.Identity).then_inc(xn_ready, 1)
                    act.wait_ge(turned, b + 1)
                    act.activation(xs[k][:, :], psT[k], ACT.Identity).then_inc(xs_ready, 1)
            act.wait_ge(exp_in, 1)
            top = s.top[:, 0:2, :] if layer else s.top[:, 1, :]
            act.activation(top, top, ACT.Sigmoid if layer else ACT.Exp).then_inc(exp_ready, 1)

        @block.gpsimd
        def _(pool):
            pool.sem_inc(xf_done, 2)
            if layer == 1:
                pool.memset(s.gate9[:, :, :], 1.0)
                with pool.Fori(0, B // 2) as i:
                    for k in two:
                        pool.wait_ge(xs_ready, 2 * i + (k + 1))
                        pool.tensor_copy(s.xf[:, bass.ds(T * (2 * i + k), T)], xs[k][:, :]).then_inc(xf_done, 1)
                pool.wait_ge(xf_done, B + 2)

        @block.tensor
        def _(pe):
            with pe.Fori(0, B // 2) as i:
                for k in two:
                    pe.wait_ge(nb_ready, 2 * i + (k + 1))
                    if k == 0 and layer == 1:
                        pe.wait_ge(xf_done, 2 * i + 2)
                    for j in range(TB):
                        m = pe.transpose(psT[k][:, j * P:j * P + P], nb[k][:, j, :], s.ident[:, :])
                    m.then_inc(turned, 1)
                for k in two:
                    pe.wait_ge(xs_ready, 2 * i + (k + 1))
                    for j in range(TB):
                        m = pe.matmul(psL[k][:, j, :], xs[k][:, j * P:j * P + P], W[:, :], start=True, stop=True)
                    m.then_inc(logit_ready, 1)
            pe.wait_ge(mb_ready, 1)
            Mb = s.Mb[:, :, :, :].rearrange("p g e j -> p (g e j)")
            pe.matmul(psR, s.before[:, :], Mb, start=True, stop=True)
            pe.matmul(psC, s.onesb[:, :], Mb, start=True, stop=True).then_inc(rank_ps, 1)


def experts(nc, s, sem, layer, out=None):
    tag = "x" + str(layer)

    def sems(name, count):
        return [sem(f"{name}{k}{tag}") for k in range(count)]

    BT = 2 * TB
    GB = GS // BT
    BODIES = NG * GB
    GD = GT // TB
    two = range(2)
    scattered, x_load, w_load, stored, gathered = (sems("scattered", NG), sems("x_load", 2), sems("w_load", BT),
                                                   sems("stored", 2), sems("gathered", GD))
    (x_turned, xT_ready, hid_ready, gelu_done, y_ready, yb_ready, combined, chain) = (
        sem(n + tag) for n in ("x_turned", "xT_ready", "hid_ready", "gelu_done", "y_ready", "yb_ready", "combined", "chain"))
    if layer == 1:
        gb_ready, gT_ps, gT_ready, sh_ready, sg_done, sy_ready, sy_read, x_done, x_out = (
            sem(n + tag) for n in ("gb_ready", "gT_ps", "gT_ready", "sh_ready", "sg_done", "sy_ready", "sy_read", "x_done", "x_out"))
    NC = F0 if layer == 0 else F1
    bank = lambda k: s.ps[:, 512 * k:512 * k + 512]
    psT, psY, psH = [bank(0), bank(1)], [bank(2), bank(3)], [bank(4), bank(5)]
    psG, psS = s.ps[0:E + 1, 512 * 6:512 * 7], bank(7)
    W1 = s.w1T if layer == 0 else s.up
    W2 = s.w2T if layer == 0 else s.down
    xrows = [x.rearrange("(n p) d -> p n d", p=P) for x in s.xslots]
    yrows = [y.rearrange("(n p) d -> p n d", p=P) for y in s.yslots]
    xt, xT, wst, hb, yb, YG = s.xt, s.xT, s.wst, s.hb, s.yb, s.YG
    flat = lambda t: t.rearrange("p j d -> p (j d)")

    def expert(eng, i, t):
        return eng.value_load(s.te[0:1, bass.ds(BT * i + t, 1)], min_val=0, max_val=E - 1)

    with nc.Block() as block:
        @block.sync
        def _(sp):
            def loads(g, n):
                i = n + g * GB
                for r in two:
                    wait_apart(sp, x_turned, 2 * i + (r + 1))
                    sp.dma_start(xt[r][:, :, :], xrows[g][:, bass.ds(BT * n + TB * r, TB), :]).then_inc(x_load[r], 16)
                    for t in range(TB * r, TB * r + TB):
                        wait_apart(sp, hid_ready, BT * i + (t + 1))
                        e = expert(sp, i, t)
                        sp.dma_start(wst[t][:, :], W1[:, bass.ds(e, 1), :].rearrange("p e f -> p (e f)"))\
                          .then_inc(w_load[t], 16)

            def stores(g, n):
                i = n + g * GB
                for r in two:
                    wait_apart(sp, yb_ready, 2 * i + (r + 3))
                    sp.dma_start(yrows[g][:, bass.ds(BT * n + TB * r, TB), :], yb[r][:, :, :]).then_inc(stored[r], 16)

            for g in range(NG):
                sp.wait_ge(scattered[g], 16 * 2 * GT)
                loads(g, 0)
                if g > 0:
                    stores(g - 1, GB - 1)
                with sp.Fori(0, GB - 1) as n:
                    loads(g, n + 1)
                    stores(g, n)
            stores(NG - 1, GB - 1)
            if layer == 1:
                for b in range(B):
                    sp.wait_ge(x_done, b + 1)
                    sp.dma_start(out[b].rearrange("(j p) d -> p j d", p=P), s.X[:, TB * b:TB * b + TB, :]).then_inc(x_out, 16)
                sp.wait_ge(x_out, 16 * B)
            for r in two:
                sp.wait_ge(stored[r], 16 * BODIES)

        @block.gpsimd
        def _(pool):
            if layer == 0:
                pool.wait_ge(s.zeroed, 16 * NG)
            for j in range(NT):
                for k in two:
                    pool.indirect_dma_start(out=s.xslots[j // GT][:, :], out_offset=bass.IndirectOffsetOnAxis(ap=s.slot[:, k, j:j + 1], axis=0),
                                            in_=s.XN[:, j, :], in_offset=None).then_inc(scattered[j // GT], 16)
            for g in range(NG):
                for r in two:
                    pool.wait_ge(stored[r], 16 * GB * (g + 1))
                for b in range(GD):
                    if g > 0:
                        pool.wait_ge(combined, GD * (g - 1) + b + 1)
                    for j in range(TB):
                        for k in two:
                            pool.indirect_dma_start(out=YG[:, TB * b + j, k, :], out_offset=None, in_=s.yslots[g][:, :],
                                                    in_offset=bass.IndirectOffsetOnAxis(
                                                        ap=s.slot[:, k, GT * g + TB * b + j:GT * g + TB * b + j + 1], axis=0))\
                                .then_inc(gathered[b], 16)

        @block.scalar
        def _(act):
            act.sem_inc(gelu_done, 2)
            if layer == 1:
                act.sem_inc(sg_done, 2)
                with act.Fori(0, B) as b:
                    for c in range(NC):
                        act.wait_ge(sh_ready, NC * b + (c + 1))
                        if c == 0:
                            act.wait_ge(sy_ready, b + 1)
                        act.activation(s.hs[:, c, :], psH[c % 2], ACT.Gelu, bias=s.vec[:, SBU + c:SBU + c + 1]).then_inc(sg_done, 1)
            with act.Fori(0, BODIES) as i:
                for t in range(BT):
                    if layer == 1:
                        e = expert(act, i, t)
                    act.wait_ge(hid_ready, BT * i + (t + 1 + BT))
                    act.wait_ge(y_ready, BT * i + (t + 1))
                    if layer == 0:
                        m = act.activation(hb[t % 2][:, 0:NC * P], psH[t % 2][:, 0:NC * P], ACT.Gelu)
                    else:
                        for c in range(NC):
                            m = act.activation(hb[t % 2][:, c * P:c * P + P], psH[t % 2][:, c * P:c * P + P], ACT.Gelu,
                                               bias=s.upb[:, bass.ds(e * NC + c, 1)])
                    m.then_inc(gelu_done, 1)

        @block.vector
        def _(dve):
            dve.sem_inc(yb_ready, 2)
            if layer == 1:
                with dve.Fori(0, B) as b:
                    tiles = bass.ds(TB * b, TB)
                    dve.tensor_copy(s.gb[:, :, :], s.gate9[:, tiles, :]).then_inc(gb_ready, 1)
                    dve.wait_ge(gT_ps, b + 1)
                    dve.tensor_copy(s.gT[:, :], psG).then_inc(gT_ready, 1)
                    dve.wait_ge(sy_ready, b + 2)
                    dve.tensor_copy(s.SH[:, tiles, :], psS.rearrange("p (j d) -> p j d", j=TB)).then_inc(sy_read, 1)

            def turned(i, r):
                dve.wait_ge(x_turned, 2 * i + (r + 3))
                dve.tensor_copy(xT[r][:, :], psT[r]).then_inc(xT_ready, 1)

            def outputs(i, r):
                dve.wait_ge(y_ready, BT * i + (TB * r + TB + 2))
                dve.wait_ge(stored[r], 16 * i) if not isinstance(i, int) else (dve.wait_ge(stored[r], 16 * i) if i else None)
                dve.tensor_copy(flat(yb[r][:, :, :]), psY[r]).then_inc(yb_ready, 1)

            for r in two:
                turned(0, r)

            def body(i, more):
                outputs(i, 0)
                if more:
                    turned(i + 1, 0)
                    turned(i + 1, 1)
                outputs(i, 1)

            body(0, True)
            with dve.Fori(1, BODIES - 1) as i:
                body(i, True)
            body(BODIES - 1, False)

            n = [0]

            def link(ins):
                n[0] += 1
                ins.then_inc(chain, 1)
                dve.wait_ge(chain, n[0])

            for b in range(B):
                g, w = b // GD, b % GD
                dve.wait_ge(gathered[w], 16 * 2 * TB * (g + 1))
                rows = YG[:, TB * w:TB * w + TB, :, :]
                gates = s.top[:, :, TB * b:TB * b + TB].rearrange("p k t -> p t k").unsqueeze(3).broadcast_to([P, TB, 2, P])
                link(dve.tensor_tensor(rows, rows, gates, ALU.mult))
                xs = s.X[:, TB * b:TB * b + TB, :]
                acc = s.acc[:, :, :]
                dve.tensor_tensor(acc, rows[:, :, 0, :], rows[:, :, 1, :], ALU.add).then_inc(combined, 1)
                dve.wait_ge(combined, b + 1)
                if layer == 1:
                    link(dve.tensor_tensor(acc, acc, s.SH[:, TB * b:TB * b + TB, :], ALU.add))
                    link(dve.tensor_scalar(acc, acc, 0.1, None, ALU.mult))
                    link(dve.tensor_reduce(s.mu[0][:, :], acc, AX.X, ALU.max, apply_absolute_value=True))
                    link(dve.tensor_scalar(s.mu[0][:, :], s.mu[0][:, :], 1e-6, None, ALU.add))
                    link(dve.reciprocal(s.mu[0][:, :], s.mu[0][:, :]))
                    link(dve.tensor_tensor(acc, acc, s.mu[0][:, :].unsqueeze(2).broadcast_to([P, TB, P]), ALU.mult))
                    dve.tensor_tensor(xs, xs, acc, ALU.add).then_inc(x_done, 1)
                    dve.wait_ge(x_done, b + 1)
                else:
                    link(dve.tensor_tensor(xs, xs, acc, ALU.add))

        @block.tensor
        def _(pe):
            pe.sem_inc(x_turned, 2)
            pe.sem_inc(hid_ready, BT)
            pe.sem_inc(y_ready, 2)
            if layer == 1:
                pe.sem_inc(sy_ready, 1)
                with pe.Fori(0, B) as b:
                    x = s.xf[:, bass.ds(T * b, T)]
                    for c in range(NC):
                        pe.wait_ge(sg_done, NC * b + (c + 1))
                        pe.matmul(psH[c % 2], s.swup[:, c * P:c * P + P], x, start=True, stop=True).then_inc(sh_ready, 1)
                    pe.wait_ge(gb_ready, b + 1)
                    for j in range(TB):
                        m = pe.transpose(psG[:, j * P:j * P + P], s.gb[:, j, :], s.ident[:, :])
                    m.then_inc(gT_ps, 1)
                    pe.wait_ge(gT_ready, b + 1)
                    pe.wait_ge(sg_done, NC * b + (NC + 2))
                    for j in range(TB):
                        o = psS[:, j * P:j * P + P]
                        for c in range(NC):
                            pe.matmul(o, s.hs[:, c, j * P:j * P + P], s.swdn[:, c, :], start=(c == 0), stop=False)
                        m = pe.matmul(o, s.gT[:, j * P:j * P + P], s.down9[:, :], start=False, stop=True)
                    m.then_inc(sy_ready, 1)

            def turn(i, r):
                pe.wait_ge(x_load[r], 16 * i + 16)
                for j in range(TB):
                    m = pe.transpose(psT[r][:, j * P:j * P + P], xt[r][:, j, :], s.ident[:, :])
                m.then_inc(x_turned, 1)

            def first(i, t):
                r = t // TB
                pe.wait_ge(w_load[t], 16 * i + 16)
                if t % TB == 0:
                    pe.wait_ge(xT_ready, 2 * i + (r + 1))
                pe.wait_ge(gelu_done, BT * i + (t + 1))
                for c in range(NC):
                    m = pe.matmul(psH[t % 2][:, c * P:c * P + P], wst[t][:, c * P:c * P + P],
                                  xT[r][:, (t % TB) * P:(t % TB) * P + P], start=True, stop=True)
                m.then_inc(hid_ready, 1)

            def second(i, t):
                r = t // TB
                e = expert(pe, i, t)
                pe.wait_ge(gelu_done, BT * i + (t + 3))
                if t % TB == 0:
                    pe.wait_ge(yb_ready, 2 * i + (r + 1))
                for c in range(NC):
                    m = pe.matmul(psY[r][:, (t % TB) * P:(t % TB) * P + P], hb[t % 2][:, c * P:c * P + P],
                                  W2[:, bass.ds(e * NC + c, 1), :].rearrange("p e d -> p (e d)"),
                                  start=(c == 0), stop=(c == NC - 1))
                m.then_inc(y_ready, 1)

            def body(i, more):
                for t in range(BT):
                    first(i, t)
                    if t >= 1:
                        second(i, t - 1)
                    if t == TB and more:
                        turn(i + 1, 0)
                if more:
                    turn(i + 1, 1)
                second(i, BT - 1)

            turn(0, 0)
            turn(0, 1)
            with pe.Fori(0, BODIES - 1) as i:
                body(i, True)
            body(BODIES - 1, False)


def attention(nc, s, sem, sb):
    NCH = 5 * HG // 2
    names = ("nb_ready", "turned", "xs_ready", "q_ps", "qh_ready", "q_ready", "v_ps", "v_ready", "kz_in", "s_ready", "s_read",
             "mc_ready", "mt_ps", "q2_ready", "st_ready", "p_ready", "pv_ready", "o_ready", "ot_ps", "a_ready",
             "at_ps", "af_ready", "wo_ps", "x_done", "misc_free")
    q = {n: sem(n + "t") for n in names}
    chain = sem("chain_t")
    zeroed = sem("zeroed")
    Q, Kd = sb("Q", [P, G, T], F32R), sb("Kd", [P, G, T], F32R)
    KZ = sb("KZ", [P, H, T], F32R)
    Hs = [sb(f"Hs{k}", [P, T], F32R) for k in range(2)]
    Vz = sb("Vz", [P, TB, H, SLAB])
    Q2 = [sb(f"Q2{k}", [P, T], F32R) for k in range(2)]
    Mc = sb("Mc", [P, TB, P])
    Pb = sb("Pb", [P, 2 * NCH, T])
    m = sb("m", [P, H, TB])
    OT, AF, AT = sb("OT", [P, T]), sb("AF", [P, T]), sb("AT", [P, TB, P])
    bank = lambda k: s.ps[:, 512 * k:512 * k + 512]
    MISC, PV = bank(7), bank(6)
    rbank = lambda k: s.ps[:, 512 * k:512 * k + 512]
    NPJ = 2 * G
    units = [((0, 1), (3,)), ((2, 3), (3,)), ((0, 1), (2, 0)), ((2, 3), (2, 0)), ((0, 1, 2, 3), (1,))]
    NU = len(units)

    def place(u):
        heads, tiles = units[u]
        if len(heads) == 4:
            return [(g, 1, 256 * g) for g in heads]
        out = []
        for k, g in enumerate(heads):
            out += [(g, tiles[0], 512 * k)] + ([(g, 0, 512 * k + 384)] if len(tiles) > 1 else [])
        return out

    chunks = []
    for p in range(2):
        for g in (2 * p, 2 * p + 1):
            chunks += [[(g, 0, 0)], [(g, 1, 0), (g, 3, 384)]]
        chunks.append([(2 * p, 2, 0), (2 * p + 1, 2, 256)])
    where = {(g, kt): (c, col) for c, ch in enumerate(chunks) for g, kt, col in ch}

    with nc.Block() as block:
        @block.sync
        def _(sp):
            sp.wait_ge(zeroed, 4)
            with sp.Fori(0, B) as b:
                wait_apart(sp, q["q_ready"], NPJ * b + NPJ)
                for g in range(HG):
                    sp.dma_start(KZ[SLAB * g:SLAB * g + SLAB, g:H:HG, :].bitcast(F32),
                                 Kd[SLAB * g:SLAB * g + SLAB, :, :].bitcast(F32))\
                      .then_inc(q["kz_in"], 16)
                wait_apart(sp, q["kz_in"], 16 * HG * b + 16 * HG)

        @block.vector
        def _(dve):
            dve.sem_inc(q["s_read"], 2)
            dve.wait_ge(zeroed, 4)
            NL = 2 + 2 * G
            with dve.Fori(0, B) as b:
                n = [0]

                def link(ins):
                    n[0] += 1
                    ins.then_inc(chain, 1)
                    dve.wait_ge(chain, NL * b + n[0])

                tiles = bass.ds(TB * b, TB)
                dve.tensor_copy(s.mu[0][:, :], s.mv[:, tiles, 0])
                dve.tensor_copy(s.r[0][:, :], s.rstd[:, tiles])
                link(dve.tensor_copy(s.nb[0][:, :, :], s.X[:, tiles, :]))
                for j in range(TB):
                    w = dve.tensor_scalar(s.nb[0][:, j, :], s.nb[0][:, j, :], s.mu[0][:, j:j + 1], s.r[0][:, j:j + 1],
                                          ALU.subtract, ALU.mult)
                w.then_inc(q["nb_ready"], 1)
                dve.wait_ge(q["v_ps"], b + 1)
                dve.tensor_copy(Vz[:, :, :, 0:DH], PV.rearrange("p (j h d) -> p j h d", j=TB, d=DH)).then_inc(q["v_ready"], 1)
                for k in range(NPJ):
                    dve.wait_ge(q["qh_ready"], NPJ * b + (k + 1))
                    dst = Q[:, k, :] if k < G else Kd[:, k - G, :]
                    dve.scalar_tensor_tensor(dst, Hs[k % 2][:, :].bitcast(F32), s.sgn[:, k // G:k // G + 1], bank(k % 4),
                                             ALU.mult, ALU.add).then_inc(q["q_ready"], 1)

                def maxima(gg):
                    for u in range(NU):
                        o = NU * gg + u
                        dve.wait_ge(q["s_ready"], NU * G * b + (o + 1))
                        ps = s.ps[:, 1024 * (o % 2):1024 * (o % 2) + 1024]
                        heads, qt = units[u]
                        h0 = HG * gg + heads[0]
                        if len(heads) == 4:
                            w = dve.tensor_reduce(m[:, h0:h0 + 4, 1], ps.rearrange("p (h k) -> p h k", h=4), AX.X, ALU.max)
                        else:
                            v = ps.rearrange("p (h k) -> p h k", h=2)
                            if len(qt) == 1:
                                w = dve.tensor_reduce(m[:, h0:h0 + 2, 3], v, AX.X, ALU.max)
                            else:
                                dve.tensor_reduce(m[:, h0:h0 + 2, 2], v[:, :, 0:384], AX.X, ALU.max)
                                w = dve.tensor_reduce(m[:, h0:h0 + 2, 0], v[:, :, 384:512], AX.X, ALU.max)
                        w.then_inc(q["s_read"], 1)

                def shift(gg):
                    dve.wait_ge(q["s_read"], NU * G * b + (NU * gg + NU + 2))
                    mg = m[:, HG * gg:HG * gg + HG, :].rearrange("p h t -> p t h")
                    slab = Mc[:, :, :].rearrange("p t (g c) -> p t g c", g=HG)
                    hi, lo = slab[:, :, :, 3 * DH], slab[:, :, :, 3 * DH + 1]
                    link(dve.tensor_scalar(hi.bitcast(F32R), mg, -1.0, None, ALU.mult))
                    dve.scalar_tensor_tensor(lo.bitcast(F32R), mg, -1.0, hi, ALU.mult, ALU.subtract).then_inc(q["mc_ready"], 1)
                    dve.wait_ge(q["mt_ps"], G * b + (gg + 1))
                    dve.tensor_tensor(Q2[gg % 2][:, :], MISC, Q[:, gg, :].bitcast(F32), ALU.add).then_inc(q["q2_ready"], 1)

                def outputs(gg):
                    dve.wait_ge(q["pv_ready"], G * b + (gg + 1))
                    dve.tensor_copy(OT[:, :], PV).then_inc(q["o_ready"], 1)
                    dve.wait_ge(q["ot_ps"], G * b + (gg + 1))
                    v = MISC.rearrange("p (t g c) -> p t g c", t=TB, g=HG)
                    link(dve.reciprocal(s.rd[:, :, :], v[:, :, :, DH]))
                    dst = AT[:, :, HG * DH * gg:HG * DH * gg + HG * DH].rearrange("p t (g d) -> p t g d", d=DH)
                    dve.tensor_tensor(dst, v[:, :, :, 0:DH], s.rd[:, :, :].unsqueeze(3).broadcast_to([P, TB, HG, DH]), ALU.mult)\
                       .then_inc(q["a_ready"], 1)

                maxima(0)
                shift(0)
                for gg in range(G):
                    if gg + 1 < G:
                        maxima(gg + 1)
                    if gg >= 1:
                        outputs(gg - 1)
                    if gg + 1 < G:
                        shift(gg + 1)
                outputs(G - 1)
                dve.wait_ge(q["wo_ps"], b + 1)
                xs = s.X[:, tiles, :]
                link(dve.tensor_tensor(xs, xs, MISC.rearrange("p (j d) -> p j d", j=TB), ALU.add))
                assert n[0] == NL, (n, NL)

        @block.scalar
        def _(act):
            act.sem_inc(q["p_ready"], 2)
            with act.Fori(0, B) as b:
                act.wait_ge(q["turned"], b + 1)
                act.activation(s.xs[0][:, :], MISC, ACT.Identity).then_inc(q["xs_ready"], 1)
                for k in range(NPJ):
                    act.wait_ge(q["q_ps"], NPJ * b + (k + 1))
                    if k >= 2:
                        act.wait_ge(q["q_ready"], NPJ * b + (k - 1))
                    act.activation(Hs[k % 2][:, :], bank(k % 4), ACT.Identity, bias=s.sgn[:, 2:3] if k >= G else 0.0)\
                       .then_inc(q["qh_ready"], 1)
                for gg in range(G):
                    for c, ch in enumerate(chunks):
                        o = NCH * gg + c
                        act.wait_ge(q["st_ready"], NCH * G * b + (o + 1))
                        if c == 0:
                            if gg >= 2:
                                act.wait_ge(q["pv_ready"], G * b + (gg - 1))
                        act.activation(Pb[:, NCH * (gg % 2) + c, :], bank(4 + o % 2), ACT.Exp, scale=DH ** -0.5)\
                           .then_inc(q["p_ready"], 1)
                act.wait_ge(q["at_ps"], b + 1)
                act.activation(AF[:, :], MISC, ACT.Identity).then_inc(q["af_ready"], 1)

        @block.gpsimd
        def _(pool):
            pool.memset(KZ[:, :, :].bitcast(F32), 0.0).then_inc(zeroed, 1)
            pool.memset(Vz[:, :, :, :], 0.0).then_inc(zeroed, 1)
            pool.memset(Mc[:, :, :], 0.0).then_inc(zeroed, 1)
            pool.wait_ge(zeroed, 3)
            pool.memset(Vz[:, :, :, DH:DH + 1], 1.0).then_inc(zeroed, 1)

        @block.tensor
        def _(pe):
            with pe.Fori(0, B) as b:
                pe.wait_ge(q["nb_ready"], b + 1)
                for j in range(TB):
                    w = pe.transpose(MISC[:, j * P:j * P + P], s.nb[0][:, j, :], s.ident[:, :])
                w.then_inc(q["turned"], 1)
                pe.wait_ge(q["xs_ready"], b + 1)
                for j in range(TB):
                    w = pe.matmul(PV[:, j * P:j * P + P], s.xs[0][:, j * P:j * P + P], s.m2T[:, 2 * P:3 * P], start=True, stop=True)
                w.then_inc(q["v_ps"], 1)
                for k in range(NPJ):
                    if k >= 4:
                        pe.wait_ge(q["q_ready"], NPJ * b + (k - 3))
                    pe.matmul(bank(k % 4), s.qkT[:, k // G, k % G, :], s.xs[0][:, :], start=True, stop=True).then_inc(q["q_ps"], 1)
                pe.wait_ge(q["q_ready"], NPJ * b + NPJ)
                pe.wait_ge(q["kz_in"], 16 * HG * b + 16 * HG)
                pe.wait_ge(q["v_ready"], b + 1)

                def row_scores(gg, first, end):
                    for u in range(first, end):
                        o = NU * gg + u
                        pe.wait_ge(q["s_read"], NU * G * b + (o + 1))
                        for g, qt, col in place(u):
                            c = 1024 * (o % 2) + col
                            w = (qt + 1) * P
                            pe.matmul(s.ps[:, c:c + w], Q[:, gg, qt * P:qt * P + P], KZ[:, HG * gg + g, 0:w], start=True, stop=False)
                            last = pe.matmul(s.ps[:, c + w - P:c + w], s.identb[:, :], s.later[:, :], start=False, stop=True)
                        last.then_inc(q["s_ready"], 1)

                def shift(gg):
                    pe.wait_ge(q["mc_ready"], G * b + (gg + 1))
                    if gg >= 2:
                        pe.wait_ge(q["a_ready"], G * b + (gg - 1))
                    for t in range(TB):
                        w = pe.transpose(MISC[:, t * P:t * P + P], Mc[:, t, :], s.ident[:, :])
                    w.then_inc(q["mt_ps"], 1)

                def weights(gg, first, end):
                    pe.wait_ge(q["q2_ready"], G * b + (gg + 1))
                    for c, ch in list(enumerate(chunks))[first:end]:
                        o = NCH * gg + c
                        pe.wait_ge(q["p_ready"], NCH * G * b + (o + 1))
                        for g, kt, col in ch:
                            ps = bank(4 + o % 2)
                            pe.matmul(ps[:, col:col + T - kt * P], KZ[:, HG * gg + g, kt * P:kt * P + P],
                                      Q2[gg % 2][:, kt * P:T], start=True, stop=False)
                            w = pe.matmul(ps[:, col:col + P], s.identb[:, :], s.laterT[:, :], start=False, stop=True)
                        w.then_inc(q["st_ready"], 1)

                def values(gg):
                    pe.wait_ge(q["p_ready"], NCH * G * b + (NCH * (gg + 1) + 2))
                    if gg >= 1:
                        pe.wait_ge(q["o_ready"], G * b + gg)
                    for kt in range(TB):
                        for g in range(HG):
                            c, col = where[g, kt]
                            w = pe.matmul(PV[SLAB * g:SLAB * g + SLAB, kt * P:T], Vz[:, kt, HG * gg + g, :],
                                          Pb[:, NCH * (gg % 2) + c, col:col + T - kt * P], start=(kt == 0), stop=(kt == TB - 1))
                    w.then_inc(q["pv_ready"], 1)

                def turn(gg):
                    pe.wait_ge(q["o_ready"], G * b + (gg + 1))
                    if gg + 1 < G:
                        pe.wait_ge(q["q2_ready"], G * b + (gg + 2))
                    for t in range(TB):
                        w = pe.transpose(MISC[:, t * P:t * P + P], OT[:, t * P:t * P + P], s.ident[:, :])
                    w.then_inc(q["ot_ps"], 1)

                row_scores(0, 0, NU)
                for gg in range(G):
                    ahead = gg + 1 < G
                    if ahead:
                        row_scores(gg + 1, 0, 2)
                    shift(gg)
                    weights(gg, 0, 4)
                    if ahead:
                        row_scores(gg + 1, 2, 3)
                    if gg >= 1:
                        values(gg - 1)
                    weights(gg, 4, 6)
                    if ahead:
                        row_scores(gg + 1, 3, 4)
                    weights(gg, 6, 8)
                    if ahead:
                        row_scores(gg + 1, 4, 5)
                    weights(gg, 8, NCH)
                    if gg >= 1:
                        turn(gg - 1)
                values(G - 1)
                turn(G - 1)
                pe.wait_ge(q["a_ready"], G * b + G)
                for t in range(TB):
                    w = pe.transpose(MISC[:, t * P:t * P + P], AT[:, t, :], s.ident[:, :])
                w.then_inc(q["at_ps"], 1)
                pe.wait_ge(q["af_ready"], b + 1)
                for j in range(TB):
                    w = pe.matmul(MISC[:, j * P:j * P + P], AF[:, j * P:j * P + P], s.m2T[:, 3 * P:4 * P], start=True, stop=True)
                w.then_inc(q["wo_ps"], 1)


def build(nc, A, out):
    with ExitStack() as ctx:
        def allocator(stack):
            return lambda name, shape, dt=F32: stack.enter_context(nc.sbuf_tensor(name, shape, dt))

        def sem(name):
            return ctx.enter_context(nc.semaphore(name))

        sb = allocator(ctx)
        wait_apart.pace = {e.engine: sem(f"pace_{n}") for n, e in
                     (("dve", nc.vector), ("sp", nc.sync))}

        def phase(fn, *args, buffers=True):
            with ExitStack() as own:
                fn(nc, s, *args, sem, *([allocator(own)] if buffers else []))

        s = Shared()
        s.ps = ctx.enter_context(nc.psum_tensor("ps", [P, 8 * 512], F32))
        s.X = sb("X", [P, NT, P])
        s.x_in = (s.X[:, :, :], ctx.enter_context(nc.semaphore("x_in")))
        s.ident, s.identb = sb("ident", [P, P]), sb("identb", [P, P], BF16)
        s.later, s.laterT = sb("later", [P, P], BF16), sb("laterT", [P, P], BF16)
        s.rev, s.eps1, s.eps2 = sb("rev", [P, E]), sb("eps1", [P, 1]), sb("eps2", [P, 1])
        s.junk = sb("junk", [P, 1])
        s.vec, s.upb, s.rT, s.gateW = sb("vec", [P, NVEC]), sb("upb", [P, E * F1]), sb("rT", [P, E]), sb("gateW", [P, E])
        s.bcast, s.sgn, s.lam = sb("bcast", [P, 2 * P + E]), sb("sgn", [P, 3]), sb("lam", [P, T])
        s.dskip, s.winT, s.m1T, s.m2T = sb("dskip", [P, P]), sb("winT", [P, P]), sb("m1T", [P, 3 * P]), sb("m2T", [P, 4 * P])
        s.zero = sb("zero", [P, P])
        s.before, s.onesb = sb("before", [P, P], BF16), sb("onesb", [P, P], BF16)
        s.keep, s.tileno = sb("keep", [P, NG * E * GT + NG * E]), sb("tileno", [1, GS])
        s.xslots, s.yslots = ([nc.dram_tensor(f"{n}slots{g}", (GS * P, P), F32, kind="Internal").ap() for g in range(NG)]
                              for n in "xy")
        s.zeroed = sem("slots_zeroed")
        s.stats_sems = [sem(f"stats_{n}") for n in ("st", "mv", "std", "done")]
        s.qkT = sb("qkT", [P, 2, G, P])
        s.down9 = sb("down9", [E + 1, P])
        s.up, s.down = sb("up", [P, E, F1 * P]), sb("down", [P, E * F1, P])
        s.swup, s.swdn = sb("swup", [P, F1 * P]), sb("swdn", [P, F1, P])
        s.st, s.mvt, s.mv = sb("st", [P, TB, 6]), sb("mvt", [P, TB, 2]), sb("mv", [P, NT, 2])
        s.std, s.std2, s.rstd, s.rr = (sb(n, [P, NT]) for n in ("std", "std2", "rstd", "rr"))
        s.mu, s.r = [sb(f"muc{k}", [P, TB]) for k in range(2)], [sb(f"rc{k}", [P, TB]) for k in range(2)]
        s.rd = sb("rd", [P, TB, HG])
        s.nb, s.xs = [sb(f"nb{k}", [P, TB, P]) for k in range(2)], [sb(f"xs{k}", [P, T]) for k in range(2)]
        s.b2row = s.bcast[:, 0:P].unsqueeze(1).broadcast_to([P, TB, P])

        def ffn(layer):
            with ExitStack() as own:
                fs = allocator(own)
                s.XN = fs(f"XN{layer}", [P, NT, P])
                if layer == 1:
                    s.xf = fs("xf", [P, B * T])
                    s.SH = fs("SH", [P, NT, P])
                    s.hs = fs("hs", [P, F1, T])
                    s.wg = fs("wg", [P, 2, NT, E])
                s.L, s.hot = fs(f"L{layer}", [P, NT, E]), fs(f"hot{layer}", [P, 2, NT, E])
                s.top, s.gt = fs(f"top{layer}", [P, 2, NT]), fs(f"gt{layer}", [P, NT])
                s.gate9, s.gb = fs(f"gate9{layer}", [P, NT, E + 1]), fs(f"gb{layer}", [P, TB, E + 1])
                s.gT, s.acc = fs(f"gT{layer}", [E + 1, T]), fs(f"acc{layer}", [P, TB, P])
                s.slot, s.te = fs(f"slot{layer}", [P, 2, NT], I32), fs(f"te{layer}", [1, NG * GS], I32)
                s.tef, s.cmp = fs(f"tef{layer}", [1, NG * GS]), fs(f"cmp{layer}", [1, GS, E])
                s.Mb = fs(f"Mb{layer}", [P, NG, E, GT], BF16)
                s.C, s.tot, s.ends = fs(f"C{layer}", [P, NG * E, GT]), fs(f"tot{layer}", [P, NG * E]), fs(f"ends{layer}", [P, NG * E])
                s.toti = fs(f"toti{layer}", [P, NG * E], I32)
                NC = F1 if layer else F0
                s.xt = [fs(f"xt{layer}{k}", [P, TB, P]) for k in range(2)]
                s.xT = [fs(f"xT{layer}{k}", [P, T]) for k in range(2)]
                s.wst = [fs(f"wst{layer}{k}", [P, NC * P]) for k in range(2 * TB)]
                s.hb = [fs(f"hb{layer}{k}", [P, NC * P]) for k in range(2)]
                s.yb = [fs(f"yb{layer}{k}", [P, TB, P]) for k in range(2)]
                s.YG = fs(f"YG{layer}", [P, GT, 2, P])
                phase(route_layer[layer], buffers=False)
                phase(experts_layer[layer], *([out] if layer else []), buffers=False)

        with ExitStack() as early:
            es = allocator(early)
            s.w1T, s.w2T = es("w1T", [P, E, F0 * P]), es("w2T", [P, E * F0, P])
            with ExitStack() as own:
                setup(nc, s, A, sem, allocator(own))
            phase(stats_a, buffers=False)
            phase(lru_block)
            phase(stats_b, buffers=False)
            ffn(0)
        phase(stats_c, buffers=False)
        phase(attention)
        phase(stats_d, buffers=False)
        ffn(1)


def stats_a(nc, s, sem):
    token_stats(nc, s, 0)


def stats_b(nc, s, sem):
    token_stats(nc, s, 1)


def stats_c(nc, s, sem):
    token_stats(nc, s, 2)


def stats_d(nc, s, sem):
    token_stats(nc, s, 3)


def route0(nc, s, sem):
    route(nc, s, sem, 0)


def route1(nc, s, sem):
    route(nc, s, sem, 1)


def experts0(nc, s, sem):
    experts(nc, s, sem, 0)


def experts1(nc, s, out, sem):
    experts(nc, s, sem, 1, out)


route_layer, experts_layer = (route0, route1), (experts0, experts1)

_INS = ['L0_attn_x', 'L0_attn_w_in', 'L0_attn_log_lambda', 'L0_attn_w_out', 'L0_attn_D_skip', 'L0_attn_ln1_g', 'L0_attn_ln1_b', 'L0_attn_ln2_g', 'L0_attn_ln2_b', 'L0_attn_w1', 'L0_attn_b1', 'L0_attn_w2', 'L0_attn_b2', 'L0_ffn_router_w', 'L0_ffn_w1', 'L0_ffn_w2', 'L1_attn_Wq', 'L1_attn_Wk', 'L1_attn_Wv', 'L1_attn_Wo', 'L1_ffn_gate_w', 'L1_ffn_bias', 'L1_ffn_up_w', 'L1_ffn_up_b', 'L1_ffn_down_w', 'L1_ffn_down_b', 'L1_ffn_sw_up', 'L1_ffn_sb_up', 'L1_ffn_sw_down', 'L1_ffn_sb_down']


def kernel(**inputs):
    import numpy as _np
    import concourse.bacc as _bacc
    from concourse import mybir as _mybir
    from concourse.bass_utils import run_bass_kernel_spmd as _run

    nc = _bacc.Bacc("TRN2", target_bir_lowering=False, num_devices=1)
    arrays, args = {}, {}
    for name in _INS:
        a = _np.ascontiguousarray(inputs[name])
        arrays[f"in_{name}_dram"] = a
        args[name] = nc.dram_tensor(f"in_{name}_dram", a.shape, _mybir.dt.from_np(a.dtype), kind="ExternalInput").ap()
    out = nc.dram_tensor("out_0_dram", (8, 512, 128), _mybir.dt.float32, kind="ExternalOutput").ap()
    build(nc, args, out)
    r = _run(nc, [arrays], core_ids=[0])
    return r.results[0]["out_0_dram"]
```

```python
import concourse.bass as bass
from concourse import mybir
from contextlib import ExitStack

F32 = mybir.dt.float32
F32R = mybir.dt.float32r
BF16 = mybir.dt.bfloat16
I32 = mybir.dt.int32
ALU = mybir.AluOpType
ACT = mybir.ActivationFunctionType
AX = mybir.AxisListType

P = 128
B, T = 8, 512
TB = T // P
NT = B * TB
E = 8
F0 = 2
F1 = 4
H, DH = 16, 8
HG = 4
NG = 2
GT = NT // NG
GS = -(-(2 * GT + E - 1) // 8) * 8
G = H // HG
SLAB = P // HG
EPS = 1e-5
NEG = -1e30
BIG = 3e38
VEC = ['L0_attn_log_lambda', 'L0_attn_D_skip', 'L0_attn_ln1_g', 'L0_attn_ln1_b', 'L0_attn_ln2_g',
       'L0_attn_ln2_b', 'L0_attn_b1', 'L1_ffn_sb_up']
LAM, DSK, G1, B1V, G2, B2V, HB, SBU = 0, 1, 2, 3, 4, 5, 6, 8
NVEC = 12


class Shared:
    pass


def wait_apart(eng, sem, count):
    eng.wait_ge(sem, count)
    if not isinstance(count, int):
        eng.sem_inc(wait_apart.pace[eng.engine])


def setup(nc, s, A, sem, sb):
    nat = sb("nat", [P, 10, P])
    vrow = sb("vrow", [NVEC, P])
    uprow = sb("uprow", [E * F1, P])
    rtrow = sb("rtrow", [E, P])
    brow = sb("brow", [1, 2 * P + E])
    sel = sb("sel", [1, 3, P])
    one = sb("one", [1, P])
    stats = sb("stats", [P, NT, 6])
    lamc = sb("lamc", [P, 2])
    win = sb("win", [P, P])
    wq_t = sb("wq_t", [P, 2, P])
    x_in = s.x_in
    w_in = sem("w_in")
    cst, cst2, chain, lam_in, win_r = (sem(n) for n in ("cst", "cst2", "chain_setup", "lam_in", "win_r"))
    turned, evac_a, evac_v = sem("turned"), sem("evac_a"), sem("evac_v")

    jobs = [([nat[:, k, :] for k in (1, 2, 3)], s.m1T[:, :]),
            ([nat[:, k, :] for k in (4, 5, 8, 9)], s.m2T[:, :]),
            ([nat[:, k, :] for k in (6, 7)], wq_t[:, :, :].rearrange("p k d -> p (k d)")),
            ([win[:, :]], s.winT[:, :])]

    with nc.Block() as block:
        @block.sync
        def _(sp):
            sp.dma_start(s.X[:, :, :], A['L0_attn_x'].rearrange("b (j p) d -> p (b j) d", p=P)).then_inc(x_in, 16)
            for k, name in enumerate(VEC):
                r = [0, 1, 2, 3, 4, 5, 6, 8][k]
                a = A[name].rearrange("(c p) -> c p", p=P)
                sp.dma_start(vrow[r:r + a.shape[0], :], a).then_inc(w_in, 16)
            sp.dma_start(uprow[:, :], A['L1_ffn_up_b'].rearrange("e (c p) -> (e c) p", p=P)).then_inc(w_in, 16)
            sp.dma_start(nat[:, 0, :], A['L0_attn_w_in']).then_inc(w_in, 16)
            sp.dma_start(nat[:, 1, :], A['L0_attn_w_out']).then_inc(w_in, 16)
            sp.dma_start(nat[:, 2:4, :], A['L0_attn_w1'].rearrange("(c p) d -> p c d", p=P)).then_inc(w_in, 16)
            sp.dma_start(nat[:, 4:6, :], A['L0_attn_w2'].rearrange("p (c d) -> p c d", c=2)).then_inc(w_in, 16)
            for k, name in enumerate(['L1_attn_Wq', 'L1_attn_Wk', 'L1_attn_Wv', 'L1_attn_Wo']):
                sp.dma_start(nat[:, 6 + k, :], A[name]).then_inc(w_in, 16)
            sp.dma_start(rtrow[:, :], A['L0_ffn_router_w']).then_inc(w_in, 16)
            sp.dma_start(brow[:, 0:P], A['L0_attn_b2'].rearrange("(a n) -> a n", a=1)).then_inc(w_in, 16)
            sp.dma_start(brow[:, 2 * P:2 * P + E], A['L1_ffn_bias'].rearrange("(a n) -> a n", a=1)).then_inc(w_in, 16)
            sp.dma_start(s.down9[0:E, :], A['L1_ffn_down_b']).then_inc(w_in, 16)
            sp.dma_start(s.down9[E:E + 1, :], A['L1_ffn_sb_down'].rearrange("(a n) -> a n", a=1)).then_inc(w_in, 16)
            sp.dma_start(s.gateW[:, :], A['L1_ffn_gate_w']).then_inc(w_in, 16)
            sp.dma_start(s.swup[:, :], A['L1_ffn_sw_up']).then_inc(w_in, 16)
            sp.dma_start(s.swdn[:, :, :], A['L1_ffn_sw_down'].rearrange("(c p) d -> p c d", p=P)).then_inc(w_in, 16)
            sp.dma_start(s.stage[:, 0:2 * E, :], A['L0_ffn_w1'].rearrange("e (c p) d -> p (e c) d", p=P)).then_inc(s.w0_in, 16)
            sp.dma_start(s.stage[:, 2 * E:4 * E, :].rearrange("p (e c) f -> p e (c f)", e=E),
                         A['L0_ffn_w2'].rearrange("e p f -> p e f")).then_inc(s.w0_in, 16)
            sp.dma_start(s.up[:, :, :], A['L1_ffn_up_w'].rearrange("e p f -> p e f")).then_inc(s.w1_in, 16)
            sp.dma_start(s.down[:, :, :], A['L1_ffn_down_w'].rearrange("e (c p) d -> p (e c) d", p=P)).then_inc(s.w1_in, 16)

            sp.wait_ge(cst, 7)
            for x in s.xslots:
                sp.dma_start(x.rearrange("(n p) d -> p n d", p=P), s.zero[:, :].unsqueeze(1).broadcast_to([P, GS, P]))\
                  .then_inc(s.zeroed, 16)

        loads = len(VEC) + 17
        CONSTANTS = 21 + E

        @block.gpsimd
        def _(pool):
            pool.memset(s.ident[:, :], 0.0).then_inc(cst, 1)
            pool.memset(s.identb[:, :], 0.0).then_inc(cst, 1)
            pool.memset(s.later[:, :], 0.0).then_inc(cst, 1)
            pool.memset(s.laterT[:, :], 0.0).then_inc(cst, 1)
            pool.memset(s.before[:, :], 1.0).then_inc(cst, 1)
            pool.memset(s.zero[:, :], 0.0).then_inc(cst, 1)
            pool.memset(s.keep[:, :], 1.0).then_inc(cst, 1)
            pool.wait_ge(cst, 7)
            pool.affine_select(out=s.before[:, :], in_=s.before[:, :], compare_op=ALU.is_gt, fill=0.0, base=0,
                               pattern=[[1, P]], channel_multiplier=-1).then_inc(cst, 1)
            pool.memset(s.keep[:, 0:NG * E * GT:GT], 0.0).then_inc(cst, 1)
            pool.memset(s.keep[:, NG * E * GT:NG * E * GT + NG * E:E], 0.0).then_inc(cst, 1)
            pool.memset(s.onesb[:, :], 1.0).then_inc(cst, 1)
            pool.iota(s.tileno[:, :], pattern=[[1, GS]], base=0, channel_multiplier=0, allow_small_or_imprecise_dtypes=True).then_inc(cst, 1)
            for m in (s.ident, s.identb):
                pool.affine_select(out=m[:, :], in_=m[:, :], compare_op=ALU.not_equal, fill=1.0, base=0,
                                   pattern=[[-1, P]], channel_multiplier=1).then_inc(cst, 1)
            pool.affine_select(out=s.later[:, :], in_=s.later[:, :], compare_op=ALU.is_ge, fill=NEG, base=0,
                               pattern=[[-1, P]], channel_multiplier=1).then_inc(cst, 1)
            pool.affine_select(out=s.laterT[:, :], in_=s.laterT[:, :], compare_op=ALU.is_ge, fill=NEG, base=0,
                               pattern=[[1, P]], channel_multiplier=-1).then_inc(cst, 1)
            for e in range(E):
                pool.memset(s.rev[:, e:e + 1], float(E - e)).then_inc(cst, 1)
            pool.memset(s.eps1[:, :], EPS).then_inc(cst, 1)
            pool.memset(s.eps2[:, :], EPS * EPS).then_inc(cst, 1)
            pool.memset(one[:, :], 1.0).then_inc(cst, 1)
            pool.memset(sel[:, :, :], 0.0).then_inc(cst, 1)
            pool.memset(s.qkT[:, :, :, :], 0.0).then_inc(cst, 1)
            pool.wait_ge(cst, CONSTANTS)
            selv = sel[:, :, :].rearrange("p r (g c) -> p r g c", g=HG)
            pool.memset(selv[:, 0, :, DH:2 * DH], -1.0).then_inc(cst2, 1)
            pool.memset(selv[:, 1, :, 2 * DH:3 * DH], -1.0).then_inc(cst2, 1)
            pool.memset(selv[:, 1, :, 3 * DH:3 * DH + 2], 1.0).then_inc(cst2, 1)
            pool.memset(selv[:, 2, :, 3 * DH:3 * DH + 2], 1.0).then_inc(cst2, 1)

        @block.scalar
        def _(act):
            act.wait_ge(evac_v, 2)
            act.activation(lamc[:, 0:1], s.vec[:, LAM:LAM + 1], ACT.Sigmoid).then_inc(lam_in, 1)
            for g in range(0, len(jobs), 2):
                act.wait_ge(turned, 5 + g + 1)
                w = P * len(jobs[g][0])
                act.copy(jobs[g][1], s.ps[:, (g % 4) * 512:(g % 4) * 512 + w]).then_inc(evac_a, 1)

        @block.vector
        def _(dve):
            dve.wait_ge(x_in, 16)
            for j in range(NT):
                w = dve.bn_stats(stats[:, j, :], s.X[:, j, :])
            w.then_inc(s.stats_sems[0], B)
            dve.wait_ge(s.stats_sems[0], B)
            for j in range(NT):
                w = dve.bn_aggr(s.mv[:, j, :], stats[:, j, :])
            w.then_inc(s.stats_sems[1], 2 * B)
            n = [0]

            def chained(ins):
                n[0] += 1
                ins.then_inc(chain, 1)
                dve.wait_ge(chain, n[0])

            bank = lambda k, w: s.ps[:, k * 512:k * 512 + w]
            dve.wait_ge(turned, 5)
            dve.tensor_copy(s.vec[:, :], bank(4, NVEC)).then_inc(evac_v, 1)
            dve.tensor_copy(s.upb[:, :], bank(5, E * F1)).then_inc(evac_v, 1)
            dve.tensor_copy(s.rT[:, :], bank(6, E)).then_inc(evac_v, 1)
            dve.tensor_copy(s.bcast[:, :], bank(7, 2 * P + E)).then_inc(evac_v, 1)
            dve.tensor_copy(s.sgn[:, :], s.ps[:, 4 * 512 + 64:4 * 512 + 67]).then_inc(evac_v, 1)
            dve.wait_ge(evac_v, 5)
            dve.wait_ge(lam_in, 1)
            chained(dve.memset(s.lam[:, :], 1.0))
            chained(dve.tensor_scalar(s.lam[:, :], s.lam[:, :], lamc[:, 0:1], None, ALU.mult))
            chained(dve.tensor_scalar(lamc[:, 1:2], lamc[:, 0:1], -1.0, 1.0, ALU.mult, ALU.add))
            dve.tensor_scalar(win[:, :], nat[:, 0, :], lamc[:, 1:2], None, ALU.mult).then_inc(win_r, 1)
            dve.tensor_scalar(s.dskip[:, :], s.ident[:, :], s.vec[:, DSK:DSK + 1], None, ALU.mult).then_inc(chain, 1)
            for g in range(1, len(jobs), 2):
                dve.wait_ge(turned, 5 + g + 1)
                w = P * len(jobs[g][0])
                dve.tensor_copy(jobs[g][1], s.ps[:, (g % 4) * 512:(g % 4) * 512 + w]).then_inc(evac_v, 1)
            dve.wait_ge(evac_a, 2)
            for k in range(2):
                for t in range(3):
                    dve.tensor_copy(s.qkT[:, k, :, :].rearrange("p G (g c) -> p (G g) c", g=HG)[:, :, DH * t:DH * t + DH],
                                    wq_t[:, k, :].rearrange("p (h d) -> p h d", d=DH)).then_inc(chain, 1)

        @block.tensor
        def _(pe):
            pe.wait_ge(w_in, 16 * loads)
            pe.wait_ge(cst, CONSTANTS)
            pe.wait_ge(cst2, 4)
            at = lambda k, a, b: s.ps[:, k * 512 + a:k * 512 + b]
            pe.transpose(at(4, 0, NVEC), vrow[:, :], s.ident[0:NVEC, 0:NVEC]).then_inc(turned, 1)
            pe.transpose(at(5, 0, E * F1), uprow[:, :], s.ident[0:E * F1, 0:E * F1]).then_inc(turned, 1)
            pe.transpose(at(6, 0, E), rtrow[:, :], s.ident[0:E, 0:E]).then_inc(turned, 1)
            for a, b in ((0, P), (2 * P, 2 * P + E)):
                pe.matmul(at(7, a, b), one[:, :], brow[:, a:b], start=True, stop=True)
            pe.matmul(at(7, P, 2 * P), one[:, :], one[:, :], start=True, stop=True).then_inc(turned, 1)
            for r in range(3):
                m = pe.matmul(at(4, 64 + r, 65 + r), sel[:, r, :], one[:, 0:1], start=True, stop=True)
            m.then_inc(turned, 1)
            for g, (sources, _) in enumerate(jobs):
                if g == len(jobs) - 1:
                    pe.wait_ge(win_r, 1)
                for k, src in enumerate(sources):
                    m = pe.transpose(at(g % 4, k * P, k * P + P), src, s.ident[:, :])
                m.then_inc(turned, 1)


def batch_stats(dve, s, b, k):
    st_ready, mv_ready, std_ready, done = s.stats_sems
    for j in range(TB):
        m = dve.bn_stats(s.st[:, j, :], s.X[:, bass.ds(TB * b + j, 1), :])
    m.then_inc(st_ready, 1)
    wait_apart(dve, st_ready, b + (B * k + 1))
    for j in range(TB):
        m = dve.bn_aggr(s.mvt[:, j, :], s.st[:, j, :])
    m.then_inc(mv_ready, 1)
    dve.wait_ge(mv_ready, 2 * b + (2 * B * k + 1))
    dve.tensor_copy(s.mv[:, bass.ds(TB * b, TB), :], s.mvt[:, :, :]).then_inc(mv_ready, 1)


STDS = (0, 2, 3, 5)
EARLY = NT // 2 - TB


def scale_roots(act, s, k):
    st_ready, mv_ready, std_ready, done = s.stats_sems
    tiles = slice(0, EARLY if k == 2 else NT)
    act.wait_ge(mv_ready, 2 * B * k + 2 * (EARLY // TB if k == 2 else B))
    act.activation(s.std[:, tiles], s.mv[:, tiles, 1], ACT.Sqrt, bias=s.eps1[:, :]).then_inc(std_ready, 1)
    if k == 0:
        act.activation(s.std2[:, :], s.mv[:, :, 1], ACT.Sqrt, bias=s.eps2[:, :], scale=1.0 + EPS).then_inc(std_ready, 1)


def scales(dve, s, k):
    st_ready, mv_ready, std_ready, done = s.stats_sems
    tiles = slice(0, EARLY if k == 2 else NT)
    dve.wait_ge(std_ready, STDS[k] + 1)
    dve.reciprocal(s.rstd[:, tiles], s.std[:, tiles]).then_inc(done, 1)
    if k == 0:
        dve.wait_ge(std_ready, 2)
        dve.reciprocal(s.rr[:, :], s.std2[:, :]).then_inc(done, 1)
    dve.wait_ge(done, STDS[k] + 1 + (k == 0))


def warm(act, s, count, function):
    if not isinstance(count, int) or count > 0:
        act.wait_ge(s.warmed, count)
    act.activation(s.junk[:, :], s.eps1[:, :], function).then_inc(s.warmed, 1)


def lru_block(nc, s, sem, sb):
    def pair(name, shape):
        return [sb(f"{name}{k}", shape) for k in range(2)]

    xin, u0, n1, n2, x1 = (pair(n, [P, TB, P]) for n in ("xin", "u0", "n1", "n2", "x1"))
    u1, y, h = (pair(n, [P, T]) for n in ("u1", "y", "h"))
    hm = pair("hm", [P, F0, T])
    st2, mv2 = pair("st2", [P, TB, 6]), pair("mv2", [P, TB, 2])
    mu, r0, r1, sd2 = (pair(n, [P, TB]) for n in ("mu", "r0", "r1", "sd2"))
    names = ("xin_ready", "cols_ready", "u0_ready", "n1_ready", "u_turned", "u1_ready", "up_ready", "y_ready", "x1_ps", "x1_ready",
             "st2_ready", "mv2_ready", "sd2_ready", "r2_ready", "n2_ready", "x1b_ready", "h_turned", "h_ready", "hid_ready",
             "hm_ready", "mlp_ready", "mlp_read", "x_done")
    q = {n: sem(n + "_l") for n in names}
    bank = lambda k: s.ps[:, 512 * k:512 * k + 512]
    psT, psU, psX, psO = ([bank(2 * n), bank(2 * n + 1)] for n in range(4))
    flat = lambda t: t[:, :, :].rearrange("p j d -> p (j d)")

    def line(eng, turn):
        turn(0, 0, False, True, True)
        with eng.Fori(0, (B - 4) // 2) as i:
            for k in (1, 2):
                turn(2 * i + k, k % 2, True, True, True)
        for t in range(B - 3, B + 1):
            turn(t, t % 2, True, t + 1 < B, t + 2 < B)

    with nc.Block() as block:
        @block.vector
        def _(dve):
            def first_norm(b, k):
                tiles = bass.ds(TB * b, TB)
                for col, source in ((mu[k][:, :], s.mv[:, tiles, 0]), (r0[k][:, :], s.rstd[:, tiles]), (r1[k][:, :], s.rr[:, tiles])):
                    dve.tensor_copy(col, source).then_inc(q["cols_ready"], 1)
                dve.wait_ge(q["cols_ready"], 3 * b + 3)
                dve.wait_ge(q["xin_ready"], b + 1)
                for j in range(TB):
                    w = dve.tensor_scalar(n1[k][:, j, :], xin[k][:, j, :], mu[k][:, j:j + 1], r1[k][:, j:j + 1],
                                          ALU.subtract, ALU.mult)
                w.then_inc(q["n1_ready"], 1)

            def recurrence(b, k):
                dve.wait_ge(q["up_ready"], b + 1)
                dve.tensor_tensor_scan(y[k][:, :], s.lam[:, :], psU[k], 0.0, ALU.mult, ALU.add).then_inc(q["y_ready"], 1)

            def residual(b, k):
                dve.wait_ge(q["u0_ready"], b + 1)
                dve.wait_ge(q["x1_ps"], b + 1)
                dve.tensor_tensor(flat(x1[k]), psX[k], flat(u0[k]), ALU.add).then_inc(q["x1_ready"], 1)
                dve.wait_ge(q["x1_ready"], b + 1)
                for j in range(TB):
                    w = dve.bn_stats(st2[k][:, j, :], x1[k][:, j, :])
                w.then_inc(q["st2_ready"], 1)
                wait_apart(dve, q["st2_ready"], b + 1)
                for j in range(TB):
                    w = dve.bn_aggr(mv2[k][:, j, :], st2[k][:, j, :])
                w.then_inc(q["mv2_ready"], 1)

            def second_norm(b, k):
                dve.wait_ge(q["sd2_ready"], b + 1)
                dve.reciprocal(sd2[k][:, :], sd2[k][:, :]).then_inc(q["r2_ready"], 1)
                dve.wait_ge(q["r2_ready"], b + 1)
                for j in range(TB):
                    w = dve.tensor_scalar(n2[k][:, j, :], x1[k][:, j, :], mv2[k][:, j, 0:1], sd2[k][:, j:j + 1],
                                          ALU.subtract, ALU.mult)
                w.then_inc(q["n2_ready"], 1)

            def finish(b, k):
                dve.wait_ge(q["x1b_ready"], b + 1)
                dve.wait_ge(q["mlp_ready"], b + 1)
                dve.tensor_tensor(flat(x1[k]), psO[k], flat(x1[k]), ALU.add).then_inc(q["mlp_read"], 1)
                dve.wait_ge(q["mlp_read"], b + 3)
                out = s.X[:, bass.ds(TB * b, TB), :]
                dve.tensor_tensor(out, out, x1[k][:, :, :], ALU.add).then_inc(q["x_done"], 1)
                wait_apart(dve, q["x_done"], b + 1)
                batch_stats(dve, s, b, 1)

            def turn(t, k, before, after, later):
                here = not (isinstance(t, int) and t == B)
                if here:
                    residual(t, k)
                if later:
                    first_norm(t + 2, k)
                if here:
                    second_norm(t, k)
                if after:
                    recurrence(t + 1, 1 - k)
                if before:
                    finish(t - 1, 1 - k)

            dve.sem_inc(q["mlp_read"], 2)
            scales(dve, s, 0)
            first_norm(0, 0)
            recurrence(0, 0)
            first_norm(1, 1)
            line(dve, turn)

        @block.gpsimd
        def _(pool):
            def norm(b, k):
                wait_apart(pool, q["cols_ready"], 3 * b + 3)
                wait_apart(pool, q["xin_ready"], b + 1)
                for j in range(TB):
                    w = pool.tensor_scalar(u0[k][:, j, :], xin[k][:, j, :], mu[k][:, j:j + 1], r0[k][:, j:j + 1],
                                           ALU.subtract, ALU.mult)
                w.then_inc(q["u0_ready"], 1)

            def turn(t, k, before, after, later):
                if not (isinstance(t, int) and t == B):
                    pool.wait_ge(q["n2_ready"], t + 1)
                    pool.tensor_tensor(x1[k][:, :, :], x1[k][:, :, :], s.b2row[:, :, :], ALU.add).then_inc(q["x1b_ready"], 1)
                if later:
                    norm(t + 2, k)

            norm(0, 0)
            norm(1, 1)
            line(pool, turn)

        @block.scalar
        def _(act):
            def load(b, k):
                act.activation(xin[k][:, :, :], s.X[:, bass.ds(TB * b, TB), :], ACT.Identity).then_inc(q["xin_ready"], 1)

            def input_(b, k):
                act.wait_ge(q["u_turned"], b + 1)
                act.activation(u1[k][:, :], psT[k], ACT.Identity, bias=s.vec[:, B1V:B1V + 1],
                               scale=s.vec[:, G1:G1 + 1]).then_inc(q["u1_ready"], 1)

            def turn(t, k, before, after, later):
                if before:
                    act.wait_ge(q["h_turned"], t)
                    act.activation(h[1 - k][:, :], psT[1 - k], ACT.Identity, bias=s.vec[:, B2V:B2V + 1],
                                   scale=s.vec[:, G2:G2 + 1]).then_inc(q["h_ready"], 1)
                if later:
                    act.wait_ge(q["u0_ready"], t + 1)
                    load(t + 2, k)
                if before:
                    act.wait_ge(q["hid_ready"], t)
                    for c, ps in enumerate((psU[1 - k], psX[1 - k])):
                        w = act.activation(hm[1 - k][:, c, :], ps, ACT.Relu, bias=s.vec[:, HB + c:HB + c + 1])
                    w.then_inc(q["hm_ready"], 1)
                if not (isinstance(t, int) and t == B):
                    act.wait_ge(q["mv2_ready"], t + 1)
                    act.activation(sd2[k][:, :], mv2[k][:, :, 1], ACT.Sqrt, bias=s.eps1[:, :]).then_inc(q["sd2_ready"], 1)
                if after:
                    input_(t + 1, 1 - k)

            scale_roots(act, s, 0)
            load(0, 0)
            load(1, 1)
            input_(0, 0)
            line(act, turn)

        @block.tensor
        def _(pe):
            def turn_rows(source, k, ready, count, done):
                pe.wait_ge(ready, count)
                for j in range(TB):
                    w = pe.transpose(psT[k][:, j * P:j * P + P], source[k][:, j, :], s.ident[:, :])
                w.then_inc(done, 1)

            def project(b, k):
                pe.wait_ge(q["u1_ready"], b + 1)
                pe.matmul(psU[k], s.winT[:, :], u1[k][:, :], start=True, stop=True).then_inc(q["up_ready"], 1)

            def turn(t, k, before, after, later):
                here = not (isinstance(t, int) and t == B)
                if here:
                    pe.wait_ge(q["y_ready"], t + 1)
                    for j in range(TB):
                        o = psX[k][:, j * P:j * P + P]
                        pe.matmul(o, y[k][:, j * P:j * P + P], s.m1T[:, 0:P], start=True, stop=False)
                        w = pe.matmul(o, u1[k][:, j * P:j * P + P], s.dskip[:, :], start=False, stop=True)
                    w.then_inc(q["x1_ps"], 1)
                if before:
                    pe.wait_ge(q["h_ready"], t)
                    pe.wait_ge(q["x1_ready"], t)
                    for c, ps in enumerate((psU[1 - k], psX[1 - k])):
                        w = pe.matmul(ps, s.m1T[:, P + c * P:2 * P + c * P], h[1 - k][:, :], start=True, stop=True)
                    w.then_inc(q["hid_ready"], 1)
                if after:
                    turn_rows(n1, 1 - k, q["n1_ready"], t + 2, q["u_turned"])
                if before:
                    pe.wait_ge(q["hm_ready"], t)
                    pe.wait_ge(q["mlp_read"], t)
                    for j in range(TB):
                        for c in range(F0):
                            w = pe.matmul(psO[1 - k][:, j * P:j * P + P], hm[1 - k][:, c, j * P:j * P + P],
                                          s.m2T[:, c * P:c * P + P], start=(c == 0), stop=(c == F0 - 1))
                    w.then_inc(q["mlp_ready"], 1)
                if after:
                    project(t + 1, 1 - k)
                if here:
                    turn_rows(n2, k, q["n2_ready"], t + 1, q["h_turned"])

            turn_rows(n1, 0, q["n1_ready"], 1, q["u_turned"])
            project(0, 0)
            line(pe, turn)


def normalise(dve, s, nb, mu, r, i, chain, count):
    tiles = bass.ds(TB * i, TB)
    dve.tensor_copy(mu[:, :], s.mv[:, tiles, 0])
    dve.tensor_copy(r[:, :], s.rstd[:, tiles])
    dve.tensor_copy(nb[:, :, :], s.X[:, tiles, :]).then_inc(chain, 1)
    dve.wait_ge(chain, count)
    for j in range(TB):
        m = dve.tensor_scalar(nb[:, j, :], nb[:, j, :], mu[:, j:j + 1], r[:, j:j + 1], ALU.subtract, ALU.mult)
    return m


def route(nc, s, sem, layer):
    tag = "_" + str(layer)
    (nb_ready, turned, xs_ready, xn_ready, logit_ready, logit_read, xf_done, chain, exp_in, exp_ready, mb_ready,
     rank_ps) = (
        sem(n + tag) for n in ("nb_ready", "turned", "xs_ready", "xn_ready", "logit_ready", "logit_read", "xf_done",
                               "chain", "exp_in", "exp_ready", "mb_ready", "rank_ps"))
    nb, xs = s.nb, s.xs
    W = s.rT if layer == 0 else s.gateW
    two = range(2)
    psT = [s.ps[:, 512 * k:512 * k + 512] for k in two]
    psL = [s.ps[:, 512 * (2 + k):512 * (2 + k) + TB * E].rearrange("p (j e) -> p j e", e=E) for k in two]
    psR, psC = s.ps[:, 4 * 512:4 * 512 + NT * E], s.ps[:, 5 * 512:5 * 512 + NT * E]
    with nc.Block() as block:
        @block.vector
        def _(dve):
            def norm(b, k):
                dve.wait_ge(turned, b + 1)
                dve.wait_ge(xn_ready, b + 1)
                normalise(dve, s, nb[k], s.mu[k], s.r[k], b, chain, b + 1).then_inc(nb_ready, 1)

            def logits(b, k):
                dve.wait_ge(logit_ready, b + 1)
                dve.tensor_copy(s.L[:, bass.ds(TB * b, TB), :], psL[k]).then_inc(logit_read, 1)

            dve.sem_inc(logit_read, 2)
            scales(dve, s, 1 + 2 * layer)
            for k in two:
                norm(k, k)
            with dve.Fori(0, B // 2 - 1) as i:
                for k in two:
                    norm(2 * i + (k + 2), k)
                    logits(2 * i + k, k)
            for k in two:
                logits(B - 2 + k, k)
            dve.wait_ge(logit_read, B + 2)
            n = [B]

            def link(ins):
                n[0] += 1
                ins.then_inc(chain, 1)
                dve.wait_ge(chain, n[0])

            wide = [P, NT, E]
            rev = s.rev[:, :].unsqueeze(1).broadcast_to(wide)
            bc = lambda t: t.unsqueeze(2).broadcast_to(wide)
            if layer == 1:
                link(dve.tensor_tensor(s.L[:, :, :], s.L[:, :, :],
                                       s.bcast[:, 2 * P:2 * P + E].unsqueeze(1).broadcast_to(wide), ALU.add))
            for k, (top, hot) in enumerate(((s.top[:, 0, :], s.hot[:, 0, :, :]), (s.top[:, 1, :], s.hot[:, 1, :, :]))):
                link(dve.tensor_reduce(top, s.L[:, :, :], AX.X, ALU.max))
                link(dve.tensor_tensor(hot, s.L[:, :, :], bc(top), ALU.is_equal))
                link(dve.tensor_tensor(hot, hot, rev, ALU.mult))
                link(dve.tensor_reduce(s.gt[:, :], hot, AX.X, ALU.max))
                link(dve.tensor_tensor(hot, hot, bc(s.gt[:, :]), ALU.is_equal))
                if k == 0:
                    link(dve.scalar_tensor_tensor(s.L[:, :, :], hot, -BIG, s.L[:, :, :], ALU.mult, ALU.add))
            by_group = lambda t: t.rearrange("p (g j) e -> p g j e", g=NG)
            Mb = s.Mb[:, :, :, :].rearrange("p g e j -> p g j e")
            dve.tensor_tensor(Mb, by_group(s.hot[:, 0, :, :]), by_group(s.hot[:, 1, :, :]), ALU.add).then_inc(mb_ready, 1)
            if layer == 0:
                dve.tensor_tensor(s.top[:, 1, :], s.top[:, 1, :], s.top[:, 0, :], ALU.subtract).then_inc(exp_in, 1)
                dve.wait_ge(exp_ready, 1)
                link(dve.tensor_scalar(s.gt[:, :], s.top[:, 1, :], 1.0, None, ALU.add))
                link(dve.reciprocal(s.top[:, 0, :], s.gt[:, :]))
                link(dve.tensor_tensor(s.top[:, 1, :], s.top[:, 1, :], s.top[:, 0, :], ALU.mult))
            else:
                dve.nop().then_inc(exp_in, 1)
                dve.wait_ge(exp_ready, 1)
                link(dve.tensor_tensor(s.gt[:, :], s.top[:, 0, :], s.top[:, 1, :], ALU.add))
                link(dve.tensor_scalar(s.gt[:, :], s.gt[:, :], 1e-6, None, ALU.add))
                link(dve.reciprocal(s.gt[:, :], s.gt[:, :]))
                link(dve.tensor_tensor(s.top[:, :, :], s.top[:, :, :], s.gt[:, :].unsqueeze(1).broadcast_to([P, 2, NT]), ALU.mult))
                for k in two:
                    link(dve.tensor_tensor(s.wg[:, k, :, :], s.hot[:, k, :, :], bc(s.top[:, k, :]), ALU.mult))
                dve.wait_ge(xf_done, B + 2)
                link(dve.tensor_tensor(s.gate9[:, :, 0:E], s.wg[:, 0, :, :], s.wg[:, 1, :, :], ALU.add))
            dve.wait_ge(rank_ps, 1)
            GE = NG * E
            C = s.C[:, :, :]
            flatC = C.rearrange("p a j -> p (a j)")
            link(dve.tensor_tensor_scan(flatC, s.keep[:, 0:GE * GT], psC, 0.0, ALU.mult, ALU.add))
            link(dve.tensor_copy(s.tot[:, :], C[:, :, GT - 1]))
            link(dve.tensor_tensor(flatC, flatC, psC, ALU.subtract))
            link(dve.tensor_tensor(flatC, flatC, psR, ALU.add))
            link(dve.tensor_scalar(s.toti[:, :], s.tot[:, :], float(P - 1), None, ALU.add))
            link(dve.tensor_scalar(s.toti[:, :], s.toti[:, :], 7, None, ALU.arith_shift_right))
            link(dve.tensor_copy(s.tot[:, :], s.toti[:, :]))
            link(dve.tensor_tensor_scan(s.ends[:, :], s.keep[:, GE * GT:GE * GT + GE], s.tot[:, :], 0.0, ALU.mult, ALU.add))
            link(dve.tensor_tensor(s.tot[:, :], s.ends[:, :], s.tot[:, :], ALU.subtract))
            link(dve.tensor_scalar(s.tot[:, :], s.tot[:, :], float(P), None, ALU.mult))
            link(dve.tensor_tensor(C, C, s.tot[:, :].unsqueeze(2).broadcast_to([P, GE, GT]), ALU.add))
            pos = C.rearrange("p (g e) j -> p g j e", g=NG)
            for k in two:
                hot = by_group(s.hot[:, k, :, :])
                link(dve.tensor_tensor(hot, hot, pos, ALU.mult))
                link(dve.tensor_reduce(s.gt[:, :], s.hot[:, k, :, :], AX.X, ALU.add))
                link(dve.tensor_copy(s.slot[:, k, :], s.gt[:, :]))
            for g in range(NG):
                cmp = s.cmp[0:1, :, :]
                link(dve.tensor_tensor(cmp, s.tileno[0:1, :].unsqueeze(2).broadcast_to([1, GS, E]),
                                       s.ends[0:1, E * g:E * g + E].unsqueeze(1).broadcast_to([1, GS, E]), ALU.is_ge))
                link(dve.tensor_reduce(s.tef[0:1, GS * g:GS * g + GS], cmp, AX.X, ALU.add))
            link(dve.tensor_scalar(s.te[0:1, :], s.tef[0:1, :], float(E - 1), None, ALU.min))

        @block.scalar
        def _(act):
            act.sem_inc(xn_ready, 2)
            scale_roots(act, s, 1 + 2 * layer)
            with act.Fori(0, B // 2) as i:
                for k in two:
                    b = 2 * i + k
                    act.wait_ge(nb_ready, b + 1)
                    act.activation(s.XN[:, bass.ds(TB * b, TB), :], nb[k][:, :, :], ACT.Identity).then_inc(xn_ready, 1)
                    act.wait_ge(turned, b + 3)
                    if layer == 1:
                        act.wait_ge(xf_done, b + 1)
                    act.activation(xs[k][:, :], psT[k], ACT.Identity).then_inc(xs_ready, 1)
            act.wait_ge(exp_in, 1)
            top = s.top[:, 0:2, :] if layer else s.top[:, 1, :]
            act.activation(top, top, ACT.Sigmoid if layer else ACT.Exp).then_inc(exp_ready, 1)

        @block.gpsimd
        def _(pool):
            pool.sem_inc(xf_done, 2)
            if layer == 1:
                pool.memset(s.gate9[:, :, :], 1.0)
                with pool.Fori(0, B // 2) as i:
                    for k in two:
                        pool.wait_ge(xs_ready, 2 * i + (k + 1))
                        pool.tensor_copy(s.xf[:, bass.ds(T * (2 * i + k), T)], xs[k][:, :]).then_inc(xf_done, 1)
                pool.wait_ge(xf_done, B + 2)

        @block.tensor
        def _(pe):
            def turn(b, k):
                pe.wait_ge(nb_ready, b + 1)
                for j in range(TB):
                    m = pe.transpose(psT[k][:, j * P:j * P + P], nb[k][:, j, :], s.ident[:, :])
                m.then_inc(turned, 1)

            def logits(b, k):
                pe.wait_ge(xs_ready, b + 1)
                pe.wait_ge(logit_read, b + 1)
                for j in range(TB):
                    m = pe.matmul(psL[k][:, j, :], xs[k][:, j * P:j * P + P], W[:, :], start=True, stop=True)
                m.then_inc(logit_ready, 1)

            pe.sem_inc(turned, 2)
            turn(0, 0)
            with pe.Fori(0, B // 2 - 1) as i:
                for k in two:
                    turn(2 * i + (k + 1), 1 - k)
                    logits(2 * i + k, k)
            turn(B - 1, 1)
            for k in two:
                logits(B - 2 + k, k)
            pe.wait_ge(mb_ready, 1)
            Mb = s.Mb[:, :, :, :].rearrange("p g e j -> p (g e j)")
            pe.matmul(psR, s.before[:, :], Mb, start=True, stop=True)
            pe.matmul(psC, s.onesb[:, :], Mb, start=True, stop=True).then_inc(rank_ps, 1)


class Sums:

    def __init__(self, sem, layer):
        self.gathered = [sem(f"gathered{w}_{layer}") for w in range(GT // TB)]
        self.combined, self.chain, self.links, self.layer = sem(f"combined_{layer}"), sem(f"chain_sums_{layer}"), 0, layer


def gather(pool, s, sums, b):
    g, w = b // (GT // TB), b % (GT // TB)
    if g > 0:
        pool.wait_ge(sums.combined, GT // TB * (g - 1) + w + 1)
    for j in range(TB):
        tile = TB * b + j
        for k in range(2):
            pool.indirect_dma_start(out=s.YG[:, TB * w + j, k, :], out_offset=None, in_=s.yslots[g][:, :],
                                    in_offset=bass.IndirectOffsetOnAxis(ap=s.slot[:, k, tile:tile + 1], axis=0))\
                .then_inc(sums.gathered[w], 16)


def combine(dve, s, sums, b, x_done=None):
    def link(ins):
        sums.links += 1
        ins.then_inc(sums.chain, 1)
        dve.wait_ge(sums.chain, sums.links)

    g, w = b // (GT // TB), b % (GT // TB)
    dve.wait_ge(sums.gathered[w], 16 * 2 * TB * (g + 1))
    rows = s.YG[:, TB * w:TB * w + TB, :, :]
    gates = s.top[:, :, TB * b:TB * b + TB].rearrange("p k t -> p t k").unsqueeze(3).broadcast_to([P, TB, 2, P])
    link(dve.tensor_tensor(rows, rows, gates, ALU.mult))
    xs = s.X[:, TB * b:TB * b + TB, :]
    acc = s.acc[:, :, :]
    dve.tensor_tensor(acc, rows[:, :, 0, :], rows[:, :, 1, :], ALU.add).then_inc(sums.combined, 1)
    dve.wait_ge(sums.combined, b + 1)
    if sums.layer == 1:
        link(dve.tensor_tensor(acc, acc, s.SH[:, TB * b:TB * b + TB, :], ALU.add))
        link(dve.tensor_reduce(s.mu[0][:, :], acc, AX.X, ALU.max, apply_absolute_value=True))
        link(dve.tensor_scalar(s.mu[0][:, :], s.mu[0][:, :], 0.1, 1e-6, ALU.mult, ALU.add))
        link(dve.reciprocal(s.mu[0][:, :], s.mu[0][:, :]))
        link(dve.tensor_scalar(s.mu[0][:, :], s.mu[0][:, :], 0.1, None, ALU.mult))
        link(dve.tensor_tensor(acc, acc, s.mu[0][:, :].unsqueeze(2).broadcast_to([P, TB, P]), ALU.mult))
        dve.tensor_tensor(xs, xs, acc, ALU.add).then_inc(x_done, 1)
        dve.wait_ge(x_done, b + 1)
    else:
        link(dve.tensor_tensor(xs, xs, acc, ALU.add))
        batch_stats(dve, s, b, 2)


def experts(nc, s, sem, layer, out=None):
    tag = "x" + str(layer)

    def sems(name, count):
        return [sem(f"{name}{k}{tag}") for k in range(count)]

    BT = 2 * TB
    GB = GS // BT
    BODIES = NG * GB
    GD = GT // TB
    two = range(2)
    RING = 4
    scattered, stored = sems("scattered", NG), sems("stored", 2)
    sums = s.sums = Sums(sem, layer)
    x_load, w_load, loaded = s.x_load, s.w_load, 16 * BODIES * layer
    (x_turned, xT_ready, hid_ready, gelu_done, y_ready, yb_ready) = (
        sem(n + tag) for n in ("x_turned", "xT_ready", "hid_ready", "gelu_done", "y_ready", "yb_ready"))
    x_done = None
    if layer == 1:
        gb_ready, gT_ps, gT_ready, sh_ready, sg_done, sy_ready, sy_read, x_done, x_out = (
            sem(n + tag) for n in ("gb_ready", "gT_ps", "gT_ready", "sh_ready", "sg_done", "sy_ready", "sy_read", "x_done", "x_out"))
    NC = F0 if layer == 0 else F1
    bank = lambda k: s.ps[:, 512 * k:512 * k + 512]
    psT, psY, psH = [bank(0), bank(1)], [bank(2), bank(3)], [bank(4 + k) for k in range(RING)]
    psG, psS = s.ps[0:E + 1, 512 * 6:512 * 7], bank(7)
    W1 = s.w1T if layer == 0 else s.up
    W2 = (s.w2T if layer == 0 else s.down)[:, :, :].rearrange("p (e c) d -> p e (c d)", c=NC)
    xrows = [x.rearrange("(n p) d -> p n d", p=P) for x in s.xslots]
    yrows = [y.rearrange("(n p) d -> p n d", p=P) for y in s.yslots]
    xt, xT, wst, hb, yb, YG = s.xt, s.xT, s.wst, s.hb, s.yb, s.YG
    flat = lambda t: t.rearrange("p j d -> p (j d)")

    jobs = []
    if layer == 0:
        w_turned, w_even, w_odd = (sem(n) for n in ("w_turned", "w_even", "w_odd"))
        for half, W in enumerate((s.w1T[:, :, :].rearrange("p e (c d) -> p (e c) d", c=F0), s.w2T[:, :, :])):
            for c in range(0, E * F0, 4):
                jobs.append(([s.stage[:, E * F0 * half + c + k, :] for k in range(4)],
                             W[:, c:c + 4, :].rearrange("p c d -> p (c d)")))

    def expert(eng, i, t):
        return eng.value_load(s.te[0:1, bass.ds(BT * i + t, 1)], min_val=0, max_val=E - 1)

    with nc.Block() as block:
        @block.sync
        def _(sp):
            def loads(g, n, start=False):
                i = n + g * GB
                for r in two:
                    wait_apart(sp, x_turned, 2 * i + (r + 1))
                    sp.dma_start(xt[r][:, :, :], xrows[g][:, bass.ds(BT * n + TB * r, TB), :]).then_inc(x_load[r], 16)
                    for t in range(TB * r, TB * r + TB):
                        if layer == 0 and t % 2 and not start:
                            continue
                        wait_apart(sp, hid_ready, BT * i + (t + 1))
                        e = expert(sp, i, t)
                        sp.dma_start(wst[t][:, :], W1[:, bass.ds(e, 1), :].rearrange("p e f -> p (e f)"))\
                          .then_inc(w_load[t], 16)

            def stores(g, n):
                i = n + g * GB
                for r in two:
                    wait_apart(sp, yb_ready, 2 * i + (r + 3))
                    sp.dma_start(yrows[g][:, bass.ds(BT * n + TB * r, TB), :], yb[r][:, :, :]).then_inc(stored[r], 16)

            for g in range(NG):
                sp.wait_ge(scattered[g], 16 * 2 * GT)
                if g == 0 and layer == 0:
                    sp.wait_ge(w_even, len(jobs) // 2)
                    sp.wait_ge(w_odd, len(jobs) // 2)
                loads(g, 0, start=g == 0)
                if g > 0:
                    stores(g - 1, GB - 1)
                with sp.Fori(0, GB - 1) as n:
                    loads(g, n + 1)
                    stores(g, n)
            stores(NG - 1, GB - 1)
            if layer == 1:
                for b in range(B):
                    sp.wait_ge(x_done, b + 1)
                    sp.dma_start(out[b].rearrange("(j p) d -> p j d", p=P), s.X[:, TB * b:TB * b + TB, :]).then_inc(x_out, 16)
                sp.wait_ge(x_out, 16 * B)
            for r in two:
                sp.wait_ge(stored[r], 16 * BODIES)

        @block.gpsimd
        def _(pool):
            if layer == 0:
                pool.wait_ge(s.zeroed, 16 * NG)
            for j in range(NT):
                for k in two:
                    pool.indirect_dma_start(out=s.xslots[j // GT][:, :], out_offset=bass.IndirectOffsetOnAxis(ap=s.slot[:, k, j:j + 1], axis=0),
                                            in_=s.XN[:, j, :], in_offset=None).then_inc(scattered[j // GT], 16)
            for g in range(NG if layer else NG - 1):
                for r in two:
                    pool.wait_ge(stored[r], 16 * GB * (g + 1))
                for w in range(GD):
                    gather(pool, s, sums, GD * g + w)

        @block.scalar
        def _(act):
            for g in range(0, len(jobs), 2):
                act.wait_ge(w_turned, g + 1)
                act.copy(jobs[g][1], bank(g % 4)).then_inc(w_even, 1)
            act.sem_inc(gelu_done, RING)

            def shared(b):
                for c in range(NC):
                    act.wait_ge(sh_ready, NC * b + (c + 1))
                    if c == 0 and b >= 2:
                        act.wait_ge(sy_ready, b - 1)
                    act.activation(s.hs[b % 2][:, c, :], psH[c % 2], ACT.Gelu, bias=s.vec[:, SBU + c:SBU + c + 1]).then_inc(sg_done, 1)

            if layer == 1:
                act.sem_inc(sg_done, 2)
                for b in range(GD):
                    shared(b)

            if layer == 0:
                warm(act, s, 0, ACT.Gelu)

            def body(i, more):
                for t in range(BT):
                    if layer == 1:
                        e = expert(act, i, t)
                    act.wait_ge(hid_ready, BT * i + (t + 1 + BT))
                    act.wait_ge(y_ready, BT * i + (t + 1))
                    if layer == 0:
                        m = act.activation(hb[t % RING][:, 0:NC * P], psH[t % RING][:, 0:NC * P], ACT.Gelu)
                    else:
                        for c in range(NC):
                            m = act.activation(hb[t % RING][:, c * P:c * P + P], psH[t % RING][:, c * P:c * P + P], ACT.Gelu,
                                               bias=s.upb[:, bass.ds(e * NC + c, 1)])
                    m.then_inc(gelu_done, 1)
                    if layer == 0 and t % 2 and more:
                        e = expert(act, i + 1, t)
                        act.dma_start(wst[t][:, :], W1[:, bass.ds(e, 1), :].rearrange("p e f -> p (e f)")).then_inc(w_load[t], 16)

            with act.Fori(0, BODIES - 1) as i:
                warm(act, s, i + (BODIES + B - 2 if layer else 1), ACT.Gelu)
                body(i, True)
            body(BODIES - 1, False)
            if layer == 1:
                for b in range(GD, B):
                    shared(b)

        @block.vector
        def _(dve):
            for g in range(1, len(jobs), 2):
                dve.wait_ge(w_turned, g + 1)
                dve.tensor_copy(jobs[g][1], bank(g % 4)).then_inc(w_odd, 1)
            dve.sem_inc(yb_ready, 2)

            def gates(b):
                dve.tensor_copy(s.gb[:, :, :], s.gate9[:, TB * b:TB * b + TB, :]).then_inc(gb_ready, 1)
                dve.wait_ge(gT_ps, b + 1)
                dve.tensor_copy(s.gT[:, :], psG).then_inc(gT_ready, 1)

            def shared(b):
                dve.wait_ge(sy_ready, b + 1)
                dve.tensor_copy(s.SH[:, TB * b:TB * b + TB, :], psS.rearrange("p (j d) -> p j d", j=TB)).then_inc(sy_read, 1)

            def turned(i, r):
                dve.wait_ge(x_turned, 2 * i + (r + 3))
                dve.tensor_copy(xT[r][:, :], psT[r]).then_inc(xT_ready, 1)

            def outputs(i, r):
                dve.wait_ge(y_ready, BT * i + (TB * r + TB + RING))
                if not isinstance(i, int) or i:
                    dve.wait_ge(stored[r], 16 * i)
                dve.tensor_copy(flat(yb[r][:, :, :]), psY[r]).then_inc(yb_ready, 1)

            def body(i, more):
                outputs(i, 0)
                if more:
                    turned(i + 1, 0)
                    turned(i + 1, 1)
                outputs(i, 1)

            LOOSE = GD
            if layer == 1:
                for b in range(GD):
                    gates(b)
                    shared(b)
            for r in two:
                turned(0, r)
            body(0, True)
            with dve.Fori(1, BODIES - LOOSE) as i:
                body(i, True)
            for i in range(BODIES - LOOSE, BODIES):
                body(i, i < BODIES - 1)
                if layer == 1 and i == BODIES - 1:
                    gates(GD)
                if layer == 1 or i < BODIES - 1:
                    combine(dve, s, sums, i - BODIES + LOOSE, x_done)
            if layer == 1:
                for b in range(GD, B):
                    shared(b)
                    if b + 1 < B:
                        gates(b + 1)
                    combine(dve, s, sums, b, x_done)

        @block.tensor
        def _(pe):
            if layer == 0:
                pe.wait_ge(s.w0_in, 32)
            for g, (sources, _) in enumerate(jobs):
                if g >= 4:
                    pe.wait_ge(w_odd if g % 2 else w_even, (g - 4) // 2 + 1)
                for k, source in enumerate(sources):
                    m = pe.transpose(bank(g % 4)[:, k * P:k * P + P], source, s.ident[:, :])
                m.then_inc(w_turned, 1)
            if layer == 0:
                pe.wait_ge(w_even, len(jobs) // 2)
                pe.wait_ge(w_odd, len(jobs) // 2)
            else:
                pe.wait_ge(s.w1_in, 32)
            pe.sem_inc(x_turned, 2)
            pe.sem_inc(hid_ready, BT)
            pe.sem_inc(y_ready, RING)

            def gates(b):
                pe.wait_ge(gb_ready, b + 1)
                for j in range(TB):
                    m = pe.transpose(psG[:, j * P:j * P + P], s.gb[:, j, :], s.ident[:, :])
                m.then_inc(gT_ps, 1)

            def shared_first(b, c):
                pe.wait_ge(sg_done, NC * b + (c + 1))
                pe.matmul(psH[c % 2], s.swup[:, c * P:c * P + P], s.xf[:, T * b:T * b + T], start=True, stop=True).then_inc(sh_ready, 1)

            def shared_second(b, j):
                if j == 0:
                    pe.wait_ge(gT_ready, b + 1)
                    pe.wait_ge(sg_done, NC * b + (NC + 2))
                o = psS[:, j * P:j * P + P]
                for c in range(NC):
                    pe.matmul(o, s.hs[b % 2][:, c, j * P:j * P + P], s.swdn[:, c, :], start=(c == 0), stop=False)
                m = pe.matmul(o, s.gT[:, j * P:j * P + P], s.down9[:, :], start=False, stop=True)
                if j == TB - 1:
                    m.then_inc(sy_ready, 1)

            def shared(start, end):
                for c in range(NC):
                    shared_first(start, c)
                gates(start)
                for b in range(start, end):
                    for j in range(TB):
                        if b + 1 < end:
                            shared_first(b + 1, j)
                        shared_second(b, j)
                    if b + 1 < end:
                        gates(b + 1)

            def turn(i, r):
                pe.wait_ge(x_load[r], 16 * i + (loaded + 16))
                for j in range(TB):
                    m = pe.transpose(psT[r][:, j * P:j * P + P], xt[r][:, j, :], s.ident[:, :])
                m.then_inc(x_turned, 1)

            def first(i, t):
                r = t // TB
                pe.wait_ge(w_load[t], 16 * i + (loaded + 16))
                if t % TB == 0:
                    pe.wait_ge(xT_ready, 2 * i + (r + 1))
                pe.wait_ge(gelu_done, BT * i + (t + 1))
                for c in range(NC):
                    m = pe.matmul(psH[t % RING][:, c * P:c * P + P], wst[t][:, c * P:c * P + P],
                                  xT[r][:, (t % TB) * P:(t % TB) * P + P], start=True, stop=True)
                m.then_inc(hid_ready, 1)

            def second(i, t):
                r = t // TB
                e = expert(pe, i, t)
                pe.wait_ge(gelu_done, BT * i + (t + 1 + RING))
                if t % TB == 0:
                    pe.wait_ge(yb_ready, 2 * i + (r + 1))
                for c in range(NC):
                    m = pe.matmul(psY[r][:, (t % TB) * P:(t % TB) * P + P], hb[t % RING][:, c * P:c * P + P],
                                  W2[:, bass.ds(e, 1), c * P:c * P + P].rearrange("p e d -> p (e d)"),
                                  start=(c == 0), stop=(c == NC - 1))
                m.then_inc(y_ready, 1)

            def body(i, more):
                for t in range(BT):
                    if t == TB - 1 and more:
                        turn(i + 1, 0)
                    if t == BT - 2 and more:
                        turn(i + 1, 1)
                    if t + 2 < BT:
                        first(i, t + 2)
                    elif more:
                        first(i + 1, t + 2 - BT)
                    second(i, t)

            if layer == 1:
                shared(0, GD)
                pe.wait_ge(sy_read, GD)
            turn(0, 0)
            turn(0, 1)
            first(0, 0)
            first(0, 1)
            with pe.Fori(0, BODIES - 1) as i:
                body(i, True)
            body(BODIES - 1, False)
            if layer == 1:
                pe.wait_ge(gelu_done, BT * BODIES + RING)
                shared(GD, B)


def attention(nc, s, sem, sb):
    NCH = 5 * HG // 2
    NPJ = 2 * G
    names = ("nb_ready", "turned", "xs_ready", "p_ps", "high_ready", "p_ready", "v_ps", "v_ready", "vz_ready", "s_ready",
             "s_read", "mh_ready", "mc_ready", "mt_ps", "q2_ready", "w_ready", "e_ready", "pv_ready", "o_ready", "ot_ps",
             "rd_ready", "a_ready", "at_ps", "af_ready", "wo_ps", "x_done", "zeroed", "vz_zero", "ln_in")
    q = {n: sem(n + "_t") for n in names}
    kz_in = [sem(f"kz_in{g}") for g in range(G)]
    Q, Kd = sb("Q", [P, G, T], F32R), sb("Kd", [P, G, T], F32R)
    KZ = sb("KZ", [P, H, T], F32R)
    Hs = [sb(f"Hs{k}", [P, T], F32R) for k in range(2)]
    Vs = sb("Vs", [P, TB, P])
    Vz = sb("Vz", [P, TB, H, SLAB])
    Q2 = [sb(f"Q2{k}", [P, T], F32R) for k in range(2)]
    Mc = sb("Mc", [P, TB, P])
    Pb = sb("Pb", [P, 2 * NCH, T])
    m = sb("m", [P, H, TB])
    OT, AF, AT = sb("OT", [P, T]), s.xs[1], s.nb[1]
    st_ready, mv_ready, std_ready, done = s.stats_sems
    nb, xs = s.nb[0], s.xs[0]
    bank = lambda k: s.ps[:, 512 * k:512 * k + 512]
    MISC, PV = bank(7), bank(6)
    units = [((0, 1), (3,)), ((2, 3), (3,)), ((0, 1), (2, 0)), ((2, 3), (2, 0)), ((0, 1, 2, 3), (1,))]
    NU = len(units)
    spare = [MISC, PV, MISC, PV, MISC, MISC, PV, MISC]

    def place(u):
        heads, tiles = units[u]
        if len(heads) == 4:
            return [(g, 1, 256 * g) for g in heads]
        out = []
        for k, g in enumerate(heads):
            out += [(g, tiles[0], 512 * k)] + ([(g, 0, 512 * k + 384)] if len(tiles) > 1 else [])
        return out

    chunks = []
    for p in range(2):
        for g in (2 * p, 2 * p + 1):
            chunks += [[(g, 0, 0)], [(g, 1, 0), (g, 3, 384)]]
        chunks.append([(2 * p, 2, 0), (2 * p + 1, 2, 256)])
    where = {(g, kt): (c, col) for c, ch in enumerate(chunks) for g, kt, col in ch}

    with nc.Block() as block:
        @block.sync
        def _(sp):
            def keys(b, gg, used):
                wait_apart(sp, q["p_ready"], NPJ * b + (gg + 1))
                if used is not None:
                    wait_apart(sp, q["w_ready"], used)
                for g in range(HG):
                    rows = slice(SLAB * g, SLAB * g + SLAB)
                    sp.dma_start(KZ[rows, HG * gg + g, :].bitcast(F32), Kd[rows, gg, :].bitcast(F32)).then_inc(kz_in[gg], 16)

            for gg in range(G):
                sp.wait_ge(q["zeroed"], gg + 2)
                keys(0, gg, None)
            with sp.Fori(0, B - 1) as b:
                for gg in range(G):
                    keys(b + 1, gg, NCH * G * b + NCH * (gg + 1))
            for gg in range(G):
                sp.wait_ge(kz_in[gg], 16 * HG * B)

        @block.gpsimd
        def _(pool):
            def norm(b, used):
                wait_apart(pool, q["turned"], used)
                tiles = bass.ds(TB * b, TB)
                pool.tensor_copy(s.mu[0][:, :], s.mv[:, tiles, 0]).then_inc(q["ln_in"], 1)
                pool.tensor_copy(s.r[0][:, :], s.rstd[:, tiles]).then_inc(q["ln_in"], 1)
                pool.tensor_copy(nb[:, :, :], s.X[:, tiles, :]).then_inc(q["ln_in"], 1)
                wait_apart(pool, q["ln_in"], 3 * b + 1)
                for j in range(TB):
                    w = pool.tensor_scalar(nb[:, j, :], nb[:, j, :], s.mu[0][:, j:j + 1], s.r[0][:, j:j + 1],
                                           ALU.subtract, ALU.mult)
                w.then_inc(q["nb_ready"], 1)

            def spread(b, used):
                wait_apart(pool, q["v_ready"], b + 1)
                if used is not None:
                    wait_apart(pool, q["pv_ready"], used)
                pool.tensor_copy(Vz[:, :, :, 0:DH], Vs[:, :, :].rearrange("p j (h d) -> p j h d", d=DH)).then_inc(q["vz_ready"], 1)

            pool.memset(Vz[:, :, :, :], 0.0).then_inc(q["vz_zero"], 1)
            pool.wait_ge(q["vz_zero"], 1)
            pool.memset(Vz[:, :, :, DH:DH + 1], 1.0).then_inc(q["vz_zero"], 1)
            pool.wait_ge(q["vz_zero"], 2)
            pool.wait_ge(done, STDS[2] + 1)
            norm(1, 1)
            gather(pool, s, s.sums, B // 2)
            spread(0, None)
            for b in range(B // 2 + 1, B):
                gather(pool, s, s.sums, b)
            norm(2, 2)
            spread(1, G)
            pool.wait_ge(done, STDS[3])
            with pool.Fori(2, B - 1) as b:
                norm(b + 1, b + 1)
                spread(b, G * b)
            spread(B - 1, G * (B - 1))

        @block.vector
        def _(dve):
            dve.sem_inc(q["s_read"], 2)
            scales(dve, s, 2)
            normalise(dve, s, nb, s.mu[1], s.r[1], 0, q["ln_in"], 1).then_inc(q["nb_ready"], 1)
            def clear(gg):
                dve.tensor_copy(KZ[:, HG * gg:HG * gg + HG, :].rearrange("p h (t c) -> p (h t) c", c=P),
                                s.zero[:, :].unsqueeze(1).broadcast_to([P, HG * TB, P])).then_inc(q["zeroed"], 1)

            dve.memset(Mc[:, :, :], 0.0).then_inc(q["zeroed"], 1)
            clear(0)
            dve.wait_ge(q["zeroed"], 1)

            def project(b, p, later=True):
                dve.wait_ge(q["high_ready"], NPJ * b + (p + 1))
                if p < G and later:
                    dve.wait_ge(kz_in[p], 16 * HG * b)
                dst = Kd[:, p, :] if p < G else Q[:, p - G, :]
                dve.scalar_tensor_tensor(dst, Hs[p % 2][:, :].bitcast(F32), s.sgn[:, (1 if p < G else 0):(2 if p < G else 1)],
                                         spare[p], ALU.mult, ALU.add).then_inc(q["p_ready"], 1)

            def values(b):
                dve.wait_ge(q["v_ps"], b + 1)
                dve.tensor_copy(Vs[:, :, :].rearrange("p j d -> p (j d)"), PV).then_inc(q["v_ready"], 1)

            def maxima(n, gg, first, end):
                for u in range(first, end):
                    dve.wait_ge(q["s_ready"], NU * n + (u + 1))
                    odd = (NU * gg + u) % 2
                    ps = s.ps[:, 1024 * odd:1024 * odd + 1024]
                    heads, qt = units[u]
                    h0 = HG * gg + heads[0]
                    v = ps.rearrange("p (h k) -> p h k", h=len(heads))
                    top = m[:, h0:h0 + len(heads), :]
                    if len(qt) == 1:
                        w = dve.tensor_reduce(top[:, :, qt[0]], v, AX.X, ALU.max)
                    else:
                        dve.tensor_reduce(top[:, :, qt[0]], v[:, :, 0:384], AX.X, ALU.max)
                        w = dve.tensor_reduce(top[:, :, qt[1]], v[:, :, 384:512], AX.X, ALU.max)
                    w.then_inc(q["s_read"], 1)

            def negate(n, gg):
                dve.wait_ge(q["s_read"], NU * n + (NU + 2))
                mg = m[:, HG * gg:HG * gg + HG, :].rearrange("p h t -> p t h")
                slab = Mc[:, :, :].rearrange("p t (g c) -> p t g c", g=HG)
                hi, lo = slab[:, :, :, 3 * DH], slab[:, :, :, 3 * DH + 1]
                dve.tensor_scalar(hi.bitcast(F32R), mg, -1.0, None, ALU.mult).then_inc(q["mh_ready"], 1)
                dve.wait_ge(q["mh_ready"], n + 1)
                dve.scalar_tensor_tensor(lo.bitcast(F32R), mg, -1.0, hi, ALU.mult, ALU.subtract).then_inc(q["mc_ready"], 1)

            def shift(n, gg):
                dve.wait_ge(q["mt_ps"], n + 1)
                dve.tensor_tensor(Q2[gg % 2][:, :], MISC, Q[:, gg, :].bitcast(F32), ALU.add).then_inc(q["q2_ready"], 1)

            def sums(n):
                dve.wait_ge(q["pv_ready"], n + 1)
                dve.tensor_copy(OT[:, :], PV).then_inc(q["o_ready"], 1)

            def divide(n, gg):
                dve.wait_ge(q["ot_ps"], n + 1)
                v = MISC.rearrange("p (t g c) -> p t g c", t=TB, g=HG)
                dve.reciprocal(s.rd[:, :, :], v[:, :, :, DH]).then_inc(q["rd_ready"], 1)
                dve.wait_ge(q["rd_ready"], n + 1)
                dst = AT[:, :, HG * DH * gg:HG * DH * gg + HG * DH].rearrange("p t (g d) -> p t g d", d=DH)
                dve.tensor_tensor(dst, v[:, :, :, 0:DH], s.rd[:, :, :].unsqueeze(3).broadcast_to([P, TB, HG, DH]), ALU.mult)\
                   .then_inc(q["a_ready"], 1)

            def finish(b):
                dve.wait_ge(q["wo_ps"], b + 1)
                out = s.X[:, bass.ds(TB * b, TB), :]
                dve.tensor_tensor(out, out, PV.rearrange("p (j d) -> p j d", j=TB), ALU.add).then_inc(q["x_done"], 1)

            def next_stats(b):
                wait_apart(dve, q["x_done"], b + 1)
                batch_stats(dve, s, b, 3)

            def body(b, first, last):
                more = not last
                for gg in range(G):
                    n = G * b + gg
                    ahead = gg + 1 < G or more
                    before = gg > 0 or not first
                    an, ag = n + 1, (gg + 1) % G
                    shift(n, gg)
                    if ahead:
                        maxima(an, ag, 0, 2)
                    if before:
                        sums(n - 1)
                    if first:
                        for late in {0: [3], 1: [4], 2: [5, 6], 3: [7]}[gg]:
                            combine(dve, s, s.sums, late)
                    elif gg == 3:
                        next_stats(b - 1)
                    if more and gg >= 2:
                        project(b + 1, {2: 4, 3: 7}[gg])
                    if ahead:
                        maxima(an, ag, 2, 3)
                    if more and gg < 3:
                        project(b + 1, {0: 0, 1: 2, 2: 5}[gg])
                    if ahead:
                        maxima(an, ag, 3, 4)
                    if gg == 1 and not first:
                        finish(b - 1)
                    if gg == 2 and more:
                        project(b + 1, 6)
                    if gg == 3 and more:
                        values(b + 1)
                    if ahead:
                        maxima(an, ag, 4, 5)
                        negate(an, ag)
                    if more and gg < 2:
                        project(b + 1, {0: 1, 1: 3}[gg])
                    if before:
                        divide(n - 1, (gg - 1) % G)
                    if first:
                        if gg == 3:
                            dve.wait_ge(std_ready, STDS[3])
                            dve.reciprocal(s.rstd[:, EARLY:NT], s.std[:, EARLY:NT]).then_inc(done, 1)

            for p in range(NPJ):
                if p < G - 1:
                    clear(p + 1)
                project(0, p, later=False)
            values(0)
            maxima(0, 0, 0, NU)
            negate(0, 0)
            body(0, True, False)
            with dve.Fori(1, B - 1) as b:
                body(b, False, False)
            body(B - 1, False, True)
            sums(G * B - 1)
            divide(G * B - 1, G - 1)
            finish(B - 1)
            next_stats(B - 1)

        @block.scalar
        def _(act):
            act.sem_inc(q["e_ready"], 2)
            scale_roots(act, s, 2)

            def to_xs(b):
                act.wait_ge(q["turned"], b + 1)
                act.activation(xs[:, :], MISC, ACT.Identity).then_inc(q["xs_ready"], 1)

            def high(b, p, prologue=False):
                act.wait_ge(q["p_ps"], NPJ * b + (p + 1))
                if not prologue or p >= 2:
                    act.wait_ge(q["p_ready"], NPJ * b + (p - 1))
                act.activation(Hs[p % 2][:, :], spare[p], ACT.Identity, bias=s.sgn[:, 2:3] if p < G else 0.0)\
                   .then_inc(q["high_ready"], 1)

            def exps(n, gg, first, end, twice):
                for c in range(first, end):
                    act.wait_ge(q["w_ready"], NCH * n + (c + 1))
                    if c == 0 and twice:
                        act.wait_ge(q["pv_ready"], n - 1)
                    act.activation(Pb[:, NCH * (gg % 2) + c, :], bank(4 + c % 2), ACT.Exp, scale=DH ** -0.5)\
                       .then_inc(q["e_ready"], 1)

            def to_af(b):
                act.wait_ge(q["at_ps"], b + 1)
                act.activation(AF[:, :], MISC, ACT.Identity).then_inc(q["af_ready"], 1)

            def body(b, first, last):
                more = not last
                for gg in range(G):
                    n = G * b + gg
                    twice = gg >= 2 or not first
                    exps(n, gg, 0, 4, twice)
                    if gg == 0 and more:
                        to_xs(b + 1)
                    if gg == 1 and not first:
                        to_af(b - 1)
                    if more and gg >= 2:
                        high(b + 1, {2: 4, 3: 7}[gg])
                    exps(n, gg, 4, 6, twice)
                    if more and gg < 3:
                        high(b + 1, {0: 0, 1: 2, 2: 5}[gg])
                    exps(n, gg, 6, 8, twice)
                    if more and gg == 2:
                        high(b + 1, 6)
                    exps(n, gg, 8, NCH, twice)
                    if more and gg < 2:
                        high(b + 1, {0: 1, 1: 3}[gg])

            to_xs(0)
            for p in range(NPJ):
                high(0, p, prologue=True)
            body(0, True, False)
            act.wait_ge(mv_ready, 2 * B * 3)
            act.activation(s.std[:, EARLY:NT], s.mv[:, EARLY:NT, 1], ACT.Sqrt, bias=s.eps1[:, :]).then_inc(std_ready, 1)
            with act.Fori(1, B - 1) as b:
                warm(act, s, b + (NG * GS // (2 * TB) - 1), ACT.Exp)
                body(b, False, False)
            body(B - 1, False, True)
            to_af(B - 1)

        @block.tensor
        def _(pe):
            def turn_in(b):
                pe.wait_ge(q["nb_ready"], b + 1)
                for j in range(TB):
                    w = pe.transpose(MISC[:, j * P:j * P + P], nb[:, j, :], s.ident[:, :])
                w.then_inc(q["turned"], 1)

            def project(b, p):
                pe.wait_ge(q["xs_ready"], b + 1)
                pe.matmul(spare[p], s.qkT[:, 1 if p < G else 0, p % G, :], xs[:, :], start=True, stop=True).then_inc(q["p_ps"], 1)

            def values_in(b):
                for j in range(TB):
                    w = pe.matmul(PV[:, j * P:j * P + P], xs[:, j * P:j * P + P], s.m2T[:, 2 * P:3 * P], start=True, stop=True)
                w.then_inc(q["v_ps"], 1)

            def row_scores(n, gg, first, end, b):
                if first == 0:
                    pe.wait_ge(q["p_ready"], NPJ * b + (G + gg + 1))
                    pe.wait_ge(kz_in[gg], 16 * HG * b + 16 * HG)
                for u in range(first, end):
                    pe.wait_ge(q["s_read"], NU * n + (u + 1))
                    for g, qt, col in place(u):
                        c = 1024 * ((NU * gg + u) % 2) + col
                        w = (qt + 1) * P
                        pe.matmul(s.ps[:, c:c + w], Q[:, gg, qt * P:qt * P + P], KZ[:, HG * gg + g, 0:w], start=True, stop=False)
                        done = pe.matmul(s.ps[:, c + w - P:c + w], s.identb[:, :], s.later[:, :], start=False, stop=True)
                    done.then_inc(q["s_ready"], 1)

            def shift(n):
                pe.wait_ge(q["mc_ready"], n + 1)
                for t in range(TB):
                    w = pe.transpose(MISC[:, t * P:t * P + P], Mc[:, t, :], s.ident[:, :])
                w.then_inc(q["mt_ps"], 1)

            def weights(n, gg, first, end):
                if first == 0:
                    pe.wait_ge(q["q2_ready"], n + 1)
                for c in range(first, end):
                    pe.wait_ge(q["e_ready"], NCH * n + (c + 1))
                    for g, kt, col in chunks[c]:
                        ps = bank(4 + c % 2)
                        pe.matmul(ps[:, col:col + T - kt * P], KZ[:, HG * gg + g, kt * P:kt * P + P],
                                  Q2[gg % 2][:, kt * P:T], start=True, stop=False)
                        w = pe.matmul(ps[:, col:col + P], s.identb[:, :], s.laterT[:, :], start=False, stop=True)
                    w.then_inc(q["w_ready"], 1)

            def sums(n, gg, b):
                pe.wait_ge(q["e_ready"], NCH * n + (NCH + 2))
                if gg == 0:
                    pe.wait_ge(q["vz_ready"], b + 1)
                for kt in range(TB):
                    for g in range(HG):
                        c, col = where[g, kt]
                        w = pe.matmul(PV[SLAB * g:SLAB * g + SLAB, kt * P:T], Vz[:, kt, HG * gg + g, :],
                                      Pb[:, NCH * (gg % 2) + c, col:col + T - kt * P], start=(kt == 0), stop=(kt == TB - 1))
                w.then_inc(q["pv_ready"], 1)

            def turn(n):
                pe.wait_ge(q["o_ready"], n + 1)
                for t in range(TB):
                    w = pe.transpose(MISC[:, t * P:t * P + P], OT[:, t * P:t * P + P], s.ident[:, :])
                w.then_inc(q["ot_ps"], 1)

            def turn_out(b):
                pe.wait_ge(q["a_ready"], G * b + G)
                for t in range(TB):
                    w = pe.transpose(MISC[:, t * P:t * P + P], AT[:, t, :], s.ident[:, :])
                w.then_inc(q["at_ps"], 1)

            def output(b):
                pe.wait_ge(q["af_ready"], b + 1)
                for j in range(TB):
                    w = pe.matmul(PV[:, j * P:j * P + P], AF[:, j * P:j * P + P], s.m2T[:, 3 * P:4 * P], start=True, stop=True)
                w.then_inc(q["wo_ps"], 1)

            def body(b, first, last):
                more = not last
                for gg in range(G):
                    n = G * b + gg
                    ahead = gg + 1 < G or more
                    before = gg > 0 or not first
                    an, ag, ab = n + 1, (gg + 1) % G, b + (gg + 1) // G
                    if ahead:
                        row_scores(an, ag, 0, 2, ab)
                    if gg >= 2 or not first:
                        pe.wait_ge(q["a_ready"], n - 1)
                    shift(n)
                    if before:
                        if gg == 0:
                            pe.wait_ge(q["v_ready"], b + 1)
                        elif more:
                            pe.wait_ge(q["p_ready"], NPJ * b + NPJ + {1: 2, 2: 4, 3: 7}[gg])
                        elif gg == 2 and not first:
                            pe.wait_ge(q["x_done"], b)
                        else:
                            pe.wait_ge(q["o_ready"], n - 1)
                        sums(n - 1, (gg - 1) % G, b - (gg == 0))
                    weights(n, gg, 0, 4)
                    if more and gg != 1:
                        if gg == 0:
                            turn_in(b + 1)
                        else:
                            project(b + 1, {2: 4, 3: 7}[gg])
                    if gg == 1 and not first:
                        turn_out(b - 1)
                    if ahead:
                        row_scores(an, ag, 2, 3, ab)
                    weights(n, gg, 4, 6)
                    if more and gg < 3:
                        if gg == 1 and not first:
                            pe.wait_ge(q["af_ready"], b)
                        if gg == 2:
                            pe.wait_ge(q["p_ready"], NPJ * b + NPJ + 5)
                        project(b + 1, {0: 0, 1: 2, 2: 5}[gg])
                    if ahead:
                        row_scores(an, ag, 3, 4, ab)
                    weights(n, gg, 6, 8)
                    if (more and gg >= 2) or (gg == 1 and not first):
                        pe.wait_ge(q["o_ready"], n)
                        if gg == 1:
                            output(b - 1)
                        elif gg == 2:
                            project(b + 1, 6)
                        else:
                            values_in(b + 1)
                    if ahead:
                        row_scores(an, ag, 4, 5, ab)
                    weights(n, gg, 8, NCH)
                    if more and gg < 2:
                        if first:
                            pe.wait_ge(*((q["v_ready"], 1) if gg == 0 else (q["o_ready"], n)))
                        else:
                            pe.wait_ge(*((q["o_ready"], n) if gg == 0 else (q["x_done"], b)))
                        project(b + 1, {0: 1, 1: 3}[gg])
                    if before:
                        if more:
                            pe.wait_ge(q["p_ready"], NPJ * b + NPJ + {0: 1, 1: 3, 2: 6, 3: 8}[gg])
                        elif gg == 1:
                            pe.wait_ge(q["af_ready"], b)
                        turn(n - 1)

            turn_in(0)
            for p in range(NPJ):
                if p >= 2:
                    pe.wait_ge(q["p_ready"], {2: 1, 3: 2, 4: 3, 5: 5, 6: 4, 7: 6}[p])
                project(0, p)
            pe.wait_ge(q["p_ready"], 7)
            values_in(0)
            row_scores(0, 0, 0, NU, 0)
            body(0, True, False)
            with pe.Fori(1, B - 1) as b:
                body(b, False, False)
            body(B - 1, False, True)
            sums(G * B - 1, G - 1, B - 1)
            pe.wait_ge(q["a_ready"], G * B - 1)
            turn(G * B - 1)
            turn_out(B - 1)
            output(B - 1)


def build(nc, A, out):
    with ExitStack() as ctx:
        def allocator(stack):
            return lambda name, shape, dt=F32: stack.enter_context(nc.sbuf_tensor(name, shape, dt))

        def sem(name):
            return ctx.enter_context(nc.semaphore(name))

        sb = allocator(ctx)
        wait_apart.pace = {e.engine: sem(f"pace_{n}") for n, e in
                     (("dve", nc.vector), ("sp", nc.sync), ("pool", nc.gpsimd))}

        def own_buffers(stage):
            with ExitStack() as own:
                stage(nc, s, sem, allocator(own))

        s = Shared()
        s.ps = ctx.enter_context(nc.psum_tensor("ps", [P, 8 * 512], F32))
        s.X = sb("X", [P, NT, P])
        s.x_in = sem("x_in")
        s.ident, s.identb = sb("ident", [P, P]), sb("identb", [P, P], BF16)
        s.later, s.laterT = sb("later", [P, P], BF16), sb("laterT", [P, P], BF16)
        s.rev, s.eps1, s.eps2 = sb("rev", [P, E]), sb("eps1", [P, 1]), sb("eps2", [P, 1])
        s.junk = sb("junk", [P, 1])
        s.vec, s.upb, s.rT, s.gateW = sb("vec", [P, NVEC]), sb("upb", [P, E * F1]), sb("rT", [P, E]), sb("gateW", [P, E])
        s.bcast, s.sgn, s.lam = sb("bcast", [P, 2 * P + E]), sb("sgn", [P, 3]), sb("lam", [P, T])
        s.dskip, s.winT, s.m1T, s.m2T = sb("dskip", [P, P]), sb("winT", [P, P]), sb("m1T", [P, 3 * P]), sb("m2T", [P, 4 * P])
        s.zero = sb("zero", [P, P])
        s.before, s.onesb = sb("before", [P, P], BF16), sb("onesb", [P, P], BF16)
        s.keep, s.tileno = sb("keep", [P, NG * E * GT + NG * E]), sb("tileno", [1, GS])
        s.xslots, s.yslots = ([nc.dram_tensor(f"{n}slots{g}", (GS * P, P), F32, kind="Internal").ap() for g in range(NG)]
                              for n in "xy")
        s.zeroed, s.w0_in, s.w1_in = sem("slots_zeroed"), sem("w0_in"), sem("w1_in")
        s.x_load, s.w_load = [sem(f"x_load{r}") for r in range(2)], [sem(f"w_load{t}") for t in range(2 * TB)]
        s.stats_sems = [sem(f"stats_{n}") for n in ("st", "mv", "std", "done")]
        s.warmed = sem("warmed")
        s.qkT = sb("qkT", [P, 2, G, P])
        s.down9 = sb("down9", [E + 1, P])
        s.up, s.down = sb("up", [P, E, F1 * P]), sb("down", [P, E * F1, P])
        s.swup, s.swdn = sb("swup", [P, F1 * P]), sb("swdn", [P, F1, P])
        s.st, s.mvt, s.mv = sb("st", [P, TB, 6]), sb("mvt", [P, TB, 2]), sb("mv", [P, NT, 2])
        s.std, s.std2, s.rstd, s.rr = (sb(n, [P, NT]) for n in ("std", "std2", "rstd", "rr"))
        s.mu, s.r = [sb(f"muc{k}", [P, TB]) for k in range(2)], [sb(f"rc{k}", [P, TB]) for k in range(2)]
        s.rd = sb("rd", [P, TB, HG])
        s.nb, s.xs = [sb(f"nb{k}", [P, TB, P]) for k in range(2)], [sb(f"xs{k}", [P, T]) for k in range(2)]
        s.b2row = s.bcast[:, 0:P].unsqueeze(1).broadcast_to([P, TB, P])

        def ffn(layer):
            with ExitStack() as own:
                fs = allocator(own)
                s.XN = fs(f"XN{layer}", [P, NT, P])
                if layer == 1:
                    s.xf = fs("xf", [P, B * T])
                    s.SH = fs("SH", [P, NT, P])
                    s.hs = [fs(f"hs{k}", [P, F1, T]) for k in range(2)]
                    s.wg = fs("wg", [P, 2, NT, E])
                s.L, s.hot = fs(f"L{layer}", [P, NT, E]), fs(f"hot{layer}", [P, 2, NT, E])
                s.gt = fs(f"gt{layer}", [P, NT])
                s.gate9, s.gb = fs(f"gate9{layer}", [P, NT, E + 1]), fs(f"gb{layer}", [P, TB, E + 1])
                s.gT, s.te = fs(f"gT{layer}", [E + 1, T]), fs(f"te{layer}", [1, NG * GS], I32)
                s.tef, s.cmp = fs(f"tef{layer}", [1, NG * GS]), fs(f"cmp{layer}", [1, GS, E])
                s.Mb = fs(f"Mb{layer}", [P, NG, E, GT], BF16)
                s.C, s.tot, s.ends = fs(f"C{layer}", [P, NG * E, GT]), fs(f"tot{layer}", [P, NG * E]), fs(f"ends{layer}", [P, NG * E])
                s.toti = fs(f"toti{layer}", [P, NG * E], I32)
                NC = F1 if layer else F0
                s.xt = [fs(f"xt{layer}{k}", [P, TB, P]) for k in range(2)]
                s.xT = [fs(f"xT{layer}{k}", [P, T]) for k in range(2)]
                s.wst = [fs(f"wst{layer}{k}", [P, NC * P]) for k in range(2 * TB)]
                s.hb = [fs(f"hb{layer}{k}", [P, NC * P]) for k in range(4)]
                s.yb = [fs(f"yb{layer}{k}", [P, TB, P]) for k in range(2)]
                route(nc, s, sem, layer)
                experts(nc, s, sem, layer, out)

        s.top, s.slot = sb("top", [P, 2, NT]), sb("slot", [P, 2, NT], I32)
        s.acc, s.YG = sb("acc", [P, TB, P]), sb("YG", [P, GT, 2, P])

        with ExitStack() as early:
            es = allocator(early)
            s.w1T, s.w2T = es("w1T", [P, E, F0 * P]), es("w2T", [P, E * F0, P])
            s.stage = es("stage", [P, 2 * E * F0, P])
            with ExitStack() as own:
                setup(nc, s, A, sem, allocator(own))
            own_buffers(lru_block)
            ffn(0)
        own_buffers(attention)
        ffn(1)


_INS = ['L0_attn_x', 'L0_attn_w_in', 'L0_attn_log_lambda', 'L0_attn_w_out', 'L0_attn_D_skip', 'L0_attn_ln1_g', 'L0_attn_ln1_b', 'L0_attn_ln2_g', 'L0_attn_ln2_b', 'L0_attn_w1', 'L0_attn_b1', 'L0_attn_w2', 'L0_attn_b2', 'L0_ffn_router_w', 'L0_ffn_w1', 'L0_ffn_w2', 'L1_attn_Wq', 'L1_attn_Wk', 'L1_attn_Wv', 'L1_attn_Wo', 'L1_ffn_gate_w', 'L1_ffn_bias', 'L1_ffn_up_w', 'L1_ffn_up_b', 'L1_ffn_down_w', 'L1_ffn_down_b', 'L1_ffn_sw_up', 'L1_ffn_sb_up', 'L1_ffn_sw_down', 'L1_ffn_sb_down']


def kernel(**inputs):
    import numpy as _np
    import concourse.bacc as _bacc
    from concourse import mybir as _mybir
    from concourse.bass_utils import run_bass_kernel_spmd as _run

    nc = _bacc.Bacc("TRN2", target_bir_lowering=False, num_devices=1)
    arrays, args = {}, {}
    for name in _INS:
        a = _np.ascontiguousarray(inputs[name])
        arrays[f"in_{name}_dram"] = a
        args[name] = nc.dram_tensor(f"in_{name}_dram", a.shape, _mybir.dt.from_np(a.dtype), kind="ExternalInput").ap()
    out = nc.dram_tensor("out_0_dram", (8, 512, 128), _mybir.dt.float32, kind="ExternalOutput").ap()
    build(nc, args, out)
    r = _run(nc, [arrays], core_ids=[0])
    return r.results[0]["out_0_dram"]
```
